# Optimizing a Trainium2 kernel written in Bass

```python
import numpy as np
import jax
import jax.numpy as jnp

def _softmax(x, axis=-1):
    return jax.nn.softmax(x, axis=axis)

def _gelu(x):
    return jax.nn.gelu(x, approximate=True)

def _silu(x):
    return jax.nn.silu(x)

def _sigmoid(x):
    return jax.nn.sigmoid(x)

def _layernorm(x, axis=-1, eps=1e-05):
    m = jnp.mean(x, axis=axis, keepdims=True)
    v = jnp.var(x, axis=axis, keepdims=True)
    return (x - m) / jnp.sqrt(v + eps)

def _scatter_add(tgt, idx, src, axis=0):
    return tgt.at[idx].add(src)

def _segment_sum(src, seg, n):
    return jax.ops.segment_sum(src, seg, n)
kernel_name = 'mk_early_fusion_d2_tok_img768_r4_45cb1a'

def setup_inputs(seed: int=0):
    np.random.seed(seed)
    _w = jnp.asarray

    def _rec_inputs():
        import jax
        import jax.numpy as jnp
        _rk = jax.random.key(seed)
        x = 7.57192e-06 + 1.00007 * jax.random.normal(jax.random.fold_in(_rk, 1), (16, 3, 128, 128), jnp.float32)
        txt = 0.363415 + 0.567636 * jax.random.normal(jax.random.fold_in(_rk, 2), (16, 128, 192), jnp.float32)
        return (x, txt)
    x, txt = _rec_inputs()

    def _L0_tok_setup():
        import jax, jax.numpy as jnp
        import numpy as np
        K = 4
        STRIDE = 4
        EPS = 1e-05
        SLOPE = 0.01

        def conv2d(x, w, b, stride):
            out = jax.lax.conv_general_dilated(x, w, (stride, stride), 'VALID', dimension_numbers=('NCHW', 'OIHW', 'NCHW'))
            return out + b[None, :, None, None]

        def batchnorm(x, g, b, m, v):
            inv = g / jnp.sqrt(v + EPS)
            return x * inv[None, :, None, None] + (b - m * inv)[None, :, None, None]

        def leaky_relu(x):
            return jnp.where(x >= 0, x, SLOPE * x)

        def deform_conv(x, offset, w, b):
            B, C, H, W = x.shape
            Ho, Wo = (offset.shape[2], offset.shape[3])
            KK = K * K
            off = offset.reshape(B, KK, 2, Ho, Wo)
            kh = jnp.repeat(jnp.arange(K), K).astype(x.dtype)
            kw = jnp.tile(jnp.arange(K), K).astype(x.dtype)
            base_y = (jnp.arange(Ho) * STRIDE).astype(x.dtype)
            base_x = (jnp.arange(Wo) * STRIDE).astype(x.dtype)
            py = base_y[None, None, :, None] + kh[None, :, None, None] + off[:, :, 0]
            px = base_x[None, None, None, :] + kw[None, :, None, None] + off[:, :, 1]
            y0 = jnp.floor(py)
            x0 = jnp.floor(px)
            wy = py - y0
            wx = px - x0

            def corner(yc, xc):
                yi = yc.astype(jnp.int32)
                xi = xc.astype(jnp.int32)
                valid = (yi >= 0) & (yi < H) & (xi >= 0) & (xi < W)
                yi = jnp.clip(yi, 0, H - 1)
                xi = jnp.clip(xi, 0, W - 1)
                v = jax.vmap(lambda img, a, c: img[:, a, c])(x, yi, xi)
                return v * valid[:, None].astype(x.dtype)
            v00 = corner(y0, x0)
            v01 = corner(y0, x0 + 1)
            v10 = corner(y0 + 1, x0)
            v11 = corner(y0 + 1, x0 + 1)
            wy_ = wy[:, None]
            wx_ = wx[:, None]
            sampled = v00 * (1 - wy_) * (1 - wx_) + v01 * (1 - wy_) * wx_ + v10 * wy_ * (1 - wx_) + v11 * wy_ * wx_
            out = jnp.einsum('bckhw,ock->bohw', sampled, w.reshape(w.shape[0], C, KK))
            return out + b[None, :, None, None]
        key = jax.random.key(seed)
        ks = jax.random.split(key, 16)
        f32 = jnp.float32
        inp = {'x': jax.random.normal(ks[0], (64, 3, 224, 224), f32), 'stem_w': jax.random.normal(ks[1], (96, 3, 4, 4), f32) * 0.1, 'stem_b': jax.random.normal(ks[2], (96,), f32) * 0.05, 'bn1_g': jax.random.uniform(ks[3], (96,), f32, 0.5, 1.5), 'bn1_b': jax.random.normal(ks[4], (96,), f32) * 0.05, 'bn1_m': jax.random.normal(ks[5], (96,), f32) * 0.05, 'bn1_v': jax.random.uniform(ks[6], (96,), f32, 0.5, 1.5), 'off_w': jax.random.normal(ks[7], (32, 96, 4, 4), f32) * 0.02, 'off_b': jax.random.normal(ks[8], (32,), f32) * 0.02, 'dcn_w': jax.random.normal(ks[9], (192, 96, 4, 4), f32) * 0.05, 'dcn_b': jax.random.normal(ks[10], (192,), f32) * 0.05, 'bn2_g': jax.random.uniform(ks[11], (192,), f32, 0.5, 1.5), 'bn2_b': jax.random.normal(ks[12], (192,), f32) * 0.05, 'bn2_m': jax.random.normal(ks[13], (192,), f32) * 0.05, 'bn2_v': jax.random.uniform(ks[14], (192,), f32, 0.5, 1.5)}
        return inp
    _L0_tok_all = _L0_tok_setup()
    _L0_tok_in = {k: v for k, v in _L0_tok_all.items() if k in ('stem_w', 'stem_b', 'bn1_g', 'bn1_b', 'bn1_m', 'bn1_v', 'off_w', 'off_b', 'dcn_w', 'dcn_b', 'bn2_g', 'bn2_b', 'bn2_m', 'bn2_v')}
    del _L0_tok_all

    def _L0_attn_setup():
        import jax, jax.numpy as jnp
        import numpy as np
        EMBED_DIM = 192
        MAX_LEN = 256
        ALPHA = 0.99
        BATCH = 16

        def _retention_mask(sl, alpha, dtype):
            i = jnp.arange(sl)[:, None]
            j = jnp.arange(sl)[None, :]
            causal = i >= j
            exponent = jnp.where(causal, (i - j).astype(dtype), 0.0)
            decay = jnp.asarray(alpha, dtype) ** exponent
            return jnp.where(causal, decay, jnp.zeros((), dtype))
        key = jax.random.key(seed)
        k1, k2, k3 = jax.random.split(key, 3)
        x = jax.random.normal(k1, (BATCH, MAX_LEN, EMBED_DIM), dtype=jnp.float32)
        scale = 1.0 / np.sqrt(EMBED_DIM)
        W_qkv = jax.random.uniform(k2, (EMBED_DIM, 3 * EMBED_DIM), dtype=jnp.float32, minval=-scale, maxval=scale)
        b_qkv = jax.random.uniform(k3, (3 * EMBED_DIM,), dtype=jnp.float32, minval=-scale, maxval=scale)
        return {'x': x, 'W_qkv': W_qkv, 'b_qkv': b_qkv}
    _L0_attn_all = _L0_attn_setup()
    _L0_attn_in = {k: v for k, v in _L0_attn_all.items() if k in ('W_qkv', 'b_qkv')}
    del _L0_attn_all

    def _L0_ffn_setup():
        import jax, jax.numpy as jnp
        import numpy as np
        D = 192
        M = 768
        G = 4
        E = 8
        KG = 2
        KE = 4
        EPS = 1e-06

        def _topk_gates(logits, k):
            top, idx = jax.lax.top_k(logits, k)
            gates = jax.nn.softmax(top, axis=-1)
            gates = jnp.where(gates >= EPS, gates, jnp.zeros_like(gates))
            return (gates, idx)
        key = jax.random.key(seed)
        ks = jax.random.split(key, 9)
        x = jax.random.normal(ks[0], (1, 256, D), dtype=jnp.float32)
        Wg = jax.random.normal(ks[1], (D, G), dtype=jnp.float32) * 0.02
        bg = jax.random.normal(ks[2], (G,), dtype=jnp.float32) * 0.01
        We = jax.random.normal(ks[3], (G, D, E), dtype=jnp.float32) * 0.02
        be = jax.random.normal(ks[4], (G, E), dtype=jnp.float32) * 0.01
        W1 = jax.random.normal(ks[5], (G, E, D, M), dtype=jnp.float32) * 0.02
        b1 = jax.random.normal(ks[6], (G, E, M), dtype=jnp.float32) * 0.01
        W2 = jax.random.normal(ks[7], (G, E, M, D), dtype=jnp.float32) * 0.02
        b2 = jax.random.normal(ks[8], (G, E, D), dtype=jnp.float32) * 0.01
        return {'x': x, 'Wg': Wg, 'bg': bg, 'We': We, 'be': be, 'W1': W1, 'b1': b1, 'W2': W2, 'b2': b2}
    _L0_ffn_all = _L0_ffn_setup()
    _L0_ffn_in = {k: v for k, v in _L0_ffn_all.items() if k in ('Wg', 'bg', 'We', 'be', 'W1', 'b1', 'W2', 'b2')}
    del _L0_ffn_all

    def _L1_attn_setup():
        import jax, jax.numpy as jnp
        import numpy as np
        D = 192
        ORDER = 2
        K = 3
        MAXLEN = 512

        def _fft_conv(h, x, Bp):
            L = x.shape[-1]
            n = 2 * L
            h_f = jnp.fft.rfft(h, n=n, norm='forward')
            x_f = jnp.fft.rfft(x, n=n)
            y = jnp.fft.irfft(h_f * x_f, n=n, norm='forward')[..., :L]
            return y + x * Bp
        key = jax.random.key(seed)
        ks = jax.random.split(key, 8)
        Bsz, L = (4, 512)
        C = D * (ORDER + 1)
        u = jax.random.normal(ks[0], (Bsz, L, D), jnp.float32)
        W_lin = jax.random.normal(ks[1], (C, D), jnp.float32) / np.float32(np.sqrt(D))
        b_lin = jnp.zeros((C,), jnp.float32)
        conv_w = jax.random.normal(ks[2], (C, 1, K), jnp.float32) / np.float32(np.sqrt(K))
        conv_b = jnp.zeros((C,), jnp.float32)
        W_out = jax.random.normal(ks[3], (D, D), jnp.float32) / np.float32(np.sqrt(D))
        b_out = jnp.zeros((D,), jnp.float32)
        h_param = jax.random.normal(ks[4], (ORDER, D, MAXLEN), jnp.float32)
        win_b = jnp.zeros((1, D, 1), jnp.float32)
        min_decay = np.log(0.01) / 1.5
        max_decay = np.log(0.01) / 0.3
        alphas = jnp.linspace(min_decay, max_decay, D, dtype=jnp.float32)[None, :, None]
        Bmat = jax.random.normal(ks[5], (ORDER, 1, D, 1), jnp.float32)
        return dict(u=u, W_lin=W_lin, b_lin=b_lin, conv_w=conv_w, conv_b=conv_b, W_out=W_out, b_out=b_out, h_param=h_param, win_b=win_b, alphas=alphas, Bmat=Bmat)
    _L1_attn_all = _L1_attn_setup()
    _L1_attn_in = {k: v for k, v in _L1_attn_all.items() if k in ('W_lin', 'b_lin', 'conv_w', 'conv_b', 'W_out', 'b_out', 'h_param', 'win_b', 'alphas', 'Bmat')}
    del _L1_attn_all

    def _L1_ffn_setup():
        import jax, jax.numpy as jnp
        import numpy as np
        NHEAD = 12
        EPS_Z = 1e-05
        EPS_LN = 1e-05

        def _zscore_last(t, n):
            m = t.mean(axis=-1, keepdims=True)
            var = ((t - m) ** 2).sum(axis=-1, keepdims=True) / (n - 1)
            return (t - m) / (jnp.sqrt(var) + EPS_Z)

        def _layernorm(x, g, b):
            m = x.mean(axis=-1, keepdims=True)
            v = ((x - m) ** 2).mean(axis=-1, keepdims=True)
            return (x - m) * jax.lax.rsqrt(v + EPS_LN) * g + b
        key = jax.random.key(seed)
        ks = jax.random.split(key, 20)
        B, T, D, FF, E = (2, 256, 192, 768, 4)
        p = lambda k, shape: jax.random.normal(k, shape, jnp.float32) * 0.02
        return {'src': jax.random.normal(ks[0], (B, T, D), jnp.float32), 'frac': jax.random.uniform(ks[1], (B, T), jnp.float32), 'Wq': p(ks[2], (D, D)), 'bq': jnp.zeros((D,), jnp.float32), 'Wk': p(ks[3], (D, D)), 'bk': jnp.zeros((D,), jnp.float32), 'Wv': p(ks[4], (D, D)), 'bv': jnp.zeros((D,), jnp.float32), 'Wo': p(ks[5], (D, D)), 'bo': jnp.zeros((D,), jnp.float32), 'gamma': jnp.float32(1.0), 'ln1_g': jnp.ones((D,), jnp.float32), 'ln1_b': jnp.zeros((D,), jnp.float32), 'ln2_g': jnp.ones((D,), jnp.float32), 'ln2_b': jnp.zeros((D,), jnp.float32), 'Wg': p(ks[6], (E, D)), 'bg': jnp.zeros((E,), jnp.float32), 'W1': p(ks[7], (E, D, FF)), 'b1': jnp.zeros((E, FF), jnp.float32), 'W2': p(ks[8], (E, FF, D)), 'b2': jnp.zeros((E, D), jnp.float32)}
    _L1_ffn_all = _L1_ffn_setup()
    _L1_ffn_in = {k: v for k, v in _L1_ffn_all.items() if k in ('frac', 'Wq', 'bq', 'Wk', 'bk', 'Wv', 'bv', 'Wo', 'bo', 'gamma', 'ln1_g', 'ln1_b', 'ln2_g', 'ln2_b', 'Wg', 'bg', 'W1', 'b1', 'W2', 'b2')}
    del _L1_ffn_all
    return {'x': x, 'txt': txt, 'L0_tok_stem_w': _L0_tok_in['stem_w'], 'L0_tok_stem_b': _L0_tok_in['stem_b'], 'L0_tok_bn1_g': _L0_tok_in['bn1_g'], 'L0_tok_bn1_b': _L0_tok_in['bn1_b'], 'L0_tok_bn1_m': _L0_tok_in['bn1_m'], 'L0_tok_bn1_v': _L0_tok_in['bn1_v'], 'L0_tok_off_w': _L0_tok_in['off_w'], 'L0_tok_off_b': _L0_tok_in['off_b'], 'L0_tok_dcn_w': _L0_tok_in['dcn_w'], 'L0_tok_dcn_b': _L0_tok_in['dcn_b'], 'L0_tok_bn2_g': _L0_tok_in['bn2_g'], 'L0_tok_bn2_b': _L0_tok_in['bn2_b'], 'L0_tok_bn2_m': _L0_tok_in['bn2_m'], 'L0_tok_bn2_v': _L0_tok_in['bn2_v'], 'L0_attn_W_qkv': _L0_attn_in['W_qkv'], 'L0_attn_b_qkv': _L0_attn_in['b_qkv'], 'L0_ffn_Wg': _L0_ffn_in['Wg'], 'L0_ffn_bg': _L0_ffn_in['bg'], 'L0_ffn_We': _L0_ffn_in['We'], 'L0_ffn_be': _L0_ffn_in['be'], 'L0_ffn_W1': _L0_ffn_in['W1'], 'L0_ffn_b1': _L0_ffn_in['b1'], 'L0_ffn_W2': _L0_ffn_in['W2'], 'L0_ffn_b2': _L0_ffn_in['b2'], 'L1_attn_W_lin': _L1_attn_in['W_lin'], 'L1_attn_b_lin': _L1_attn_in['b_lin'], 'L1_attn_conv_w': _L1_attn_in['conv_w'], 'L1_attn_conv_b': _L1_attn_in['conv_b'], 'L1_attn_W_out': _L1_attn_in['W_out'], 'L1_attn_b_out': _L1_attn_in['b_out'], 'L1_attn_h_param': _L1_attn_in['h_param'], 'L1_attn_win_b': _L1_attn_in['win_b'], 'L1_attn_alphas': _L1_attn_in['alphas'], 'L1_attn_Bmat': _L1_attn_in['Bmat'], 'L1_ffn_frac': _L1_ffn_in['frac'], 'L1_ffn_Wq': _L1_ffn_in['Wq'], 'L1_ffn_bq': _L1_ffn_in['bq'], 'L1_ffn_Wk': _L1_ffn_in['Wk'], 'L1_ffn_bk': _L1_ffn_in['bk'], 'L1_ffn_Wv': _L1_ffn_in['Wv'], 'L1_ffn_bv': _L1_ffn_in['bv'], 'L1_ffn_Wo': _L1_ffn_in['Wo'], 'L1_ffn_bo': _L1_ffn_in['bo'], 'L1_ffn_gamma': _L1_ffn_in['gamma'], 'L1_ffn_ln1_g': _L1_ffn_in['ln1_g'], 'L1_ffn_ln1_b': _L1_ffn_in['ln1_b'], 'L1_ffn_ln2_g': _L1_ffn_in['ln2_g'], 'L1_ffn_ln2_b': _L1_ffn_in['ln2_b'], 'L1_ffn_Wg': _L1_ffn_in['Wg'], 'L1_ffn_bg': _L1_ffn_in['bg'], 'L1_ffn_W1': _L1_ffn_in['W1'], 'L1_ffn_b1': _L1_ffn_in['b1'], 'L1_ffn_W2': _L1_ffn_in['W2'], 'L1_ffn_b2': _L1_ffn_in['b2']}

def reference(x, txt, L0_tok_stem_w, L0_tok_stem_b, L0_tok_bn1_g, L0_tok_bn1_b, L0_tok_bn1_m, L0_tok_bn1_v, L0_tok_off_w, L0_tok_off_b, L0_tok_dcn_w, L0_tok_dcn_b, L0_tok_bn2_g, L0_tok_bn2_b, L0_tok_bn2_m, L0_tok_bn2_v, L0_attn_W_qkv, L0_attn_b_qkv, L0_ffn_Wg, L0_ffn_bg, L0_ffn_We, L0_ffn_be, L0_ffn_W1, L0_ffn_b1, L0_ffn_W2, L0_ffn_b2, L1_attn_W_lin, L1_attn_b_lin, L1_attn_conv_w, L1_attn_conv_b, L1_attn_W_out, L1_attn_b_out, L1_attn_h_param, L1_attn_win_b, L1_attn_alphas, L1_attn_Bmat, L1_ffn_frac, L1_ffn_Wq, L1_ffn_bq, L1_ffn_Wk, L1_ffn_bk, L1_ffn_Wv, L1_ffn_bv, L1_ffn_Wo, L1_ffn_bo, L1_ffn_gamma, L1_ffn_ln1_g, L1_ffn_ln1_b, L1_ffn_ln2_g, L1_ffn_ln2_b, L1_ffn_Wg, L1_ffn_bg, L1_ffn_W1, L1_ffn_b1, L1_ffn_W2, L1_ffn_b2):
    import jax
    import jax.numpy as jnp

    def _L0_tok_ref(x, stem_w, stem_b, bn1_g, bn1_b, bn1_m, bn1_v, off_w, off_b, dcn_w, dcn_b, bn2_g, bn2_b, bn2_m, bn2_v):
        import jax, jax.numpy as jnp
        import numpy as np
        K = 4
        STRIDE = 4
        EPS = 1e-05
        SLOPE = 0.01

        def conv2d(x, w, b, stride):
            out = jax.lax.conv_general_dilated(x, w, (stride, stride), 'VALID', dimension_numbers=('NCHW', 'OIHW', 'NCHW'))
            return out + b[None, :, None, None]

        def batchnorm(x, g, b, m, v):
            inv = g / jnp.sqrt(v + EPS)
            return x * inv[None, :, None, None] + (b - m * inv)[None, :, None, None]

        def leaky_relu(x):
            return jnp.where(x >= 0, x, SLOPE * x)

        def deform_conv(x, offset, w, b):
            B, C, H, W = x.shape
            Ho, Wo = (offset.shape[2], offset.shape[3])
            KK = K * K
            off = offset.reshape(B, KK, 2, Ho, Wo)
            kh = jnp.repeat(jnp.arange(K), K).astype(x.dtype)
            kw = jnp.tile(jnp.arange(K), K).astype(x.dtype)
            base_y = (jnp.arange(Ho) * STRIDE).astype(x.dtype)
            base_x = (jnp.arange(Wo) * STRIDE).astype(x.dtype)
            py = base_y[None, None, :, None] + kh[None, :, None, None] + off[:, :, 0]
            px = base_x[None, None, None, :] + kw[None, :, None, None] + off[:, :, 1]
            y0 = jnp.floor(py)
            x0 = jnp.floor(px)
            wy = py - y0
            wx = px - x0

            def corner(yc, xc):
                yi = yc.astype(jnp.int32)
                xi = xc.astype(jnp.int32)
                valid = (yi >= 0) & (yi < H) & (xi >= 0) & (xi < W)
                yi = jnp.clip(yi, 0, H - 1)
                xi = jnp.clip(xi, 0, W - 1)
                v = jax.vmap(lambda img, a, c: img[:, a, c])(x, yi, xi)
                return v * valid[:, None].astype(x.dtype)
            v00 = corner(y0, x0)
            v01 = corner(y0, x0 + 1)
            v10 = corner(y0 + 1, x0)
            v11 = corner(y0 + 1, x0 + 1)
            wy_ = wy[:, None]
            wx_ = wx[:, None]
            sampled = v00 * (1 - wy_) * (1 - wx_) + v01 * (1 - wy_) * wx_ + v10 * wy_ * (1 - wx_) + v11 * wy_ * wx_
            out = jnp.einsum('bckhw,ock->bohw', sampled, w.reshape(w.shape[0], C, KK))
            return out + b[None, :, None, None]
        h = conv2d(x, stem_w, stem_b, 4)
        h = leaky_relu(batchnorm(h, bn1_g, bn1_b, bn1_m, bn1_v))
        offset = conv2d(h, off_w, off_b, 4)
        h = deform_conv(h, offset, dcn_w, dcn_b)
        h = leaky_relu(batchnorm(h, bn2_g, bn2_b, bn2_m, bn2_v))
        B, C, Ho, Wo = h.shape
        return h.reshape(B, C, Ho * Wo).transpose(0, 2, 1)

    def _L0_attn_ref(x, W_qkv, b_qkv):
        import jax, jax.numpy as jnp
        import numpy as np
        EMBED_DIM = 192
        MAX_LEN = 256
        ALPHA = 0.99
        BATCH = 16

        def _retention_mask(sl, alpha, dtype):
            i = jnp.arange(sl)[:, None]
            j = jnp.arange(sl)[None, :]
            causal = i >= j
            exponent = jnp.where(causal, (i - j).astype(dtype), 0.0)
            decay = jnp.asarray(alpha, dtype) ** exponent
            return jnp.where(causal, decay, jnp.zeros((), dtype))
        bs, sl, d = x.shape
        qkv = x @ W_qkv + b_qkv
        q, k, v = jnp.split(qkv, 3, axis=-1)
        M = _retention_mask(sl, ALPHA, x.dtype)
        scores = jnp.einsum('bsd,btd->bst', q, k) / jnp.sqrt(jnp.asarray(d, x.dtype))
        out = jnp.einsum('bst,btd->bsd', scores * M[None, :, :], v)
        return out

    def _L0_ffn_ref(x, Wg, bg, We, be, W1, b1, W2, b2):
        import jax, jax.numpy as jnp
        import numpy as np
        D = 192
        M = 768
        G = 4
        E = 8
        KG = 2
        KE = 4
        EPS = 1e-06

        def _topk_gates(logits, k):
            top, idx = jax.lax.top_k(logits, k)
            gates = jax.nn.softmax(top, axis=-1)
            gates = jnp.where(gates >= EPS, gates, jnp.zeros_like(gates))
            return (gates, idx)
        orig_shape = x.shape
        xf = x.reshape(-1, D)
        glog = xf @ Wg + bg
        ggates, gidx = _topk_gates(glog, KG)
        gw = jnp.einsum('nk,nkg->ng', ggates, jax.nn.one_hot(gidx, G, dtype=xf.dtype))
        elog = jnp.einsum('nd,gde->nge', xf, We) + be
        egates, eidx = _topk_gates(elog, KE)
        ew = jnp.einsum('ngk,ngke->nge', egates, jax.nn.one_hot(eidx, E, dtype=xf.dtype))
        combine = gw[:, :, None] * ew
        y = jnp.zeros_like(xf)
        for g in range(G):
            h = jax.nn.gelu(jnp.einsum('nd,edm->enm', xf, W1[g]) + b1[g][:, None, :], approximate=False)
            o = jnp.einsum('enm,emd->end', h, W2[g]) + b2[g][:, None, :]
            y = y + jnp.einsum('end,ne->nd', o, combine[:, g, :])
        return y.reshape(orig_shape)

    def _L1_attn_ref(u, W_lin, b_lin, conv_w, conv_b, W_out, b_out, h_param, win_b, alphas, Bmat):
        import jax, jax.numpy as jnp
        import numpy as np
        D = 192
        ORDER = 2
        K = 3
        MAXLEN = 512

        def _fft_conv(h, x, Bp):
            L = x.shape[-1]
            n = 2 * L
            h_f = jnp.fft.rfft(h, n=n, norm='forward')
            x_f = jnp.fft.rfft(x, n=n)
            y = jnp.fft.irfft(h_f * x_f, n=n, norm='forward')[..., :L]
            return y + x * Bp
        Bsz, L, d = u.shape
        z = (u @ W_lin.T + b_lin).transpose(0, 2, 1)
        z = jax.lax.conv_general_dilated(z, conv_w, window_strides=(1,), padding=[(K - 1, K - 1)], feature_group_count=z.shape[1], dimension_numbers=('NCH', 'OIH', 'NCH'))[..., :L] + conv_b[None, :, None]
        xs = [z[:, i * d:(i + 1) * d] for i in range(ORDER)]
        v = z[:, ORDER * d:] + u.transpose(0, 2, 1)
        t = jnp.linspace(0.0, 1.0, MAXLEN, dtype=u.dtype)[None, None, :L]
        h = h_param[:, :, :L] * (jnp.exp(alphas * t) + win_b)
        h = h / jnp.sum(jnp.abs(h), axis=-2, keepdims=True)
        for i in range(ORDER):
            v = v + jax.nn.softmax(xs[i], axis=1) * _fft_conv(h[i][None], v, Bmat[i])
        v = v.transpose(0, 2, 1)
        return v + v @ W_out.T + b_out

    def _L1_ffn_ref(src, frac, Wq, bq, Wk, bk, Wv, bv, Wo, bo, gamma, ln1_g, ln1_b, ln2_g, ln2_b, Wg, bg, W1, b1, W2, b2):
        import jax, jax.numpy as jnp
        import numpy as np
        NHEAD = 12
        EPS_Z = 1e-05
        EPS_LN = 1e-05

        def _zscore_last(t, n):
            m = t.mean(axis=-1, keepdims=True)
            var = ((t - m) ** 2).sum(axis=-1, keepdims=True) / (n - 1)
            return (t - m) / (jnp.sqrt(var) + EPS_Z)

        def _layernorm(x, g, b):
            m = x.mean(axis=-1, keepdims=True)
            v = ((x - m) ** 2).mean(axis=-1, keepdims=True)
            return (x - m) * jax.lax.rsqrt(v + EPS_LN) * g + b
        B, T, D = src.shape
        H = NHEAD
        hd = D // H
        scale = hd ** (-0.5)
        Q = (src @ Wq.T + bq).reshape(B, T, H, hd)
        K = (src @ Wk.T + bk).reshape(B, T, H, hd)
        V = (src @ Wv.T + bv).reshape(B, T, H, hd)
        logits = jnp.einsum('bqhd,bkhd->bhqk', Q, K) * scale
        logits = gamma * _zscore_last(logits, T)
        probs = jax.nn.softmax(logits, axis=-1)
        attn = jnp.einsum('bhqk,bkhd->bqhd', probs, V).reshape(B, T, D)
        attn = attn @ Wo.T + bo
        x = _layernorm(src + attn, ln1_g, ln1_b)
        E = Wg.shape[0]
        gate_scores = jax.nn.softmax(x @ Wg.T + bg, axis=-1)
        top2_val, top2_idx = jax.lax.top_k(gate_scores, 2)
        combine = (jax.nn.one_hot(top2_idx, E, dtype=x.dtype) * top2_val[..., None]).sum(axis=-2)
        h = jax.nn.relu(jnp.einsum('btd,edf->ebtf', x, W1) + b1[:, None, None, :])
        y = jnp.einsum('ebtf,efd->ebtd', h, W2) + b2[:, None, None, :]
        ff = jnp.einsum('ebtd,bte->btd', y, combine)
        return _layernorm(x + ff, ln2_g, ln2_b)
    h = _L0_tok_ref(x, L0_tok_stem_w, L0_tok_stem_b, L0_tok_bn1_g, L0_tok_bn1_b, L0_tok_bn1_m, L0_tok_bn1_v, L0_tok_off_w, L0_tok_off_b, L0_tok_dcn_w, L0_tok_dcn_b, L0_tok_bn2_g, L0_tok_bn2_b, L0_tok_bn2_m, L0_tok_bn2_v)
    h = jnp.concatenate([h, txt], axis=1)
    h = h + _L0_attn_ref(_layernorm(h, axis=-1), L0_attn_W_qkv, L0_attn_b_qkv)
    h = h + _L0_ffn_ref(_layernorm(h, axis=-1), L0_ffn_Wg, L0_ffn_bg, L0_ffn_We, L0_ffn_be, L0_ffn_W1, L0_ffn_b1, L0_ffn_W2, L0_ffn_b2)
    h = h + _L1_attn_ref(_layernorm(h, axis=-1), L1_attn_W_lin, L1_attn_b_lin, L1_attn_conv_w, L1_attn_conv_b, L1_attn_W_out, L1_attn_b_out, L1_attn_h_param, L1_attn_win_b, L1_attn_alphas, L1_attn_Bmat)
    h = h + _L1_ffn_ref(_layernorm(h, axis=-1), L1_ffn_frac, L1_ffn_Wq, L1_ffn_bq, L1_ffn_Wk, L1_ffn_bk, L1_ffn_Wv, L1_ffn_bv, L1_ffn_Wo, L1_ffn_bo, L1_ffn_gamma, L1_ffn_ln1_g, L1_ffn_ln1_b, L1_ffn_ln2_g, L1_ffn_ln2_b, L1_ffn_Wg, L1_ffn_bg, L1_ffn_W1, L1_ffn_b1, L1_ffn_W2, L1_ffn_b2)
    return h

_drawn_inputs = setup_inputs


def setup_inputs(seed=0):
    import zlib

    import numpy as np

    out = dict(_drawn_inputs(seed))
    spreads = {'L1_attn_b_lin': (0.0, 0.1),
     'L1_attn_conv_b': (0.0, 0.1),
     'L1_attn_b_out': (0.0, 0.301),
     'L1_attn_win_b': (0.0, 2.0),
     'L1_ffn_bq': (0.0, 0.8),
     'L1_ffn_bk': (0.0, 2.0),
     'L1_ffn_bv': (0.0, 0.8),
     'L1_ffn_bo': (0.0, 0.423),
     'L1_ffn_ln1_g': (1.0, 0.2),
     'L1_ffn_ln1_b': (0.0, 0.404),
     'L1_ffn_ln2_g': (1.0, 0.2),
     'L1_ffn_ln2_b': (0.0, 0.371),
     'L1_ffn_bg': (0.0, 0.8),
     'L1_ffn_b1': (0.0, 0.8),
     'L1_ffn_b2': (0.0, 0.8)}
    factors = {'L0_ffn_Wg': 4.442,
     'L0_ffn_bg': 8.0,
     'L0_ffn_We': 4.949,
     'L0_ffn_be': 8.0,
     'L0_ffn_W1': 3.567,
     'L0_ffn_b1': 8.0,
     'L0_ffn_W2': 3.419,
     'L0_ffn_b2': 22.463,
     'L1_attn_h_param': 200.0,
     'L1_attn_alphas': 200.0,
     'L1_attn_Bmat': 3.9,
     'L1_ffn_Wq': 8.0,
     'L1_ffn_Wk': 8.0,
     'L1_ffn_Wv': 8.0,
     'L1_ffn_Wo': 7.502,
     'L1_ffn_Wg': 6.652,
     'L1_ffn_W1': 6.642,
     'L1_ffn_W2': 5.346}
    for name, (base, spread) in spreads.items():
        noise = np.random.default_rng([zlib.crc32(name.encode()), seed]).standard_normal(out[name].shape)
        drawn = base * np.exp(spread * noise) if base else spread * noise
        out[name] = jnp.asarray(drawn.astype(out[name].dtype))
    for name, factor in factors.items():
        out[name] = (out[name] * factor).astype(out[name].dtype)
    return out
```

```python
from contextlib import ExitStack

import concourse.bass as bass
from concourse import mybir

F32 = mybir.dt.float32
ALU = mybir.AluOpType
ACT = mybir.ActivationFunctionType
AX = mybir.AxisListType

P = 128
B = 16
PAIRS = B // 2
IMG, TXT = 64, 128
L = IMG + TXT
D = 192
D1 = D - P
PC = 2 * L
CS = 96
HW = 1024
TAPS = 16
OFFC = 2 * TAPS
YCH = HW // P
FF = 768
MC = FF // P
G0, E0 = 4, 8
NX0 = G0 * E0
NX1 = 4
HEADS, HD = 12, 16
LN_EPS = 1e-5
HALF = L // 2
FPITCH = HALF + L
FC = 24
CG = 16
NCG = D // CG


def wait(eng, sem, value):
    if not isinstance(value, int) or value > 0:
        eng.wait_ge(sem, value)


class Chain:

    def __init__(self, eng, sem):
        self.eng, self.sem, self.base, self.n = eng, sem, 0, 0

    def did(self, ins):
        ins.then_inc(self.sem, 1)
        self.n += 1

    def sync(self):
        self.eng.wait_ge(self.sem, self.base + self.n)

    def link(self, ins):
        self.did(ins)
        self.sync()

    def enter(self, index, per):
        self.start, self.per = self.base + self.n, per
        self.base, self.n = index * per + self.start, 0

    def leave(self, turns):
        assert self.n == self.per, (self.n, self.per)
        self.base, self.n = self.start + turns * self.per, 0


class Core:

    def __init__(self, nc, ctx):
        self.nc, self.ctx = nc, ctx
        self.sems = []
        self.h = self.sb(ctx, "h", [P, PAIRS, 3, D])
        self.xn = self.sb(ctx, "xn", [P, PAIRS, 3, D])
        self.xT0 = self.sb(ctx, "xT0", [P, PAIRS * PC])
        self.xT1 = self.sb(ctx, "xT1", [P, PAIRS * PC])
        self.ident = self.sb(ctx, "ident", [P, P])
        self.ones = self.sb(ctx, "ones", [P, P])
        self.eps = self.sb(ctx, "eps", [P, 1])
        self.nought = self.sb(ctx, "nought", [P, 8 * D])
        self.bank = [ctx.enter_context(nc.psum_tensor(f"bank{i}", [P, 512], F32)) for i in range(8)]
        self.setup_done = self.sem("setup_done")
        self.zeroed = self.sem("queue_zeroed")

    def sb(self, ctx, name, shape, dt=F32):
        return ctx.enter_context(self.nc.sbuf_tensor(name, shape, dt))

    def sem(self, name):
        s = self.nc.alloc_semaphore(name=name)
        self.sems.append(s)
        return s

    def clear_semaphores(self):
        self.nc.clear_and_free_semaphores(self.sems)
        self.nc.all_engine_barrier()
        self.sems = []


def bcast_rows(ap, n, parts=P):
    return bass.AP(ap.tensor, ap.offset, [[0, parts], [1, n]])



def setup(k, d):
    nc = k.nc
    loaded, zeroed = k.sem("su_loaded"), k.sem("su_zeroed")
    e_done, sums, act_done, stored = k.sem("su_e"), k.sem("su_sums"), k.sem("su_act"), k.sem("su_stored")
    chain_s = k.sem("su_chain")
    with ExitStack() as ctx, nc.Block() as block:
        tl = k.sb(ctx, "su_t", [P, L])
        par = k.sb(ctx, "su_par", [P, 2, 2])
        hz = k.sb(ctx, "su_h", [P, 2, 2, FPITCH])
        hf = hz[:, :, :, HALF:FPITCH]
        e = k.sb(ctx, "su_exp", [P, 2, L])
        ab = k.sb(ctx, "su_abs", [P, 2, 2, L])
        rec = k.sb(ctx, "su_rec", [P, 2, L])
        parts = (P, D1)

        @block.sync
        def _(sp):
            sp.dma_start(k.ident[:, :], d["ident"]).then_inc(k.setup_done, 16)
            sp.dma_start(tl[:, :], bcast_rows(d["times"], L)).then_inc(loaded, 16)
            for c, n in enumerate(parts):
                sp.dma_start(par[0:n, c, :], d["filter_par"][c * P:c * P + n, :]).then_inc(loaded, 16)
                sp.dma_start(hf[0:n, :, c, :],
                             d["h_param"][:, c * P:c * P + n, 0:L].rearrange("o p l -> p o l")).then_inc(loaded, 16)
            txt = d["txt"].rearrange("(j i) t d -> i t j d", i=2)
            sp.dma_start(k.h[IMG:P, :, 0, :], txt[0, 0:IMG]).then_inc(k.setup_done, 16)
            sp.dma_start(k.h[0:IMG, :, 1, :], txt[0, IMG:TXT]).then_inc(k.setup_done, 16)
            sp.dma_start(k.h[:, :, 2, :], txt[1]).then_inc(k.setup_done, 16)
            sp.wait_ge(zeroed, 2)
            sp.wait_ge(chain_s, 1 + 4 + 4 + 2 + 4)
            for o in range(2):
                for c, n in enumerate(parts):
                    sp.dma_start(d["filters"][o, c * P:c * P + n, :, :],
                                 hz[0:n, o, c, :].unsqueeze(1).broadcast_to([n, FC, FPITCH])).then_inc(stored, 16)
            rows = d["queue"].rearrange("(n p r) d -> p n (r d)", p=P, r=8)
            sp.dma_start(rows, k.nought[:, :].unsqueeze(1).broadcast_to(list(rows.shape))).then_inc(k.zeroed, 16)
            sp.wait_ge(stored, 64)
            sp.wait_ge(k.setup_done, 64)

        @block.gpsimd
        def _(pool):
            nc.gpsimd.memset(hz[:, :, :, 0:HALF], 0.0).then_inc(zeroed, 1)
            pool.wait_ge(zeroed, 1)
            nc.gpsimd.memset(k.nought[:, :], 0.0).then_inc(zeroed, 1)

        @block.scalar
        def _(act):
            act.wait_ge(loaded, 80)
            act.wait_ge(chain_s, 1)
            for c, n in enumerate(parts):
                nc.scalar.activation(e[0:n, c, :], tl[0:n, :], ACT.Exp, scale=par[0:n, c, 0:1]).then_inc(e_done, 1)

        @block.tensor
        def _(pe):
            pe.wait_ge(chain_s, 1 + 4 + 4)
            for o in range(2):
                for c, n in enumerate(parts):
                    nc.tensor.matmul(k.bank[0][:, o * L:o * L + L], k.ones[0:n, :], ab[0:n, o, c, :],
                                     start=(c == 0), stop=(c == 1)).then_inc(sums, 1)

        @block.vector
        def _(dve):
            ch = Chain(dve, chain_s)
            ch.n = 0
            nc.vector.memset(k.eps[:, :], LN_EPS)
            nc.vector.memset(k.xT1[D1:D1 + 1, :], 1.0)
            ch.did(nc.vector.memset(k.ones[:, :], 1.0))
            dve.wait_ge(loaded, 80)
            dve.wait_ge(e_done, 2)
            for o in range(2):
                for c, n in enumerate(parts):
                    ch.did(nc.vector.scalar_tensor_tensor(hf[0:n, o, c, :], e[0:n, c, :], par[0:n, c, 1:2],
                                                          hf[0:n, o, c, :], ALU.add, ALU.mult))
            ch.sync()
            for o in range(2):
                for c, n in enumerate(parts):
                    ch.did(nc.vector.scalar_tensor_tensor(ab[0:n, o, c, :], hf[0:n, o, c, :], -1.0,
                                                          hf[0:n, o, c, :], ALU.mult, ALU.max))
            dve.wait_ge(sums, 4)
            for o in range(2):
                ch.did(nc.vector.reciprocal(rec[:, o, :], k.bank[0][:, o * L:o * L + L]))
            ch.sync()
            for o in range(2):
                for c, n in enumerate(parts):
                    ch.did(nc.vector.tensor_tensor(hf[0:n, o, c, :], hf[0:n, o, c, :], rec[0:n, o, :], ALU.mult))



def tokenizer(k, d):
    nc = k.nc
    S = {n: k.sem("tk_" + n) for n in (
        "consts", "stem", "bn", "leaky", "off", "tr", "pxy", "htcopy", "scr", "hx", "hy",
        "weighted", "sampcopy", "dcn", "bn2", "prep", "act_chain", "dve_chain", "sqrt", "samp_mm")}
    S["patch"], S["bc"] = ([k.sem(f"tk_{n}{u}") for u in range(2)] for n in ("patch", "bc"))
    with ExitStack() as ctx, nc.Block() as block:
        stem_w = k.sb(ctx, "tk_stem_w", [48, CS])
        off_w = k.sb(ctx, "tk_off_w", [CS, TAPS, OFFC])
        dcn_w = k.sb(ctx, "tk_dcn_w", [CS, TAPS, D])
        v96 = k.sb(ctx, "tk_v96", [CS, 5])
        v192 = k.sb(ctx, "tk_v192", [P, 5, D])
        offb = k.sb(ctx, "tk_offb", [OFFC, 1])
        grid = k.sb(ctx, "tk_grid", [OFFC, 64])
        xy = k.sb(ctx, "tk_xy", [P, 1 + YCH])
        pat = k.sb(ctx, "tk_pat", [48, 2, HW])
        pre = k.sb(ctx, "tk_pre", [CS, HW])
        h1 = k.sb(ctx, "tk_h1", [CS, HW])
        pxy = k.sb(ctx, "tk_pxy", [OFFC, 2, 64])
        pos = k.sb(ctx, "tk_pos", [P, 2, TAPS, 2, 64])
        hT = k.sb(ctx, "tk_hT", [P, 2, YCH, CS])
        hx = k.sb(ctx, "tk_hx", [P, HW])
        ab = k.sb(ctx, "tk_ab", [P, 2, HW])
        hy = k.sb(ctx, "tk_hy", [P, 2, HW])
        wt = k.sb(ctx, "tk_wt", [P, 3, HW])
        samp = k.sb(ctx, "tk_samp", [CS, TAPS, 2, 64])
        inv1, sh1 = k.sb(ctx, "tk_inv1", [CS, 1]), k.sb(ctx, "tk_sh1", [CS, 1])
        inv2, sh2 = k.sb(ctx, "tk_inv2", [P, D]), k.sb(ctx, "tk_sh2", [P, D])
        tmp2 = k.sb(ctx, "tk_tmp2", [P, D])
        ps_stem = [k.bank[0], k.bank[1]]
        ps_t = [k.bank[2], k.bank[3]]
        ps_off, ps_dcn = k.bank[4], k.bank[5]
        ps_s = [k.bank[6], k.bank[7]]
        scr = d["positions"]

        @block.sync
        def _(sp):
            for t, name in ((stem_w, "stem_w"), (off_w, "off_w"), (v96, "v96"), (offb, "off_b"), (grid, "grid"),
                            (xy, "xy"), (dcn_w, "dcn_w")):
                flat = t[:] if len(t.shape) == 2 else t[:].rearrange("p a b -> p (a b)")
                sp.dma_start(flat, d[name]).then_inc(S["consts"], 16)
            sp.dma_start(v192[:].rearrange("p a b -> p (a b)"), bcast_rows(d["v192"], 5 * D)).then_inc(S["consts"], 16)

            def load(b, u):
                sp.dma_start(pat[:, u, :], d["patches"][b]).then_inc(S["patch"][u], 16)

            def spread(b, u):
                sp.wait_ge(S["pxy"], b + 1)
                sp.dma_start(scr[b], pxy[:, u, :]).then_inc(S["scr"], 16)
                sp.wait_ge(S["scr"], b * 16 + 16)
                sp.dma_start(pos[:, u, :, :, :].rearrange("p k a s -> p (k a s)"),
                             bass.AP(scr.tensor, b * (OFFC * 64), [[0, P], [1, OFFC * 64]])).then_inc(S["bc"][u], 16)

            load(0, 0)
            load(1, 1)
            with sp.Fori(0, PAIRS - 1) as j:
                for u in range(2):
                    spread(j * 2 + u, u)
                    load(j * 2 + (2 + u), u)
            for u in range(2):
                spread(2 * PAIRS - 2 + u, u)

        @block.tensor
        def _(pe):
            def stem(q, u):
                b = q * 2 + u
                pe.wait_ge(S["patch"][u], q * 16 + 16)
                wait(pe, S["bn"], b)
                for n in range(2):
                    mm = nc.tensor.matmul(ps_stem[n][0:CS, :], stem_w[:, :], pat[:, u, n * 512:n * 512 + 512],
                                          start=True, stop=True)
                mm.then_inc(S["stem"], 1)

            def offsets(b, u):
                pe.wait_ge(S["leaky"], b + 1)
                wait(pe, S["pxy"], b)
                taps = h1[:, :].rearrange("c (a e b f) -> c e f a b", a=8, e=4, b=8)
                for t in range(TAPS):
                    mm = nc.tensor.matmul(ps_off[0:OFFC, 0:64], off_w[:, t, :], taps[:, t // 4, t % 4],
                                          start=(t == 0), stop=(t == TAPS - 1))
                mm.then_inc(S["off"], 1)
                wait(pe, S["htcopy"], b)
                for i in range(YCH):
                    mm = nc.tensor.transpose(ps_t[i // 4][:, i % 4 * CS:i % 4 * CS + CS], h1[:, i * P:i * P + P],
                                             k.ident[0:CS, 0:CS])
                mm.then_inc(S["tr"], 1)

            def sample(b, u):
                pe.wait_ge(S["htcopy"], b + 1)
                wait(pe, S["sampcopy"], b)
                for i in range(YCH):
                    pe.wait_ge(S["weighted"], b * YCH + (i + 1))
                    for n in range(2):
                        mm = nc.tensor.matmul(ps_s[n][0:CS, :], hT[:, u, i, :], wt[:, i % 2, n * 512:n * 512 + 512],
                                              start=(i == 0), stop=(i == YCH - 1))
                    mm.then_inc(S["samp_mm"], 1)

            def deform(j):
                pe.wait_ge(S["sampcopy"], j * 2 + 2)
                wait(pe, S["bn2"], j)
                for t in range(TAPS):
                    mm = nc.tensor.matmul(ps_dcn[:, 0:D], samp[:, t, :, :].rearrange("c u s -> c (u s)"), dcn_w[:, t, :],
                                          start=(t == 0), stop=(t == TAPS - 1))
                mm.then_inc(S["dcn"], 1)

            pe.wait_ge(S["consts"], 128)
            stem(0, 0)
            offsets(0, 0)

            def pair(j, last):
                stem(j, 1)
                offsets(j * 2 + 1, 1)
                sample(j * 2, 0)
                if not last:
                    stem(j + 1, 0)
                    offsets(j * 2 + 2, 0)
                sample(j * 2 + 1, 1)
                deform(j)

            pair(0, False)
            with pe.Fori(1, PAIRS - 1) as j:
                pair(j, False)
            pair(PAIRS - 1, True)

        @block.scalar
        def _(act):
            ch = Chain(act, S["act_chain"])
            act.wait_ge(S["consts"], 128)
            act.wait_ge(S["prep"], 2)
            ch.did(nc.scalar.activation(inv1[:, :], v96[:, 4:5], ACT.Sqrt, bias=k.eps[0:CS, :]))
            nc.scalar.activation(inv2[:, :], v192[:, 4, :], ACT.Sqrt, bias=k.eps[:, :]).then_inc(S["sqrt"], 1)
            act.wait_ge(S["prep"], 6)

            def norm(b, u):
                act.wait_ge(S["stem"], b + 1)
                wait(act, S["leaky"], b)
                for n in range(2):
                    a = nc.scalar.activation(pre[:, n * 512:n * 512 + 512], ps_stem[n][0:CS, :], ACT.Identity,
                                             bias=sh1[:, :], scale=inv1[:, :])
                a.then_inc(S["bn"], 1)

            def hats(q, u):
                b = q * 2 + u
                act.wait_ge(S["bc"][u], q * 16 + 16)
                wait(act, S["weighted"], b * YCH)
                ch.link(nc.scalar.activation(hx[:, :], pos[:, u, :, 1, :], ACT.Abs, bias=xy[:, 0:1]))
                ch.did(nc.scalar.activation(hx[:, :], hx[:, :], ACT.Relu, bias=1.0, scale=-1.0))
                for i in range(YCH):
                    ch.link(nc.scalar.activation(ab[:, i % 2, :], pos[:, u, :, 0, :], ACT.Abs,
                                                 bias=xy[:, 1 + i:2 + i]))
                    if i >= 2:
                        act.wait_ge(S["weighted"], b * YCH + (i - 1))
                    nc.scalar.activation(hy[:, i % 2, :], ab[:, i % 2, :], ACT.Relu, bias=1.0,
                                         scale=-1.0).then_inc(S["hy"], 1)

            per = 2 + YCH
            norm(0, 0)

            def pair(j, last):
                norm(j * 2 + 1, 1)
                hats(j, 0)
                if not last:
                    norm(j * 2 + 2, 0)
                hats(j, 1)

            pair(0, False)
            with act.Fori(1, PAIRS - 1) as j:
                ch.enter(j - 1, 2 * per)
                pair(j, False)
                ch.leave(PAIRS - 2)
            pair(PAIRS - 1, True)

        @block.vector
        def _(dve):
            ch = Chain(dve, S["dve_chain"])
            dve.wait_ge(S["consts"], 128)
            nc.vector.memset(tmp2[:, :], 0.0).then_inc(S["prep"], 2)
            dve.wait_ge(S["sqrt"], 1)
            for inv, sh, v, in ((inv1[:, :], sh1[:, :], [v96[:, i:i + 1] for i in range(5)]),
                                (inv2[:, :], sh2[:, :], [v192[:, i, :] for i in range(5)])):
                ch.link(nc.vector.reciprocal(inv, inv))
                ch.link(nc.vector.tensor_tensor(inv, inv, v[1], ALU.mult))
                ch.link(nc.vector.tensor_tensor(sh, v[0], v[3], ALU.subtract))
                ch.link(nc.vector.tensor_tensor(sh, sh, inv, ALU.mult))
                last = nc.vector.tensor_tensor(sh, sh, v[2], ALU.add)
                last.then_inc(S["prep"], 2)
            dve.wait_ge(S["prep"], 6)

            def leaky(b, u):
                dve.wait_ge(S["bn"], b + 1)
                nc.vector.scalar_tensor_tensor(h1[:, :], pre[:, :], 0.01, pre[:, :], ALU.mult,
                                               ALU.max).then_inc(S["leaky"], 1)

            def where(b, u):
                dve.wait_ge(S["off"], b + 1)
                nc.vector.scalar_tensor_tensor(pxy[:, u, :], ps_off[0:OFFC, 0:64], offb[:, 0:1], grid[:, :],
                                               ALU.add, ALU.add).then_inc(S["pxy"], 1)
                dve.wait_ge(S["tr"], b + 1)
                for n in range(2):
                    c = nc.vector.tensor_copy(hT[:, u, 4 * n:4 * n + 4, :].rearrange("p a c -> p (a c)"),
                                              ps_t[n][:, 0:4 * CS])
                c.then_inc(S["htcopy"], 1)

            def weights(b, u):
                for i in range(YCH):
                    dve.wait_ge(S["hy"], b * YCH + (i + 1))
                    if i >= 2:
                        dve.wait_ge(S["samp_mm"], b * YCH + (i - 1))
                    else:
                        wait(dve, S["samp_mm"], b * YCH + (i - 1) if isinstance(b, int) else b * YCH + (i - 1))
                    nc.vector.tensor_tensor(wt[:, i % 2, :], hy[:, i % 2, :], hx[:, :],
                                            ALU.mult).then_inc(S["weighted"], 1)
                dve.wait_ge(S["samp_mm"], b * YCH + YCH)
                for n in range(2):
                    c = nc.vector.tensor_copy(samp[:, 8 * n:8 * n + 8, u, :],
                                              ps_s[n][0:CS, :].rearrange("c (t s) -> c t s", t=8))
                c.then_inc(S["sampcopy"], 1)

            def norm2(j):
                dve.wait_ge(S["dcn"], j + 1)
                ch.link(nc.vector.tensor_tensor(tmp2[:, :], ps_dcn[:, 0:D], inv2[:, :], ALU.mult))
                ch.link(nc.vector.tensor_tensor(tmp2[:, :], tmp2[:, :], sh2[:, :], ALU.add))
                for t, lo in ((0, 0), (1, IMG)):
                    o = nc.vector.scalar_tensor_tensor(k.h[lo:lo + IMG, j, t, :], tmp2[lo:lo + IMG, :], 0.01,
                                                       tmp2[lo:lo + IMG, :], ALU.mult, ALU.max)
                o.then_inc(S["bn2"], 1)

            leaky(0, 0)
            where(0, 0)

            def pair(j, last):
                leaky(j * 2 + 1, 1)
                where(j * 2 + 1, 1)
                weights(j * 2, 0)
                if not last:
                    leaky(j * 2 + 2, 0)
                    where(j * 2 + 2, 0)
                weights(j * 2 + 1, 1)
                norm2(j)

            pair(0, False)
            with dve.Fori(1, PAIRS - 1) as j:
                ch.enter(j - 1, 2)
                pair(j, False)
                ch.leave(PAIRS - 2)
            pair(PAIRS - 1, True)



def norm(k, name, d, src, affine=None, dst=None):
    nc = k.nc
    S = {n: k.sem(f"{name}_{n}") for n in ("vars", "rstd", "inv", "normed", "turned", "x0", "x1", "chain", "rows")}
    tiles = PAIRS * 3
    with ExitStack() as ctx, nc.Block() as block:
        st = k.sb(ctx, name + "_st", [P, PAIRS, 3, 6])
        mv = k.sb(ctx, name + "_mv", [P, 3, PAIRS, 3])
        rs = k.sb(ctx, name + "_rs", [P, PAIRS, 3])
        gb = k.sb(ctx, name + "_gb", [P, 2, D]) if affine else None
        xn = dst if dst is not None else k.xn

        if affine:
            @block.sync
            def _(sp):
                sp.dma_start(gb[:, :, :].rearrange("p a d -> p (a d)"),
                             bcast_rows(d[affine], 2 * D)).then_inc(S["rows"], 16)
                sp.wait_ge(S["rows"], 16)

        @block.scalar
        def _(act):
            act.wait_ge(S["vars"], 1)
            nc.scalar.activation(rs[:, :, :], mv[:, 1], ACT.Sqrt, bias=k.eps[:, :]).then_inc(S["rstd"], 1)
            if dst is None:
                def copy(j, u):
                    act.wait_ge(S["turned"], j + 1)
                    nc.scalar.activation(k.xT0[:, bass.ds(j * PC, PC)], k.bank[2 * u][:, 0:PC],
                                         ACT.Copy).then_inc(S["x0"], 1)

                with act.Fori(0, PAIRS // 2) as q:
                    copy(q * 2, 0)
                    copy(q * 2 + 1, 1)

        @block.tensor
        def _(pe):
            if dst is None:
                def turn(j, u, first):
                    pe.wait_ge(S["normed"], j + 1)
                    if not first:
                        pe.wait_ge(S["x0"], j - 1)
                        pe.wait_ge(S["x1"], j - 1)
                    for t in range(3):
                        nc.tensor.transpose(k.bank[2 * u][:, t * P:t * P + P], xn[:, j, t, 0:P], k.ident[:, :])
                        mm = nc.tensor.transpose(k.bank[2 * u + 1][0:D1, t * P:t * P + P], xn[:, j, t, P:D],
                                                 k.ident[:, :])
                    mm.then_inc(S["turned"], 1)

                for j in range(PAIRS):
                    turn(j, j % 2, j < 2)

        @block.vector
        def _(dve):
            ch = Chain(dve, S["chain"])
            with dve.Fori(0, PAIRS) as j:
                ch.enter(j, 3)
                for t in range(3):
                    ch.did(nc.vector.bn_stats(st[:, j, t, :], src[:, j, t, :]))
                ch.leave(PAIRS)
            ch.sync()
            half = float(D // 2)
            ch.did(nc.vector.tensor_tensor(mv[:, 0], st[:, :, :, 1], st[:, :, :, 4], ALU.add))
            ch.did(nc.vector.tensor_tensor(mv[:, 1], st[:, :, :, 1], st[:, :, :, 4], ALU.subtract))
            ch.did(nc.vector.tensor_tensor(mv[:, 2], st[:, :, :, 2], st[:, :, :, 5], ALU.add))
            ch.sync()
            ch.did(nc.vector.tensor_scalar(mv[:, 0], mv[:, 0], 0.5, None, ALU.mult))
            ch.link(nc.vector.scalar_tensor_tensor(mv[:, 1], mv[:, 1], 0.25, mv[:, 1], ALU.mult, ALU.mult))
            nc.vector.scalar_tensor_tensor(mv[:, 1], mv[:, 2], 0.5 / half, mv[:, 1], ALU.mult,
                                           ALU.add).then_inc(S["vars"], 1)
            dve.wait_ge(S["rstd"], 1)
            if affine:
                dve.wait_ge(S["rows"], 16)
            nc.vector.reciprocal(rs[:, :, :], rs[:, :, :]).then_inc(S["inv"], 1)
            dve.wait_ge(S["inv"], 1)

            def scale(j):
                for t in range(3):
                    ins = nc.vector.tensor_scalar(xn[:, j, t, :], src[:, j, t, :], mv[:, 0, j, t:t + 1], rs[:, j, t:t + 1],
                                                  ALU.subtract, ALU.mult)
                    if affine:
                        ch.did(ins)
                if affine:
                    ch.sync()
                    for t in range(3):
                        ch.did(nc.vector.tensor_tensor(xn[:, j, t, :], xn[:, j, t, :], gb[:, 0, :], ALU.mult))
                    ch.sync()
                    for t in range(3):
                        ins = nc.vector.tensor_tensor(xn[:, j, t, :], xn[:, j, t, :], gb[:, 1, :], ALU.add)
                ins.then_inc(S["normed"], 1)

            def copy(j, u):
                dve.wait_ge(S["turned"], j + 1)
                nc.vector.tensor_copy(k.xT1[0:D1, bass.ds(j * PC, PC)],
                                      k.bank[2 * u + 1][0:D1, 0:PC]).then_inc(S["x1"], 1)

            if dst is not None:
                with dve.Fori(0, PAIRS) as j:
                    ch.enter(j, 6)
                    scale(j)
                    ch.leave(PAIRS)
            else:
                with dve.Fori(0, PAIRS // 2) as q:
                    ch.enter(q, 12 if affine else 0)
                    scale(q * 2)
                    scale(q * 2 + 1)
                    copy(q * 2, 0)
                    copy(q * 2 + 1, 1)
                    ch.leave(PAIRS // 2)



def retention(k, d):
    nc = k.nc
    S = {n: k.sem("re_" + n) for n in ("loaded", "proj", "qk", "v", "scores", "decayed", "out", "added")}
    with ExitStack() as ctx, nc.Block() as block:
        w0, w1 = k.sb(ctx, "re_w0", [P, 3 * D]), k.sb(ctx, "re_w1", [D1 + 1, 3 * D])
        decay = k.sb(ctx, "re_decay", [P, 2, PC])
        qk = k.sb(ctx, "re_qk", [P, 4, PC])
        v = k.sb(ctx, "re_v", [P, 2, 3, D])
        pt = k.sb(ctx, "re_pt", [P, 2, PC])
        Q0, Q1, K0, K1, V0, V1, R0, R1 = k.bank

        @block.sync
        def _(sp):
            sp.dma_start(w0[:, :], d["qkv"][0:P, :]).then_inc(S["loaded"], 16)
            sp.dma_start(w1[:, :], d["qkv"][P:D + 1, :]).then_inc(S["loaded"], 16)
            sp.dma_start(decay[:, :, :].rearrange("p a b -> p (a b)"), d["decay"]).then_inc(S["loaded"], 16)
            sp.wait_ge(S["loaded"], 48)

        @block.tensor
        def _(pe):
            def project(j):
                c = j * PC
                x0, x1 = k.xT0[:, bass.ds(c, PC)], k.xT1[0:D1 + 1, bass.ds(c, PC)]
                for n, (ps, at) in enumerate(((Q0, 0), (Q1, P), (K0, D), (K1, D + P))):
                    m = P if n % 2 == 0 else D1
                    nc.tensor.matmul(ps[0:m, 0:PC], w0[:, at:at + m], x0, start=True, stop=False)
                    nc.tensor.matmul(ps[0:m, 0:PC], w1[:, at:at + m], x1, start=False, stop=True)
                for t in range(3):
                    ps = V0[:, t * D:t * D + D] if t < 2 else V1[:, 0:D]
                    nc.tensor.matmul(ps, k.xT0[:, bass.ds(c + t * P, P)], w0[:, 2 * D:], start=True, stop=False)
                    mm = nc.tensor.matmul(ps, k.xT1[0:D1 + 1, bass.ds(c + t * P, P)], w1[:, 2 * D:],
                                          start=False, stop=True)
                mm.then_inc(S["proj"], 1)

            def scores(j):
                pe.wait_ge(S["qk"], j + 1)
                wait(pe, S["added"], j)
                for e, keys, m, lo, at, q0, q1 in ((0, 0, P, 0, 0, 0, L), (0, P, 64, 0, L, P, L),
                                                   (1, L, 64, 64, L, L, PC), (1, L + 64, P, 0, 0, L + 64, PC)):
                    ps = (R0, R1)[e][lo:lo + m, at + q0 - e * L:at + q1 - e * L]
                    for n, r in enumerate((P, D1)):
                        mm = nc.tensor.matmul(ps, qk[0:r, 2 + n, keys:keys + m], qk[0:r, n, q0:q1],
                                              start=(n == 0), stop=(n == 1))
                mm.then_inc(S["scores"], 1)

            def mix(j, u):
                pe.wait_ge(S["decayed"], j + 1)
                big0, big2 = pt[:, 0, 0:L], pt[:, 1, 0:L]
                small0, small2 = pt[0:64, 0, L:PC], pt[64:P, 1, L:PC]
                nc.tensor.matmul(R0[:, 0:D], big0[:, 0:P], v[:, u, 0, :], start=True, stop=True)
                nc.tensor.matmul(R1[:, 0:D], big2[:, 64:L], v[:, u, 2, :], start=True, stop=False)
                nc.tensor.matmul(R1[:, 0:D], small2[:, 64:L], v[64:P, u, 1, :], start=False, stop=True)
                nc.tensor.matmul(R0[0:64, D:2 * D], big0[:, P:L], v[:, u, 0, :], start=True, stop=False)
                nc.tensor.matmul(R0[0:64, D:2 * D], small0[:, P:L], v[0:64, u, 1, :], start=False, stop=True)
                nc.tensor.matmul(R0[64:P, D:2 * D], small2[:, 0:64], v[64:P, u, 1, :], start=True,
                                 stop=True).then_inc(S["out"], 1)

            def step(j, u, last=False):
                scores(j)
                if not last:
                    pe.wait_ge(S["v"], j + 1)
                    project(j + 1)
                mix(j, u)

            pe.wait_ge(S["loaded"], 48)
            project(0)
            for j in range(PAIRS):
                step(j, j % 2, j == PAIRS - 1)

        @block.scalar
        def _(act):
            with act.Fori(0, PAIRS) as j:
                act.wait_ge(S["proj"], j + 1)
                for n, ps in enumerate((Q0, Q1, K0, K1)):
                    m = P if n % 2 == 0 else D1
                    a = nc.scalar.activation(qk[0:m, n, :], ps[0:m, 0:PC], ACT.Copy)
                a.then_inc(S["qk"], 1)

        @block.vector
        def _(dve):
            def values(j, u):
                dve.wait_ge(S["proj"], j + 1)
                nc.vector.tensor_copy(v[:, u, 0:2, :].rearrange("p a d -> p (a d)"), V0[:, 0:2 * D])
                nc.vector.tensor_copy(v[:, u, 2, :], V1[:, 0:D]).then_inc(S["v"], 1)

            def step(j, u, last=False):
                dve.wait_ge(S["scores"], j + 1)
                for e, ps, lo, hi, c0, c1 in ((0, R0, 0, P, 0, L), (0, R0, 0, 64, L + P, PC),
                                              (1, R1, 0, P, 64, L), (1, R1, 64, P, L, PC)):
                    o = nc.vector.tensor_tensor(pt[lo:hi, e, c0:c1], ps[lo:hi, c0:c1], decay[lo:hi, e, c0:c1], ALU.mult)
                o.then_inc(S["decayed"], 1)
                if not last:
                    values(j + 1, 1 - u)
                dve.wait_ge(S["out"], j + 1)
                nc.vector.tensor_tensor(k.h[:, j, 0:2, :].rearrange("p a d -> p (a d)"), R0[:, 0:2 * D],
                                        k.h[:, j, 0:2, :].rearrange("p a d -> p (a d)"), ALU.add)
                nc.vector.tensor_tensor(k.h[:, j, 2, :], R1[:, 0:D], k.h[:, j, 2, :], ALU.add).then_inc(S["added"], 1)

            values(0, 0)
            step(0, 0)
            step(1, 1)
            with dve.Fori(1, PAIRS // 2 - 1) as q:
                step(q * 2, 0)
                step(q * 2 + 1, 1)
            step(PAIRS - 2, 0)
            step(PAIRS - 1, 1, True)



def norm_a(k, d):
    norm(k, "na", d, k.h)


def norm_b(k, d):
    norm(k, "nb", d, k.h)



def choose(nc, ch, x, rank, c, chosen, kept):
    n = x.shape[-1]
    for i in range(n):
        ch.did(nc.vector.memset(rank[:, :, i:i + 1], float(n - 1 - i)))
    ch.sync()
    for step in range(1, n):
        m = n - step
        ch.link(nc.vector.tensor_tensor(c[:, :, 0:m], x[:, :, 0:m], x[:, :, step:n], ALU.is_ge))
        ch.link(nc.vector.tensor_tensor(rank[:, :, step:n], rank[:, :, step:n], c[:, :, 0:m], ALU.add))
        ch.link(nc.vector.tensor_tensor(rank[:, :, 0:m], rank[:, :, 0:m], c[:, :, 0:m], ALU.subtract))
    ch.link(nc.vector.tensor_scalar(chosen, rank, kept - 0.5, None, ALU.is_lt))


def over(ap, n):
    return ap.unsqueeze(2).broadcast_to([ap.shape[0], ap.shape[1], n])


def gates(k, d, name, groups, experts, combine, weight, chosen=None):
    nc = k.nc
    tiles = PAIRS * 3
    nx = groups * experts
    cols = nx + (groups if groups > 1 else 0)
    S = {n: k.sem(f"{name}_{n}") for n in ("loaded", "logits", "shift", "exp", "chain")}
    with ExitStack() as ctx, nc.Block() as block:
        w0, w1 = k.sb(ctx, name + "_w0", [P, cols]), k.sb(ctx, name + "_w1", [D1 + 1, cols])
        lg = k.sb(ctx, name + "_lg", [P, tiles, cols])
        n_all = tiles * groups
        xs = [(k.sb(ctx, name + "_xe", [P, n_all, experts]), n_all, experts, 4 if groups > 1 else 2)]
        if groups > 1:
            xs.append((k.sb(ctx, name + "_xg", [P, tiles, groups]), tiles, groups, 2))
        most = [k.sb(ctx, f"{name}_most{i}", [P, n]) for i, (_, n, _, _) in enumerate(xs)]
        rank = k.sb(ctx, name + "_rank", [P, n_all, experts])
        c = k.sb(ctx, name + "_c", [P, n_all, experts])
        sel = [k.sb(ctx, f"{name}_sel{i}", [P, n, m]) for i, (_, n, m, _) in enumerate(xs)]
        tpb = 12

        @block.sync
        def _(sp):
            sp.dma_start(w0[:, :], d[weight][0:P, :]).then_inc(S["loaded"], 16)
            sp.dma_start(w1[:, :], d[weight][P:D + 1, :]).then_inc(S["loaded"], 16)
            sp.wait_ge(S["loaded"], 32)

        @block.tensor
        def _(pe):
            pe.wait_ge(S["loaded"], 32)
            for t in range(tiles):
                ps = k.bank[t // tpb][:, t % tpb * cols:t % tpb * cols + cols]
                nc.tensor.matmul(ps, k.xT0[:, t * P:t * P + P], w0[:, :], start=True, stop=False)
                mm = nc.tensor.matmul(ps, k.xT1[0:D1 + 1, t * P:t * P + P], w1[:, :], start=False, stop=True)
            mm.then_inc(S["logits"], 1)

        @block.scalar
        def _(act):
            act.wait_ge(S["shift"], 1)
            for x, _, _, _ in xs:
                a = nc.scalar.activation(x[:, :, :], x[:, :, :], ACT.Exp)
            a.then_inc(S["exp"], 1)

        @block.vector
        def _(dve):
            ch = Chain(dve, S["chain"])
            dve.wait_ge(S["logits"], 1)
            for i in range(tiles // tpb):
                ch.did(nc.vector.tensor_copy(lg[:, i * tpb:i * tpb + tpb, :].rearrange("p a c -> p (a c)"),
                                             k.bank[i][:, 0:tpb * cols]))
            ch.sync()
            if groups > 1:
                ch.did(nc.vector.tensor_copy(xs[1][0][:, :, :], lg[:, :, 0:groups]))
                ch.link(nc.vector.tensor_copy(xs[0][0][:, :, :].rearrange("p (t g) e -> p t (g e)", g=groups),
                                              lg[:, :, groups:cols]))
            else:
                ch.link(nc.vector.tensor_copy(xs[0][0][:, :, :], lg[:, :, :]))
            for i, (x, n, m, kept) in enumerate(xs):
                choose(nc, ch, x[:, :, :], rank[:, 0:n, 0:m], c[:, 0:n, 0:m], sel[i][:, :, :], kept)
                ch.link(nc.vector.tensor_reduce(most[i][:, :], x[:, :, :], AX.X, ALU.max))
                s = nc.vector.tensor_tensor(x[:, :, :], x[:, :, :], over(most[i][:, :], m), ALU.subtract)
            s.then_inc(S["shift"], 1)
            if chosen is not None:
                ch.did(nc.vector.tensor_tensor(
                    chosen[:, :, :].rearrange("p t (g e) -> p (t g) e", g=groups), sel[0][:, :, :],
                    over(sel[1][:, :, :].rearrange("p t g -> p (t g)"), experts), ALU.mult))
                ch.sync()
            dve.wait_ge(S["exp"], 1)
            for i, (x, n, m, _) in enumerate(xs):
                if groups > 1:
                    ch.link(nc.vector.tensor_tensor(x[:, :, :], x[:, :, :], sel[i][:, :, :], ALU.mult))
                ch.link(nc.vector.tensor_reduce(most[i][:, :], x[:, :, :], AX.X, ALU.add))
                ch.link(nc.vector.reciprocal(most[i][:, :], most[i][:, :]))
                ch.link(nc.vector.tensor_tensor(x[:, :, :], x[:, :, :], over(most[i][:, :], m), ALU.mult))
                if groups > 1:
                    ch.link(nc.vector.tensor_scalar(sel[i][:, :, :], x[:, :, :], 1e-6, None, ALU.is_ge))
                    ch.link(nc.vector.tensor_tensor(x[:, :, :], x[:, :, :], sel[i][:, :, :], ALU.mult))
            if groups > 1:
                ch.link(nc.vector.tensor_tensor(
                    combine[:, :, :].rearrange("p t (g e) -> p (t g) e", g=groups), xs[0][0][:, :, :],
                    over(xs[1][0][:, :, :].rearrange("p t g -> p (t g)"), experts), ALU.mult))
            else:
                ch.link(nc.vector.tensor_tensor(combine[:, :, :], xs[0][0][:, :, :], sel[0][:, :, :], ALU.mult))



def bias(k, d, name, nx, combine, acc, b2n):
    nc = k.nc
    S = {n: k.sem(f"{name}_{n}") for n in ("b2", "ct", "ctcopy", "bias", "added")}
    with ExitStack() as ctx, nc.Block() as block:
        b2 = k.sb(ctx, name + "_b2", [nx, D])
        cT = k.sb(ctx, name + "_cT", [nx, 2, 3 * P])

        @block.sync
        def _(sp):
            sp.dma_start(b2[:, :], d[b2n]).then_inc(S["b2"], 16)

        @block.tensor
        def _(pe):
            pe.wait_ge(S["b2"], 16)
            for j in range(PAIRS):
                u = j % 2
                if j >= 2:
                    pe.wait_ge(S["ctcopy"], j - 1)
                for t in range(3):
                    mm = nc.tensor.transpose(k.bank[6 + u][0:nx, t * P:t * P + P], combine[:, j * 3 + t, :],
                                             k.ident[:, :])
                mm.then_inc(S["ct"], 1)
                pe.wait_ge(S["ctcopy"], j + 1)
                if j:
                    pe.wait_ge(S["added"], j)
                for t in range(3):
                    mm = nc.tensor.matmul(k.bank[3 + t][:, 0:D], cT[:, u, t * P:t * P + P], b2[:, :],
                                          start=True, stop=True)
                mm.then_inc(S["bias"], 1)

        @block.vector
        def _(dve):
            for j in range(PAIRS):
                dve.wait_ge(S["ct"], j + 1)
                nc.vector.tensor_copy(cT[:, j % 2, :], k.bank[6 + j % 2][0:nx, 0:PC]).then_inc(S["ctcopy"], 1)
                dve.wait_ge(S["bias"], j + 1)
                for t in range(3):
                    a = nc.vector.tensor_tensor(acc[:, j, t, :], k.bank[3 + t][:, 0:D], acc[:, j, t, :], ALU.add)
                a.then_inc(S["added"], 1)



def experts(k, d, name, nx, func, combine, acc, w1n, w2n):
    nc = k.nc
    S = {n: k.sem(f"{name}_{n}") for n in ("up", "act", "down", "acc")}
    win = [k.sem(f"{name}_win{u}") for u in range(2)]
    tiles = PAIRS * 3
    UPC, ACC = 3, 24
    with ExitStack() as ctx, nc.Block() as block:
        wa = k.sb(ctx, name + "_wa", [P, 2, FF])
        wb = k.sb(ctx, name + "_wb", [D1 + 1, 2, FF])
        wc = k.sb(ctx, name + "_wc", [P, 2, MC, D])
        hT = k.sb(ctx, name + "_hT", [P, 2, MC, PC])

        @block.sync
        def _(sp):
            def load(e, u):
                w1, w2 = d[w1n], d[w2n]
                sp.dma_start(wa[:, u, :], w1[e, 0:P, :]).then_inc(win[u], 16)
                sp.dma_start(wb[:, u, :], w1[e, P:D + 1, :]).then_inc(win[u], 16)
                sp.dma_start(wc[:, u, :, :].rearrange("p m d -> p (m d)"), w2[e]).then_inc(win[u], 16)

            load(0, 0)
            load(1, 1)
            with sp.Fori(1, nx // 2) as q:
                for u in range(2):
                    sp.wait_ge(S["down"], q * 48 + 24 * (u - 1))
                    load(q * 2 + u, u)
            sp.wait_ge(win[0], nx // 2 * 48)
            sp.wait_ge(win[1], nx // 2 * 48)

        @block.tensor
        def _(pe):
            def up(t, pair, u):
                x0, x1 = k.xT0[:, bass.ds(pair * PC, PC)], k.xT1[0:D1 + 1, bass.ds(pair * PC, PC)]
                for m in range(MC):
                    ps = k.bank[m % 3][:, 0:PC]
                    pe.wait_ge(S["act"], t * MC + (UPC + m - 2))
                    nc.tensor.matmul(ps, wa[:, u, m * P:m * P + P], x0, start=True, stop=False)
                    nc.tensor.matmul(ps, wb[:, u, m * P:m * P + P], x1, start=False,
                                     stop=True).then_inc(S["up"], 1)

            def down(t, v, u):
                for i in range(3):
                    pe.wait_ge(S["acc"], t * 3 + (ACC + i - 2))
                    for m in range(MC):
                        if i == 0:
                            pe.wait_ge(S["act"], t * MC + (UPC + m + 1))
                        mm = nc.tensor.matmul(k.bank[3 + i][:, 0:D], hT[:, v, m, i * P:i * P + P], wc[:, u, m, :],
                                              start=(m == 0), stop=(m == MC - 1))
                    mm.then_inc(S["down"], 1)
                return mm

            with pe.Fori(0, nx // 2) as q:
                for u in range(2):
                    pe.wait_ge(win[u], q * 48 + 48)
                    at = q * 16 + u * PAIRS
                    up(at, 0, u)
                    with pe.Fori(0, PAIRS // 2 - 1) as i:
                        up(at + i * 2 + 1, i * 2 + 1, u)
                        down(at + i * 2, 0, u)
                        up(at + i * 2 + 2, i * 2 + 2, u)
                        down(at + i * 2 + 1, 1, u)
                    up(at + (PAIRS - 1), PAIRS - 1, u)
                    down(at + (PAIRS - 2), 0, u)
                    down(at + (PAIRS - 1), 1, u)

        @block.scalar
        def _(act):
            act.sem_inc(S["act"], UPC)
            with act.Fori(0, nx * PAIRS // 2) as i:
                for v in range(2):
                    for m in range(MC):
                        act.wait_ge(S["up"], i * (2 * MC) + (v * MC + m + 1))
                        nc.scalar.activation(hT[:, v, m, :], k.bank[m % 3][:, 0:PC], func).then_inc(S["act"], 1)

        @block.vector
        def _(dve):
            dve.sem_inc(S["acc"], ACC)
            with dve.Fori(0, nx) as e:
                with dve.Fori(0, PAIRS) as j:
                    for t in range(3):
                        at = e * (3 * PAIRS) + j * 3 + t
                        dve.wait_ge(S["down"], at + 1)
                        dve.wait_ge(S["acc"], at + 1)
                        nc.vector.scalar_tensor_tensor(acc[:, j, t, :], k.bank[3 + t][:, 0:D],
                                                       combine[:, j * 3 + t, bass.ds(e, 1)], acc[:, j, t, :],
                                                       ALU.mult, ALU.add).then_inc(S["acc"], 1)



UNIT = 2 * P
TILES = PAIRS * 3
KEPT = 8
UNITS = (TILES * P * KEPT - NX0) // UNIT + NX0
UNITS += UNITS % 2


def slots(k, d, chosen, combine, index, share, expert_of):
    nc = k.nc
    S = {n: k.sem("sl_" + n) for n in ("loaded", "sums", "chain")}
    NB = TILES * NX0 // 2
    with ExitStack() as ctx, nc.Block() as block:
        before = k.sb(ctx, "sl_before", [P, P])
        number = k.sb(ctx, "sl_number", [1, UNITS])
        key = k.sb(ctx, "sl_key", [P, TILES, NX0])
        tot = k.sb(ctx, "sl_tot", [P, TILES, NX0])
        run = k.sb(ctx, "sl_run", [P, TILES + 1, NX0])
        whole = k.sb(ctx, "sl_whole", [P, NX0], mybir.dt.int32)
        ends = k.sb(ctx, "sl_ends", [P, 2, NX0])
        top = k.sb(ctx, "sl_top", [P, TILES, KEPT])
        past = k.sb(ctx, "sl_past", [1, UNITS, NX0])
        exp = k.sb(ctx, "sl_exp", [1, UNITS])

        @block.sync
        def _(sp):
            sp.dma_start(before[:, :], d["before"]).then_inc(S["loaded"], 16)
            sp.dma_start(number[:, :], d["unit_numbers"]).then_inc(S["loaded"], 16)
            sp.wait_ge(S["loaded"], 32)

        @block.tensor
        def _(pe):
            pe.wait_ge(S["loaded"], 32)
            flat = chosen[:, :, :].rearrange("p t e -> p (t e)")
            for i in range(2):
                nc.tensor.matmul(k.bank[i][:, 0:NB], before[:, :], flat[:, i * NB:i * NB + NB], start=True, stop=True)
                mm = nc.tensor.matmul(k.bank[2 + i][:, 0:NB], k.ones[:, :], flat[:, i * NB:i * NB + NB],
                                      start=True, stop=True)
            mm.then_inc(S["sums"], 1)

        @block.vector
        def _(dve):
            ch = Chain(dve, S["chain"])
            ch.did(nc.vector.memset(run[:, 0, :], 0.0))
            dve.wait_ge(S["sums"], 1)
            for i in range(2):
                half = slice(i * TILES // 2, (i + 1) * TILES // 2)
                ch.did(nc.vector.tensor_copy(key[:, half, :].rearrange("p t e -> p (t e)"), k.bank[i][:, 0:NB]))
                ch.did(nc.vector.tensor_copy(tot[:, half, :].rearrange("p t e -> p (t e)"), k.bank[2 + i][:, 0:NB]))
            ch.sync()
            for t in range(TILES):
                ch.link(nc.vector.tensor_tensor(run[:, t + 1, :], run[:, t, :], tot[:, t, :], ALU.add))
            ch.link(nc.vector.tensor_scalar(ends[:, 0, :], run[:, TILES, :], float(UNIT - 1), None, ALU.add))
            ch.link(nc.vector.tensor_copy(whole[:, :], ends[:, 0, :]))
            ch.link(nc.vector.tensor_scalar(whole[:, :], whole[:, :], UNIT.bit_length() - 1, None,
                                            ALU.arith_shift_right))
            ch.link(nc.vector.tensor_copy(ends[:, 0, :], whole[:, :]))
            a, step = 0, 1
            while step < NX0:
                ch.did(nc.vector.tensor_copy(ends[:, 1 - a, 0:step], ends[:, a, 0:step]))
                ch.link(nc.vector.tensor_tensor(ends[:, 1 - a, step:NX0], ends[:, a, step:NX0],
                                                ends[:, a, 0:NX0 - step], ALU.add))
                a, step = 1 - a, 2 * step
            ch.did(nc.vector.tensor_tensor(key[:, :, :], key[:, :, :], run[:, 0:TILES, :], ALU.add))
            ch.link(nc.vector.tensor_scalar(ends[:, 1 - a, 1:NX0], ends[:, a, 0:NX0 - 1], float(UNIT), 1.0,
                                            ALU.mult, ALU.add))
            ch.link(nc.vector.memset(ends[:, 1 - a, 0:1], 1.0))
            ch.link(nc.vector.tensor_tensor(key[:, :, :], key[:, :, :],
                                            ends[:, 1 - a, :].unsqueeze(1).broadcast_to([P, TILES, NX0]), ALU.add))
            ch.link(nc.vector.tensor_tensor(key[:, :, :], key[:, :, :], chosen[:, :, :], ALU.mult))
            for t in range(TILES):
                ch.did(nc.vector.max(top[:, t, :], key[:, t, :]))
            ch.sync()
            ch.did(nc.vector.tensor_scalar(index[:, :, :], top[:, :, :], -1.0, None, ALU.add))
            ch.link(nc.vector.tensor_tensor(past[:, :, :], ends[0:1, a, :].unsqueeze(1).broadcast_to([1, UNITS, NX0]),
                                            over(number[:, :], NX0), ALU.is_le))
            ch.link(nc.vector.tensor_reduce(exp[:, :], past[:, :, :], AX.X, ALU.add))
            ch.link(nc.vector.tensor_scalar(expert_of[:, :], exp[:, :], float(NX0 - 1), None, ALU.min))
            for i in range(KEPT):
                ch.link(nc.vector.tensor_tensor(tot[:, :, :], key[:, :, :],
                                                top[:, :, i:i + 1].broadcast_to([P, TILES, NX0]), ALU.is_equal))
                ch.link(nc.vector.tensor_tensor(tot[:, :, :], tot[:, :, :], combine[:, :, :], ALU.mult))
                ch.link(nc.vector.tensor_reduce(share[:, :, i], tot[:, :, :], AX.X, ALU.add))


def routed(k, d, index, share, expert_of):
    nc = k.nc
    S = {n: k.sem("ro_" + n) for n in ("sent", "turned", "x", "up", "act", "down", "y", "added")}
    w_in, x_in, y_out = ([k.sem(f"ro_{n}{v}") for v in range(2)] for n in ("w", "xin", "yout"))
    got = [k.sem(f"ro_got{i}") for i in range(KEPT)]
    queue, answers = d["queue"], d["answers"]
    UPC, YC = 3, 4
    with ExitStack() as ctx, nc.Block() as block:
        wa = k.sb(ctx, "ro_wa", [P, 2, FF])
        wb = k.sb(ctx, "ro_wb", [D1 + 1, 2, FF])
        wc = k.sb(ctx, "ro_wc", [P, 2, MC, D])
        xq = k.sb(ctx, "ro_xq", [P, 2, 2, D])
        g0, g1 = k.sb(ctx, "ro_g0", [P, UNIT]), k.sb(ctx, "ro_g1", [D1 + 1, UNIT])
        hT = k.sb(ctx, "ro_hT", [P, 2, MC, UNIT])
        y = k.sb(ctx, "ro_y", [P, 2, 2, D])
        back = k.sb(ctx, "ro_back", [P, KEPT, D])
        tile = k.h[:].rearrange("p j t d -> p (j t) d")
        xt = k.xn[:].rearrange("p j t d -> p (j t) d")

        @block.gpsimd
        def _(pool):
            pool.wait_ge(k.zeroed, 16)
            for t in range(TILES):
                for i in range(KEPT):
                    nc.gpsimd.indirect_dma_start(
                        out=queue, out_offset=bass.IndirectOffsetOnAxis(ap=index[:, t, i:i + 1], axis=0),
                        in_=xt[:, t, :], in_offset=None).then_inc(S["sent"], 16)
            for v in range(2):
                pool.wait_ge(y_out[v], UNITS // 2 * 16 + 16)
            for t in range(TILES):
                for i in range(KEPT):
                    if t:
                        pool.wait_ge(S["added"], (t - 1) * KEPT + i + 1)
                    nc.gpsimd.indirect_dma_start(
                        out=back[:, i, :], out_offset=None, in_=answers,
                        in_offset=bass.IndirectOffsetOnAxis(ap=index[:, t, i:i + 1], axis=0)).then_inc(got[i], 16)

        @block.sync
        def _(sp):
            def load(t, v):
                expert = sp.value_load(expert_of[0:1, bass.ds(t, 1)], min_val=0, max_val=NX0 - 1)
                sp.dma_start(wa[:, v, :], d["w1_0"][expert, 0:P, :]).then_inc(w_in[v], 16)
                sp.dma_start(wb[:, v, :], d["w1_0"][expert, P:D + 1, :]).then_inc(w_in[v], 16)
                sp.dma_start(wc[:, v, :, :].rearrange("p m d -> p (m d)"), d["w2_0"][expert]).then_inc(w_in[v], 16)

            def load_x(t, v):
                sp.dma_start(xq[:, v, :, :],
                             queue[bass.ds(t * UNIT, UNIT), :].rearrange("(i p) d -> p i d", p=P)).then_inc(x_in[v], 16)

            def save(t, v):
                sp.wait_ge(S["y"], t * 2 + (YC + 2))
                sp.dma_start(answers[bass.ds(t * UNIT, UNIT), :].rearrange("(i p) d -> p i d", p=P),
                             y[:, v, :, :]).then_inc(y_out[v], 16)

            for v in range(2):
                load(v, v)
            sp.wait_ge(S["sent"], TILES * KEPT * 16)
            for v in range(2):
                load_x(v, v)
            with sp.Fori(0, UNITS // 2 - 1) as q:
                for v in range(2):
                    sp.wait_ge(S["down"], q * 4 + (2 * v + 2))
                    load(q * 2 + (v + 2), v)
                    load_x(q * 2 + (v + 2), v)
                    save(q * 2 + v, v)
            for v in range(2):
                save(UNITS - 2 + v, v)

        @block.tensor
        def _(pe):
            def turn(q, v):
                pe.wait_ge(x_in[v], q * 16 + 16)
                for i in range(2):
                    nc.tensor.transpose(k.bank[3][:, i * P:i * P + P], xq[:, v, i, 0:P], k.ident[:, :])
                    mm = nc.tensor.transpose(k.bank[3][0:D1, UNIT + i * P:UNIT + i * P + P], xq[:, v, i, P:D],
                                             k.ident[:, :])
                mm.then_inc(S["turned"], 1)

            def up(q, v):
                t = q * 2 + v
                pe.wait_ge(w_in[v], q * 48 + 48)
                pe.wait_ge(S["x"], t + 1)
                for m in range(MC):
                    ps = k.bank[m % 3][:, 0:UNIT]
                    pe.wait_ge(S["act"], t * MC + (UPC + m - 2))
                    nc.tensor.matmul(ps, wa[:, v, m * P:m * P + P], g0[:, :], start=True, stop=False)
                    nc.tensor.matmul(ps, wb[:, v, m * P:m * P + P], g1[:, :], start=False,
                                     stop=True).then_inc(S["up"], 1)

            def down(q, v):
                t = q * 2 + v
                for i in range(2):
                    pe.wait_ge(S["y"], t * 2 + (YC + i - 3))
                    for m in range(MC):
                        if i == 0:
                            pe.wait_ge(S["act"], t * MC + (UPC + m + 1))
                        mm = nc.tensor.matmul(k.bank[4 + 2 * v + i][:, 0:D], hT[:, v, m, i * P:i * P + P],
                                              wc[:, v, m, :], start=(m == 0), stop=(m == MC - 1))
                    mm.then_inc(S["down"], 1)

            turn(0, 0)
            with pe.Fori(0, UNITS // 2 - 1) as q:
                up(q, 0)
                turn(q, 1)
                down(q, 0)
                up(q, 1)
                turn(q + 1, 0)
                down(q, 1)
            q = UNITS // 2 - 1
            up(q, 0)
            turn(q, 1)
            down(q, 0)
            up(q, 1)
            down(q, 1)

        @block.scalar
        def _(act):
            act.sem_inc(S["act"], UPC)
            with act.Fori(0, UNITS // 2) as q:
                for v in range(2):
                    for m in range(MC):
                        act.wait_ge(S["up"], q * (2 * MC) + (v * MC + m + 1))
                        nc.scalar.activation(hT[:, v, m, :], k.bank[m % 3][:, 0:UNIT], ACT.Gelu).then_inc(S["act"], 1)

        @block.vector
        def _(dve):
            nc.vector.memset(g1[D1:D1 + 1, :], 1.0)
            dve.sem_inc(S["y"], YC)
            for v in range(2):
                dve.sem_inc(y_out[v], 16)

            def turned(t):
                dve.wait_ge(S["turned"], t + 1)
                nc.vector.tensor_copy(g0[:, :], k.bank[3][:, 0:UNIT])
                nc.vector.tensor_copy(g1[0:D1, :], k.bank[3][0:D1, UNIT:2 * UNIT]).then_inc(S["x"], 1)

            def out(q, v):
                t = q * 2 + v
                dve.wait_ge(y_out[v], q * 16 + 16)
                for i in range(2):
                    dve.wait_ge(S["down"], t * 2 + (i + 1))
                    nc.vector.tensor_copy(y[:, v, i, :], k.bank[4 + 2 * v + i][:, 0:D]).then_inc(S["y"], 1)

            turned(0)
            with dve.Fori(0, UNITS // 2 - 1) as q:
                turned(q * 2 + 1)
                out(q, 0)
                turned(q * 2 + 2)
                out(q, 1)
            turned(UNITS - 1)
            out(UNITS // 2 - 1, 0)
            out(UNITS // 2 - 1, 1)
            for t in range(TILES):
                for i in range(KEPT):
                    dve.wait_ge(got[i], 16 * t + 16)
                    if i:
                        dve.wait_ge(S["added"], t * KEPT + i)
                    nc.vector.scalar_tensor_tensor(tile[:, t, :], back[:, i, :], share[:, t, i:i + 1], tile[:, t, :],
                                                   ALU.mult, ALU.add).then_inc(S["added"], 1)


def experts0(k, d):
    with ExitStack() as ctx:
        index = k.sb(ctx, "index", [P, TILES, KEPT], mybir.dt.uint32)
        share = k.sb(ctx, "share", [P, TILES, KEPT])
        expert_of = k.sb(ctx, "expert_of", [1, UNITS], mybir.dt.int32)
        combine = k.sb(ctx, "combine0", [P, TILES, NX0])
        with ExitStack() as own:
            chosen = k.sb(own, "chosen0", [P, TILES, NX0])
            gates(k, d, "g0", G0, E0, combine, "gate0", chosen)
            bias(k, d, "b0", NX0, combine, k.h, "b2_0")
            slots(k, d, chosen, combine, index, share, expert_of)
        routed(k, d, index, share, expert_of)



def norm_c(k, d):
    norm(k, "nc", d, k.h)


def hyena(k, d):
    nc = k.nc
    S = {n: k.sem("hy_" + n) for n in ("loaded", "z", "zs", "conv", "turned", "zcopy", "shift", "exp", "chain",
                                       "long", "upd", "vt", "vt0", "vt1", "out", "added", "wout")}
    tin = [k.sem(f"hy_tin{u}") for u in range(2)]
    NT = 2 * B
    CH = 5
    with ExitStack() as ctx:
        z = k.sb(ctx, "hy_z", [HALF, NT, 3 * D])
        bm = k.sb(ctx, "hy_b", [HALF, 2, D])
        wo0, wo1 = k.sb(ctx, "hy_wo0", [P, D]), k.sb(ctx, "hy_wo1", [D1 + 1, D])
        with ExitStack() as own, nc.Block() as block:
            w0, w1 = k.sb(own, "hy_w0", [P, 3 * D]), k.sb(own, "hy_w1", [D1 + 1, 3 * D])
            cw = k.sb(own, "hy_cw", [P, CH, 4])
            zs = k.sb(own, "hy_zs", [P, 2, PC])
            zc = k.sb(own, "hy_zc", [P, 2, PC])

            @block.sync
            def _(sp):
                for dst, src in ((w0[:, :], d["w_lin"][0:P, :]), (w1[:, :], d["w_lin"][P:D + 1, :]),
                                 (cw[:, :, :].rearrange("p a b -> p (a b)"), d["conv"]),
                                 (bm[:, :, :].rearrange("p a b -> p (a b)"), bcast_rows(d["bmat"], 2 * D, HALF)),
                                 (wo0[:, :], d["w_out"][0:P, :]), (wo1[:, :], d["w_out"][P:D + 1, :])):
                    sp.dma_start(dst, src).then_inc(S["loaded"], 16)
                sp.wait_ge(S["loaded"], 96)

            units = [(j, c) for j in range(PAIRS) for c in range(CH)]

            @block.tensor
            def _(pe):
                pe.wait_ge(S["loaded"], 96)
                def linear(n):
                    j, c = units[n]
                    m = P if c < CH - 1 else D1
                    if n >= 2:
                        pe.wait_ge(S["zs"], n - 1)
                    ps = k.bank[n % 2][0:m, 0:PC]
                    nc.tensor.matmul(ps, w0[:, c * P:c * P + m], k.xT0[:, j * PC:j * PC + PC], start=True, stop=False)
                    nc.tensor.matmul(ps, w1[:, c * P:c * P + m], k.xT1[0:D1 + 1, j * PC:j * PC + PC], start=False,
                                     stop=True).then_inc(S["z"], 1)

                def turn(n):
                    j, c = units[n]
                    m = P if c < CH - 1 else D1
                    pe.wait_ge(S["conv"], n + 1)
                    if n >= 2:
                        pe.wait_ge(S["zcopy"], n - 1)
                    for i in range(4):
                        mm = nc.tensor.transpose(k.bank[2 + n % 2][0:HALF, i * P:i * P + m],
                                                 zc[0:m, n % 2, i * HALF:i * HALF + HALF], k.ident[0:m, 0:m])
                    mm.then_inc(S["turned"], 1)

                linear(0)
                linear(1)
                for n in range(len(units)):
                    if n + 2 < len(units):
                        linear(n + 2)
                    turn(n)

            @block.scalar
            def _(act):
                def out(n):
                    j, c = units[n]
                    m = P if c < CH - 1 else D1
                    act.wait_ge(S["z"], n + 1)
                    if n >= 2:
                        act.wait_ge(S["conv"], n - 1)
                    nc.scalar.activation(zs[0:m, n % 2, :], k.bank[n % 2][0:m, 0:PC], ACT.Copy).then_inc(S["zs"], 1)

                def back(n):
                    j, c = units[n]
                    m = P if c < CH - 1 else D1
                    act.wait_ge(S["turned"], n + 1)
                    nc.scalar.activation(z[:, 4 * j:4 * j + 4, c * P:c * P + m],
                                         k.bank[2 + n % 2][0:HALF, :].rearrange("p (a b) -> p a b", a=4)[:, :, 0:m],
                                         ACT.Copy).then_inc(S["zcopy"], 1)

                out(0)
                out(1)
                for n in range(len(units)):
                    if n + 2 < len(units):
                        out(n + 2)
                    back(n)

            @block.vector
            def _(dve):
                ch = Chain(dve, S["chain"])
                dve.wait_ge(S["loaded"], 96)
                ch.did(nc.vector.tensor_tensor(wo0[:, 0:P], wo0[:, 0:P], k.ident[:, :], ALU.add))
                ch.did(nc.vector.tensor_tensor(wo1[0:D1, P:D], wo1[0:D1, P:D], k.ident[0:D1, 0:D1], ALU.add))
                for n, (j, c) in enumerate(units):
                    m = P if c < CH - 1 else D1
                    dve.wait_ge(S["zs"], n + 1)
                    if n >= 2:
                        dve.wait_ge(S["turned"], n - 1)
                    src = zs[0:m, n % 2, :].rearrange("p (b l) -> p b l", b=2)
                    dst = zc[0:m, n % 2, :].rearrange("p (b l) -> p b l", b=2)
                    ch.link(nc.vector.tensor_scalar(dst, src, cw[0:m, c, 2:3], cw[0:m, c, 3:4], ALU.mult, ALU.add))
                    if c >= 3:
                        x = (k.xT0, k.xT1)[c - 3][0:m, j * PC:j * PC + PC].rearrange("p (b l) -> p b l", b=2)
                        ch.link(nc.vector.tensor_tensor(dst, dst, x, ALU.add))
                    ch.link(nc.vector.scalar_tensor_tensor(dst[:, :, 1:L], src[:, :, 0:L - 1], cw[0:m, c, 1:2],
                                                           dst[:, :, 1:L], ALU.mult, ALU.add))
                    nc.vector.scalar_tensor_tensor(dst[:, :, 2:L], src[:, :, 0:L - 2], cw[0:m, c, 0:1],
                                                   dst[:, :, 2:L], ALU.mult, ALU.add).then_inc(S["conv"], 1)

        with ExitStack() as own, nc.Block() as block:
            most = k.sb(own, "hy_most", [HALF, 2, NT])
            T = k.sb(own, "hy_T", [HALF, 2, CG, L])
            tmp = k.sb(own, "hy_tmp", [HALF, NT, CG])
            v = z[:, :, 2 * D:3 * D]
            hp = d["filters"]

            @block.sync
            def _(sp):
                def load(g, o):
                    for s in range(0, HALF, FC):
                        src = bass.AP(hp.tensor, g * (CG * FC * FPITCH) + (o * D * FC * FPITCH + HALF - s),
                                      [[FPITCH - 1, FC], [FC * FPITCH, CG], [1, L]])
                        sp.dma_start(T[s:s + FC, o, :, :], src).then_inc(tin[o], 16)

                for o in range(2):
                    load(0, o)
                with sp.Fori(1, NCG) as g:
                    for o in range(2):
                        sp.wait_ge(S["long"], g * 2 + (o - 1))
                        load(g, o)
                for o in range(2):
                    sp.wait_ge(tin[o], NCG * 16 * (HALF // FC))

            @block.tensor
            def _(pe):
                with pe.Fori(0, NCG) as g:
                    for o in range(2):
                        pe.wait_ge(tin[o], g * (16 * (HALF // FC)) + 16 * (HALF // FC))
                        pe.wait_ge(S["upd"], g * 2 + (o + 1))
                        ps = k.bank[o][0:HALF, :].rearrange("p (c n) -> p c n", c=CG)
                        for c in range(CG):
                            vc = v[:, :, bass.ds(g * CG + c, 1)]
                            nc.tensor.matmul(ps[:, c, :], T[:, o, c, 0:HALF], vc.rearrange("p n a -> p (n a)"),
                                             start=True, stop=False)
                            first = v.rearrange("p (b i) c -> p b i c", i=2)[:, :, 0, bass.ds(g * CG + c, 1)]
                            mm = nc.tensor.matmul(ps.rearrange("p c (b i) -> p c b i", i=2)[:, c, :, 1],
                                                  T[:, o, c, HALF:L], first.rearrange("p b a -> p (b a)"),
                                                  start=False, stop=True)
                        mm.then_inc(S["long"], 1)

            @block.scalar
            def _(act):
                act.wait_ge(S["shift"], 1)
                nc.scalar.activation(z[:, :, 0:2 * D], z[:, :, 0:2 * D], ACT.Exp).then_inc(S["exp"], 1)

            @block.vector
            def _(dve):
                ch = Chain(dve, S["chain"])
                ch.n = 0
                base = sum(2 if c < 3 else 3 for c in range(CH)) * PAIRS + 2
                ch.base = base
                dve.wait_ge(S["chain"], base)
                x = [z[:, :, o * D:o * D + D] for o in range(2)]
                for o in range(2):
                    ch.did(nc.vector.tensor_reduce(most[:, o, :], x[o], AX.X, ALU.max))
                ch.sync()
                for o in range(2):
                    ins = nc.vector.tensor_tensor(x[o], x[o], over(most[:, o, :], D), ALU.subtract)
                ins.then_inc(S["shift"], 1)
                dve.wait_ge(S["exp"], 1)
                for o in range(2):
                    ch.link(nc.vector.tensor_reduce(most[:, o, :], x[o], AX.X, ALU.add))
                    ch.link(nc.vector.reciprocal(most[:, o, :], most[:, o, :]))
                for o in range(2):
                    ch.did(nc.vector.tensor_tensor(x[o], x[o], over(most[:, o, :], D), ALU.mult))
                ch.sync()
                dve.sem_inc(S["upd"], 1)
                with dve.Fori(0, NCG) as g:
                    ch.enter(g, 6)
                    for o in range(2):
                        vg = v[:, :, bass.ds(g * CG, CG)]
                        xg = x[o][:, :, bass.ds(g * CG, CG)]
                        ps = k.bank[o][0:HALF, :].rearrange("p (c n) -> p n c", c=CG)
                        bg = bm[:, o, bass.ds(g * CG, CG)].unsqueeze(1).broadcast_to([HALF, NT, CG])
                        dve.wait_ge(S["upd"], g * 2 + (o + 1))
                        ch.link(nc.vector.tensor_tensor(tmp[:, :, :], vg, bg, ALU.mult))
                        dve.wait_ge(S["long"], g * 2 + (o + 1))
                        ch.link(nc.vector.tensor_tensor(tmp[:, :, :], ps, tmp[:, :, :], ALU.add))
                        ch.link(nc.vector.tensor_tensor(tmp[:, :, :], tmp[:, :, :], xg, ALU.mult))
                        nc.vector.tensor_tensor(vg, vg, tmp[:, :, :], ALU.add).then_inc(S["upd"], 1)
                    ch.leave(NCG)

        with ExitStack() as own, nc.Block() as block:
            v = z[:, :, 2 * D:3 * D]

            @block.tensor
            def _(pe):
                for j in range(PAIRS):
                    u = j % 2
                    if j >= 2:
                        pe.wait_ge(S["vt0"], j - 1)
                        pe.wait_ge(S["vt1"], j - 1)
                    for i in range(4):
                        nc.tensor.transpose(k.bank[u][:, i * HALF:i * HALF + HALF], v[:, 4 * j + i, 0:P],
                                            k.ident[0:HALF, 0:HALF])
                        mm = nc.tensor.transpose(k.bank[2 + u][0:D1, i * HALF:i * HALF + HALF], v[:, 4 * j + i, P:D],
                                                 k.ident[0:HALF, 0:HALF])
                    mm.then_inc(S["vt"], 1)
                for j in range(PAIRS):
                    pe.wait_ge(S["vt0"], j + 1)
                    pe.wait_ge(S["vt1"], j + 1)
                    if j:
                        pe.wait_ge(S["added"], j)
                    for t in range(3):
                        at = j * PC + t * P
                        nc.tensor.matmul(k.bank[4 + t][:, 0:D], k.xT0[:, at:at + P], wo0[:, :], start=True, stop=False)
                        mm = nc.tensor.matmul(k.bank[4 + t][:, 0:D], k.xT1[0:D1 + 1, at:at + P], wo1[:, :],
                                              start=False, stop=True)
                    mm.then_inc(S["out"], 1)

            @block.scalar
            def _(act):
                for j in range(PAIRS):
                    act.wait_ge(S["vt"], j + 1)
                    nc.scalar.activation(k.xT0[:, j * PC:j * PC + PC], k.bank[j % 2][:, 0:PC],
                                         ACT.Copy).then_inc(S["vt0"], 1)

            @block.vector
            def _(dve):
                for j in range(PAIRS):
                    dve.wait_ge(S["vt"], j + 1)
                    nc.vector.tensor_copy(k.xT1[0:D1, j * PC:j * PC + PC],
                                          k.bank[2 + j % 2][0:D1, 0:PC]).then_inc(S["vt1"], 1)
                for j in range(PAIRS):
                    dve.wait_ge(S["out"], j + 1)
                    for t in range(3):
                        a = nc.vector.tensor_tensor(k.h[:, j, t, :], k.bank[4 + t][:, 0:D], k.h[:, j, t, :], ALU.add)
                    a.then_inc(S["added"], 1)



def norm_d(k, d):
    norm(k, "nd", d, k.h)


def attention(k, d):
    nc = k.nc
    names = ("loaded", "consts", "staged", "kq", "kt", "qt", "vals", "qtok", "qcopy", "s1", "stats", "sd", "rt",
             "aug", "turned", "qat", "s2", "probs", "pv", "attn", "at", "at0", "at1", "out", "added", "chain",
             "zero", "sign", "dev")
    S = {n: k.sem("at_" + n) for n in names}
    HC = 3
    NCH = HEADS // HC
    HP = HC * 32
    N_S = 3 * HEADS // 2
    with ExitStack() as ctx, nc.Block() as block:
        wq0, wq1 = k.sb(ctx, "at_wq0", [P, NCH * HP]), k.sb(ctx, "at_wq1", [D1 + 1, NCH * HP])
        wk0, wk1 = k.sb(ctx, "at_wk0", [P, NCH * HP]), k.sb(ctx, "at_wk1", [D1 + 1, NCH * HP])
        w0, w1 = k.sb(ctx, "at_w0", [P, 3, D]), k.sb(ctx, "at_w1", [D1 + 1, 3, D])
        gam = k.sb(ctx, "at_gamma", [P, 3])
        x0, x1 = k.sb(ctx, "at_x0", [P, PC]), k.sb(ctx, "at_x1", [D1 + 1, PC])
        kT, qT = k.sb(ctx, "at_kT", [HP, NCH, PC]), k.sb(ctx, "at_qT", [HP, NCH, PC])
        va = k.sb(ctx, "at_va", [P, 3, HEADS, HD + 1])
        qa = k.sb(ctx, "at_qa", [P, 3, HEADS, 32])
        qaT = k.sb(ctx, "at_qaT", [HP, NCH, PC])
        st = k.sb(ctx, "at_st", [P, 3 * HEADS, 6])
        mx = k.sb(ctx, "at_mx", [P, 3 * HEADS])
        dv = k.sb(ctx, "at_dv", [P, 3, 3 * HEADS])
        pT = k.sb(ctx, "at_pT", [P, 3, HEADS, L])
        rec = k.sb(ctx, "at_rec", [P, 3, HEADS])
        att = k.sb(ctx, "at_att", [P, 3, D])
        a0, a1 = k.sb(ctx, "at_a0", [P, PC]), k.sb(ctx, "at_a1", [D1 + 1, PC])
        bank = k.bank
        Q_BANKS = ((0, 0), (0, D), (1, 0))
        V_BANKS = ((2, 0), (2, D), (3, 0))
        O_BANKS = ((5, 0), (5, D), (6, 0))
        PARTS = (((0, P, 0),), ((0, 64, 0), (64, P, L)), ((0, P, L),))
        S1B, S2B = 6, (4, 5, 6, 7)

        def pair_of(n):
            t, m, i = n // (HEADS // 2), n % (HEADS // 2) // HC, n % HC
            return t, (2 * HC * m + i, 2 * HC * m + i + HC)

        def two(ap, heads):
            return ap[:, heads[0]:heads[1] + 1:HC]

        @block.sync
        def _(sp):
            for dst, src in ((wq0, d["wq_heads"][0:P, :]), (wq1, d["wq_heads"][P:D + 1, :]),
                             (wk0, d["wk_heads"][0:P, :]), (wk1, d["wk_heads"][P:D + 1, :])):
                sp.dma_start(dst[:, :], src).then_inc(S["loaded"], 16)
            for n, w in enumerate(("wq", "wv", "wo")):
                sp.dma_start(w0[:, n, :], d[w][0:P, :]).then_inc(S["loaded"], 16)
                sp.dma_start(w1[:, n, :], d[w][P:D + 1, :]).then_inc(S["loaded"], 16)
            sp.dma_start(gam[:, 0:1], bcast_rows(d["gamma"], 1)).then_inc(S["loaded"], 16)
            sp.wait_ge(S["loaded"], 176)

        @block.gpsimd
        def _(pool):
            nc.gpsimd.memset(qa[:, :, :, :].rearrange("p a b c -> p (a b c)"), 0.0).then_inc(S["zero"], 1)
            pool.wait_ge(S["zero"], 1)
            nc.gpsimd.memset(va[:, :, :, :].rearrange("p a b c -> p (a b c)"), 1.0).then_inc(S["zero"], 1)
            pool.wait_ge(S["zero"], 2)
            nc.gpsimd.memset(a1[D1:D1 + 1, :], 1.0).then_inc(S["zero"], 1)
            pool.wait_ge(S["zero"], 3)

            def stage(j):
                nc.gpsimd.tensor_copy(x0[:, :], k.xT0[:, bass.ds(j * PC, PC)]).then_inc(S["staged"], 1)
                pool.wait_ge(S["staged"], j * 2 + 1)
                nc.gpsimd.tensor_copy(x1[:, :], k.xT1[0:D1 + 1, bass.ds(j * PC, PC)]).then_inc(S["staged"], 1)

            stage(0)
            with pool.Fori(1, PAIRS) as j:
                pool.wait_ge(S["qtok"], j)
                pool.wait_ge(S["staged"], j * 2)
                stage(j)

        @block.tensor
        def _(pe):
            pe.wait_ge(S["loaded"], 176)
            pe.wait_ge(S["zero"], 3)
            with pe.Fori(0, PAIRS) as j:
                pe.wait_ge(S["staged"], j * 2 + 2)
                pe.wait_ge(S["added"], j + 1)
                for wa, wb, b in ((wk0, wk1, 0), (wq0, wq1, NCH)):
                    for c in range(NCH):
                        ps = bank[b + c][0:HP, 0:PC]
                        nc.tensor.matmul(ps, wa[:, c * HP:c * HP + HP], x0[:, :], start=True, stop=False)
                        mm = nc.tensor.matmul(ps, wb[:, c * HP:c * HP + HP], x1[:, :], start=False, stop=True)
                    mm.then_inc(S["kq"], 1)

                def tokens(n, places):
                    for t, (b, at) in enumerate(places):
                        nc.tensor.matmul(bank[b][:, at:at + D], x0[:, t * P:t * P + P], w0[:, n, :],
                                         start=True, stop=False)
                        mm = nc.tensor.matmul(bank[b][:, at:at + D], x1[:, t * P:t * P + P], w1[:, n, :],
                                              start=False, stop=True)
                    return mm

                pe.wait_ge(S["kt"], j + 1)
                tokens(1, V_BANKS).then_inc(S["vals"], 1)
                tokens(0, Q_BANKS).then_inc(S["qtok"], 1)
                pe.wait_ge(S["qt"], j + 1)
                pe.wait_ge(S["qcopy"], j + 1)
                for n in range(N_S):
                    t, heads = pair_of(n)
                    if n >= S1B:
                        pe.wait_ge(S["stats"], j * N_S + (n - S1B + 1))
                    for i, h in enumerate(heads):
                        r, c = 32 * (h % HC), h // HC
                        for lo, hi, b0 in PARTS[t]:
                            mm = nc.tensor.matmul(bank[n % S1B][lo:hi, i * L:i * L + L],
                                                  qT[r:r + HD, c, t * P + lo:t * P + hi],
                                                  kT[r:r + HD, c, b0:b0 + L], start=True, stop=True)
                    mm.then_inc(S["s1"], 1)
                pe.wait_ge(S["aug"], j + 1)
                for c in range(NCH):
                    for t in range(3):
                        mm = nc.tensor.transpose(bank[c][0:HP, t * P:t * P + P],
                                                 qa[:, t, HC * c:HC * c + HC, :].rearrange("p a b -> p (a b)"),
                                                 k.ident[:, :])
                mm.then_inc(S["turned"], 1)
                pe.wait_ge(S["qat"], j + 1)
                for n in range(N_S):
                    t, heads = pair_of(n)
                    if n >= len(S2B):
                        pe.wait_ge(S["probs"], j * N_S + (n - len(S2B) + 1))
                    for i, h in enumerate(heads):
                        r, c = 32 * (h % HC), h // HC
                        for lo, hi, b0 in PARTS[t]:
                            mm = nc.tensor.matmul(bank[S2B[n % len(S2B)]][lo:hi, i * L:i * L + L],
                                                  kT[r:r + HD + 1, c, t * P + lo:t * P + hi],
                                                  qaT[r:r + HD + 1, c, b0:b0 + L], start=True, stop=True)
                    mm.then_inc(S["s2"], 1)
                pe.wait_ge(S["probs"], j * N_S + N_S)
                for t in range(3):
                    for lo, hi, b0 in PARTS[t]:
                        q0 = t * P + lo - b0
                        e = b0 // L
                        big, s0 = 2 * e, 64 * e
                        for h in range(HEADS):
                            o = bank[t][lo:hi, h * (HD + 1):(h + 1) * (HD + 1)]
                            nc.tensor.matmul(o, pT[:, big, h, q0:q0 + hi - lo], va[:, big, h, :],
                                             start=True, stop=False)
                            mm = nc.tensor.matmul(o, pT[s0:s0 + 64, 1, h, q0:q0 + hi - lo],
                                                  va[s0:s0 + 64, 1, h, :], start=False, stop=True)
                    mm.then_inc(S["pv"], 1)
                pe.wait_ge(S["attn"], j * 3 + 3)
                for t in range(3):
                    nc.tensor.transpose(bank[7][:, t * P:t * P + P], att[:, t, 0:P], k.ident[:, :])
                    mm = nc.tensor.transpose(bank[3][0:D1, t * P:t * P + P], att[:, t, P:D], k.ident[:, :])
                mm.then_inc(S["at"], 1)
                pe.wait_ge(S["at0"], j + 1)
                pe.wait_ge(S["at1"], j + 1)
                for t, (b, at) in enumerate(O_BANKS):
                    nc.tensor.matmul(bank[b][:, at:at + D], a0[:, t * P:t * P + P], w0[:, 2, :], start=True, stop=False)
                    mm = nc.tensor.matmul(bank[b][:, at:at + D], a1[:, t * P:t * P + P], w1[:, 2, :], start=False,
                                          stop=True)
                mm.then_inc(S["out"], 1)

        @block.scalar
        def _(act):
            act.wait_ge(S["loaded"], 176)
            nc.scalar.activation(gam[:, 1:2], gam[:, 0:1], ACT.Sign).then_inc(S["sign"], 1)
            nc.scalar.activation(gam[:, 2:3], gam[:, 0:1], ACT.Abs).then_inc(S["sign"], 1)
            act.wait_ge(S["consts"], 1)
            with act.Fori(0, PAIRS) as j:
                act.wait_ge(S["kq"], j * 2 + 1)
                for c in range(NCH):
                    a = nc.scalar.activation(kT[:, c, :], bank[c][0:HP, 0:PC], ACT.Copy)
                a.then_inc(S["kt"], 1)
                act.wait_ge(S["kq"], j * 2 + 2)
                for c in range(NCH):
                    a = nc.scalar.activation(qT[:, c, :], bank[NCH + c][0:HP, 0:PC], ACT.Copy, scale=gam[0:HP, 1:2])
                a.then_inc(S["qt"], 1)
                act.wait_ge(S["dev"], j + 1)
                nc.scalar.activation(dv[:, 1, :], dv[:, 0, :], ACT.Sqrt).then_inc(S["sd"], 1)
                act.wait_ge(S["turned"], j + 1)
                for c in range(NCH):
                    a = nc.scalar.activation(qaT[:, c, :], bank[c][0:HP, 0:PC], ACT.Copy)
                a.then_inc(S["qat"], 1)
                for n in range(N_S):
                    t, heads = pair_of(n)
                    act.wait_ge(S["s2"], j * N_S + (n + 1))
                    nc.scalar.activation(two(pT[:, t], heads),
                                         bank[S2B[n % len(S2B)]][:, 0:2 * L].rearrange("p (a b) -> p a b", a=2),
                                         ACT.Exp).then_inc(S["probs"], 1)
                act.wait_ge(S["at"], j + 1)
                nc.scalar.activation(a0[:, :], bank[7][:, 0:PC], ACT.Copy).then_inc(S["at0"], 1)

        @block.vector
        def _(dve):
            ch = Chain(dve, S["chain"])
            dve.wait_ge(S["sign"], 2)
            nc.vector.tensor_scalar(gam[:, 1:2], gam[:, 1:2], float(HD) ** -0.5, None,
                                    ALU.mult).then_inc(S["consts"], 1)
            dve.wait_ge(S["consts"], 1)
            dve.wait_ge(S["zero"], 3)
            dve.sem_inc(S["added"], 1)
            with dve.Fori(0, PAIRS) as j:
                ch.enter(j, 3 + 2 * N_S + 4 + 3 + 3 + 3)
                dve.wait_ge(S["vals"], j + 1)
                for t, (b, at) in enumerate(V_BANKS):
                    ch.did(nc.vector.tensor_copy(va[:, t, :, 0:HD],
                                                 bank[b][:, at:at + D].rearrange("p (h e) -> p h e", h=HEADS)))
                dve.wait_ge(S["qtok"], j + 1)
                for t, (b, at) in enumerate(Q_BANKS):
                    a = nc.vector.tensor_scalar(qa[:, t, :, 0:HD],
                                                bank[b][:, at:at + D].rearrange("p (h e) -> p h e", h=HEADS),
                                                gam[:, 1:2], None, ALU.mult)
                a.then_inc(S["qcopy"], 1)
                for n in range(N_S):
                    t, heads = pair_of(n)
                    dve.wait_ge(S["s1"], j * N_S + (n + 1))
                    ps = bank[n % S1B][:, 0:2 * L].rearrange("p (a b) -> p a b", a=2)
                    for i, h in enumerate(heads):
                        ch.did(nc.vector.bn_stats(st[:, t * HEADS + h, :], ps[:, i, :]))
                    nc.vector.tensor_reduce(two(mx[:, t * HEADS:t * HEADS + HEADS], heads), ps, AX.X, ALU.max).then_inc(S["stats"], 1)
                ch.sync()
                dve.wait_ge(S["stats"], j * N_S + N_S)
                ch.did(nc.vector.tensor_tensor(dv[:, 0, :], st[:, :, 1], st[:, :, 4], ALU.subtract))
                ch.did(nc.vector.tensor_tensor(dv[:, 1, :], st[:, :, 2], st[:, :, 5], ALU.add))
                ch.sync()
                ch.link(nc.vector.scalar_tensor_tensor(dv[:, 0, :], dv[:, 0, :], L / 4, dv[:, 0, :], ALU.mult, ALU.mult))
                ch.link(nc.vector.tensor_tensor(dv[:, 0, :], dv[:, 0, :], dv[:, 1, :], ALU.add))
                nc.vector.tensor_scalar(dv[:, 0, :], dv[:, 0, :], 1.0 / (L - 1), None, ALU.mult).then_inc(S["dev"], 1)
                dve.wait_ge(S["sd"], j + 1)
                ch.link(nc.vector.tensor_scalar(dv[:, 1, :], dv[:, 1, :], 1e-5, None, ALU.add))
                ch.link(nc.vector.reciprocal(dv[:, 1, :], dv[:, 1, :]))
                ch.link(nc.vector.tensor_scalar(dv[:, 2, :], dv[:, 1, :], gam[:, 2:3], None, ALU.mult))
                r = dv[:, 2, :].rearrange("p (t h) -> p t h", t=3)
                for t in range(3):
                    ch.did(nc.vector.tensor_tensor(qa[:, t, :, 0:HD], qa[:, t, :, 0:HD], over(r[:, t, :], HD),
                                                   ALU.mult))
                nc.vector.scalar_tensor_tensor(qa[:, :, :, HD], mx[:, :].rearrange("p (t h) -> p t h", t=3), -1.0, r,
                                               ALU.mult, ALU.mult).then_inc(S["aug"], 1)
                for t in range(3):
                    dve.wait_ge(S["pv"], j * 3 + (t + 1))
                    o = bank[t][:, 0:HEADS * (HD + 1)].rearrange("p (h e) -> p h e", h=HEADS)
                    ch.link(nc.vector.reciprocal(rec[:, t, :], o[:, :, HD]))
                    nc.vector.tensor_tensor(att[:, t, :].rearrange("p (h e) -> p h e", h=HEADS), o[:, :, 0:HD],
                                            over(rec[:, t, :], HD), ALU.mult).then_inc(S["attn"], 1)
                dve.wait_ge(S["at"], j + 1)
                nc.vector.tensor_copy(a1[0:D1, :], bank[3][0:D1, 0:PC]).then_inc(S["at1"], 1)
                dve.wait_ge(S["out"], j + 1)
                for t, (b, at) in enumerate(O_BANKS):
                    a = nc.vector.tensor_tensor(k.xn[:, j, t, :], bank[b][:, at:at + D], k.xn[:, j, t, :], ALU.add)
                a.then_inc(S["added"], 1)
                ch.leave(PAIRS)


def norm_e(k, d):
    norm(k, "ne", d, k.xn, affine="ln1")


def experts1(k, d):
    with ExitStack() as ctx:
        combine = k.sb(ctx, "combine1", [P, PAIRS * 3, NX1])
        gates(k, d, "g1", 1, NX1, combine, "gate1")
        bias(k, d, "b1", NX1, combine, k.xn, "b2_1")
        experts(k, d, "x1", NX1, ACT.Relu, combine, k.xn, "w1_1", "w2_1")


def finish(k, d):
    nc = k.nc
    norm(k, "nf", d, k.xn, affine="ln2", dst=k.xn)
    done = k.sem("fi_done")
    with nc.Block() as block:
        @block.vector
        def _(dve):
            nc.vector.tensor_tensor(k.h[:].rearrange("p a b c -> p (a b c)"),
                                    k.h[:].rearrange("p a b c -> p (a b c)"),
                                    k.xn[:].rearrange("p a b c -> p (a b c)"), ALU.add).then_inc(done, 1)


PHASES = (setup, tokenizer, norm_a, retention, norm_b, experts0, norm_c, hyena, norm_d, attention, norm_e, experts1,
          finish)



def store(k, out):
    nc = k.nc
    stored = k.sem("stored")
    with nc.Block() as block:
        @block.sync
        def _(sp):
            tiles = out.rearrange("b l d -> (b l) d").rearrange("(j t p) d -> p j t d", t=3, p=P)
            sp.dma_start(tiles, k.h[:, :, :, :]).then_inc(stored, 16)
            sp.wait_ge(stored, 16)


def program(nc, d, out):
    d = dict(d)
    for name, shape in (("filters", (2, D, FC, FPITCH)), ("positions", (B, OFFC, 64)),
                    ("queue", (UNITS * UNIT, D)), ("answers", (UNITS * UNIT, D))):
        d[name] = nc.dram_tensor(name + "_scratch", shape, F32, kind="Internal").ap()
    with ExitStack() as ctx:
        k = Core(nc, ctx)
        for phase in PHASES:
            phase(k, d)
            if phase is experts0:
                k.clear_semaphores()
        store(k, out)



def lay_out(i):
    import numpy as np

    def rows(w, b):
        return np.concatenate([w, b.reshape(w.shape[:-2] + (1, w.shape[-1]))], axis=-2)

    def heads(w, b, one):
        full = rows(w, b)
        out = np.zeros((D + 1, HEADS, 32), np.float32)
        out[:, :, 0:HD] = full.reshape(D + 1, HEADS, HD)
        if one:
            out[D, :, HD] = 1.0
        return out.reshape(D + 1, HEADS * 32)

    part = np.arange(P)
    a = {}
    a["patches"] = i["x"].reshape(B, 3, 32, 4, 32, 4).transpose(0, 1, 3, 5, 2, 4).reshape(B, 48, HW)
    a["txt"] = i["txt"]
    a["stem_w"] = i["L0_tok_stem_w"].reshape(CS, 48).T
    a["v96"] = np.stack([i["L0_tok_" + n] for n in ("stem_b", "bn1_g", "bn1_b", "bn1_m", "bn1_v")], 1)
    a["v192"] = np.stack([i["L0_tok_" + n] for n in ("dcn_b", "bn2_g", "bn2_b", "bn2_m", "bn2_v")]).reshape(-1)
    a["off_w"] = i["L0_tok_off_w"].transpose(1, 2, 3, 0).reshape(CS, TAPS * OFFC)
    a["off_b"] = i["L0_tok_off_b"].reshape(OFFC, 1)
    a["dcn_w"] = i["L0_tok_dcn_w"].transpose(1, 2, 3, 0).reshape(CS, TAPS * D)
    tap, o = np.arange(TAPS), np.arange(8)
    gy = (4 * o[None, :, None] + (tap // 4)[:, None, None]) + 0 * o[None, None, :]
    gx = (4 * o[None, None, :] + (tap % 4)[:, None, None]) + 0 * o[None, :, None]
    a["grid"] = np.stack([gy, gx], 1).reshape(OFFC, 64).astype(np.float32)
    a["xy"] = -np.concatenate([(part % 32)[:, None], 4 * np.arange(YCH)[None, :] + (part // 32)[:, None]],
                              1).astype(np.float32)
    a["ident"] = np.eye(P, dtype=np.float32)
    a["times"] = np.linspace(0.0, 1.0, 512, dtype=np.float32)[0:L]
    a["h_param"] = i["L1_attn_h_param"]
    a["filter_par"] = np.stack([i["L1_attn_alphas"].reshape(D), i["L1_attn_win_b"].reshape(D)], 1)
    at = np.arange(L)
    dist = at[None, :] - at[:, None]
    decay = np.where(dist >= 0, np.float32(0.99) ** np.maximum(dist, 0).astype(np.float32), 0)
    decay = (decay / np.sqrt(np.float32(D))).astype(np.float32)
    a["decay"] = np.zeros((P, 2, 2, L), np.float32)
    a["decay"][:, 0, 0], a["decay"][0:64, 0, 1] = decay[0:P], decay[P:L]
    a["decay"][64:P, 1, 1], a["decay"][:, 1, 0] = decay[0:64], decay[64:L]
    a["decay"] = a["decay"].reshape(P, 4 * L)
    a["qkv"] = rows(i["L0_attn_W_qkv"], i["L0_attn_b_qkv"])
    we = i["L0_ffn_We"].transpose(1, 0, 2).reshape(D, NX0)
    a["gate0"] = rows(np.concatenate([i["L0_ffn_Wg"], we], 1),
                      np.concatenate([i["L0_ffn_bg"], i["L0_ffn_be"].reshape(-1)]))
    a["w1_0"] = rows(i["L0_ffn_W1"].reshape(NX0, D, FF), i["L0_ffn_b1"].reshape(NX0, FF))
    a["w2_0"] = i["L0_ffn_W2"].reshape(NX0, MC, P, D).transpose(0, 2, 1, 3).reshape(NX0, P, MC * D)
    a["before"] = (part[:, None] < part[None, :]).astype(np.float32)
    a["unit_numbers"] = np.arange(UNITS, dtype=np.float32)[None, :]
    a["b2_0"] = i["L0_ffn_b2"].reshape(NX0, D)
    a["w_lin"] = rows(i["L1_attn_W_lin"].T, i["L1_attn_b_lin"])
    conv = np.zeros((5 * P, 4), np.float32)
    conv[0:3 * D, 0:3] = i["L1_attn_conv_w"].reshape(3 * D, 3)
    conv[0:3 * D, 3] = i["L1_attn_conv_b"]
    a["conv"] = conv.reshape(5, P, 4).transpose(1, 0, 2).reshape(P, 20)
    a["bmat"] = i["L1_attn_Bmat"].reshape(2 * D)
    a["w_out"] = rows(i["L1_attn_W_out"].T, i["L1_attn_b_out"])
    a["wq_heads"] = heads(i["L1_ffn_Wq"].T, i["L1_ffn_bq"], False)
    a["wk_heads"] = heads(i["L1_ffn_Wk"].T, i["L1_ffn_bk"], True)
    a["wq"] = rows(i["L1_ffn_Wq"].T, i["L1_ffn_bq"])
    a["wv"] = rows(i["L1_ffn_Wv"].T, i["L1_ffn_bv"])
    a["wo"] = rows(i["L1_ffn_Wo"].T, i["L1_ffn_bo"])
    a["gamma"] = i["L1_ffn_gamma"].reshape(1)
    a["ln1"] = np.concatenate([i["L1_ffn_ln1_g"], i["L1_ffn_ln1_b"]])
    a["ln2"] = np.concatenate([i["L1_ffn_ln2_g"], i["L1_ffn_ln2_b"]])
    a["gate1"] = rows(i["L1_ffn_Wg"].T, i["L1_ffn_bg"])
    a["w1_1"] = rows(i["L1_ffn_W1"], i["L1_ffn_b1"])
    a["w2_1"] = i["L1_ffn_W2"].reshape(NX1, MC, P, D).transpose(0, 2, 1, 3).reshape(NX1, P, MC * D)
    a["b2_1"] = i["L1_ffn_b2"]
    return {n: np.ascontiguousarray(v) for n, v in a.items()}


def kernel(**inputs):
    import numpy as np
    import concourse.bacc as bacc
    from concourse.bass_utils import run_bass_kernel_spmd

    arrays = lay_out({n: np.asarray(v) for n, v in inputs.items()})
    nc = bacc.Bacc("TRN2", target_bir_lowering=False, num_devices=1)
    d = {n: nc.dram_tensor("in_" + n, a.shape, F32, kind="ExternalInput").ap() for n, a in arrays.items()}
    out = nc.dram_tensor("out", (B, L, D), F32, kind="ExternalOutput").ap()
    program(nc, d, out)
    r = run_bass_kernel_spmd(nc, [{"in_" + n: a for n, a in arrays.items()}], core_ids=[0])
    return r.results[0]["out"]
```

```python
from contextlib import ExitStack

import concourse.bass as bass
from concourse import mybir

F32 = mybir.dt.float32
F32R = mybir.dt.float32r
ALU = mybir.AluOpType
ACT = mybir.ActivationFunctionType
AX = mybir.AxisListType

P = 128
B = 16
PAIRS = B // 2
IMG, TXT = 64, 128
L = IMG + TXT
D = 192
D1 = D - P
PC = 2 * L
CS = 96
HW = 1024
TAPS = 16
OFFC = 2 * TAPS
YCH = HW // P
FF = 768
MC = FF // P
G0, E0 = 4, 8
NX0 = G0 * E0
NX1 = 4
HEADS, HD = 12, 16
LN_EPS = 1e-5
HALF = L // 2
FPITCH = HALF + L
FC = 24
CG = 16
NCG = D // CG


def wait(eng, sem, value):
    if not isinstance(value, int) or value > 0:
        eng.wait_ge(sem, value)


class Chain:

    def __init__(self, eng, sem):
        self.eng, self.sem, self.base, self.n = eng, sem, 0, 0

    def did(self, ins):
        ins.then_inc(self.sem, 1)
        self.n += 1

    def sync(self):
        self.eng.wait_ge(self.sem, self.base + self.n)

    def link(self, ins):
        self.did(ins)
        self.sync()

    def enter(self, index, per):
        self.start, self.per = self.base + self.n, per
        self.base, self.n = index * per + self.start, 0

    def leave(self, turns):
        assert self.n == self.per, (self.n, self.per)
        self.base, self.n = self.start + turns * self.per, 0


class Core:

    def __init__(self, nc, ctx):
        self.nc, self.ctx = nc, ctx
        self.sems = []
        self.h = self.sb(ctx, "h", [P, PAIRS, 3, D])
        self.xn = self.sb(ctx, "xn", [P, PAIRS, 3, D])
        self.xT0 = self.sb(ctx, "xT0", [P, PAIRS * PC])
        self.xT1 = self.sb(ctx, "xT1", [P, PAIRS * PC])
        self.ident = self.sb(ctx, "ident", [P, P])
        self.ones = self.sb(ctx, "ones", [P, P])
        self.eps = self.sb(ctx, "eps", [P, 1])
        self.nought = self.sb(ctx, "nought", [P, 8 * D])
        self.hz = self.sb(ctx, "hz", [P, 2, 2, FPITCH])
        self.bank = [ctx.enter_context(nc.psum_tensor(f"bank{i}", [P, 512], F32)) for i in range(8)]
        self.setup_done = self.sem("setup_done")
        self.zeroed = self.sem("queue_zeroed")
        self.filters_stored = self.sem("filters_stored")

    def sb(self, ctx, name, shape, dt=F32):
        return ctx.enter_context(self.nc.sbuf_tensor(name, shape, dt))

    def sem(self, name):
        s = self.nc.alloc_semaphore(name=name)
        self.sems.append(s)
        return s

    def clear_semaphores(self):
        self.nc.clear_and_free_semaphores(self.sems)
        self.nc.all_engine_barrier()
        self.sems = []


def bcast_rows(ap, n, parts=P):
    return bass.AP(ap.tensor, ap.offset, [[0, parts], [1, n]])



def setup(k, d):
    nc = k.nc
    loaded, zeroed = k.sem("su_loaded"), k.sem("su_zeroed")
    e_done, sums = k.sem("su_e"), k.sem("su_sums")
    chain_s = k.sem("su_chain")
    with ExitStack() as ctx, nc.Block() as block:
        tl = k.sb(ctx, "su_t", [P, L])
        par = k.sb(ctx, "su_par", [P, 2, 2])
        hz = k.hz
        hf = hz[:, :, :, HALF:FPITCH]
        e = k.sb(ctx, "su_exp", [P, 2, L])
        ab = k.sb(ctx, "su_abs", [P, 2, 2, L])
        rec = k.sb(ctx, "su_rec", [P, 2, L])
        parts = (P, D1)

        @block.sync
        def _(sp):
            sp.dma_start(k.ident[:, :], d["ident"]).then_inc(k.setup_done, 16)
            sp.dma_start(tl[:, :], bcast_rows(d["times"], L)).then_inc(loaded, 16)
            for c, n in enumerate(parts):
                sp.dma_start(par[0:n, c, :], d["filter_par"][c * P:c * P + n, :]).then_inc(loaded, 16)
                sp.dma_start(hf[0:n, :, c, :],
                             d["h_param"][:, c * P:c * P + n, 0:L].rearrange("o p l -> p o l")).then_inc(loaded, 16)
            txt = d["txt"].rearrange("(j i) t d -> i t j d", i=2)
            sp.dma_start(k.h[IMG:P, :, 0, :], txt[0, 0:IMG]).then_inc(k.setup_done, 16)
            sp.dma_start(k.h[0:IMG, :, 1, :], txt[0, IMG:TXT]).then_inc(k.setup_done, 16)
            sp.dma_start(k.h[:, :, 2, :], txt[1]).then_inc(k.setup_done, 16)
            sp.wait_ge(k.setup_done, 64)

        @block.gpsimd
        def _(pool):
            nc.gpsimd.memset(hz[:, :, :, 0:HALF], 0.0).then_inc(zeroed, 1)
            pool.wait_ge(zeroed, 1)
            nc.gpsimd.memset(k.nought[:, :], 0.0).then_inc(zeroed, 1)

        @block.scalar
        def _(act):
            act.wait_ge(loaded, 80)
            act.wait_ge(chain_s, 1)
            for c, n in enumerate(parts):
                nc.scalar.activation(e[0:n, c, :], tl[0:n, :], ACT.Exp, scale=par[0:n, c, 0:1]).then_inc(e_done, 1)

        @block.tensor
        def _(pe):
            pe.wait_ge(chain_s, 1 + 4 + 4)
            for o in range(2):
                for c, n in enumerate(parts):
                    nc.tensor.matmul(k.bank[0][:, o * L:o * L + L], k.ones[0:n, :], ab[0:n, o, c, :],
                                     start=(c == 0), stop=(c == 1)).then_inc(sums, 1)

        @block.vector
        def _(dve):
            ch = Chain(dve, chain_s)
            ch.n = 0
            nc.vector.memset(k.eps[:, :], LN_EPS)
            nc.vector.memset(k.xT1[D1:D1 + 1, :], 1.0)
            ch.did(nc.vector.memset(k.ones[:, :], 1.0))
            dve.wait_ge(loaded, 80)
            dve.wait_ge(e_done, 2)
            for o in range(2):
                for c, n in enumerate(parts):
                    ch.did(nc.vector.scalar_tensor_tensor(hf[0:n, o, c, :], e[0:n, c, :], par[0:n, c, 1:2],
                                                          hf[0:n, o, c, :], ALU.add, ALU.mult))
            ch.sync()
            for o in range(2):
                for c, n in enumerate(parts):
                    ch.did(nc.vector.scalar_tensor_tensor(ab[0:n, o, c, :], hf[0:n, o, c, :], -1.0,
                                                          hf[0:n, o, c, :], ALU.mult, ALU.max))
            dve.wait_ge(sums, 4)
            for o in range(2):
                ch.did(nc.vector.reciprocal(rec[:, o, :], k.bank[0][:, o * L:o * L + L]))
            ch.sync()
            for o in range(2):
                for c, n in enumerate(parts):
                    ch.did(nc.vector.tensor_tensor(hf[0:n, o, c, :], hf[0:n, o, c, :], rec[0:n, o, :], ALU.mult))



def tokenizer(k, d):
    nc = k.nc
    S = {n: k.sem("tk_" + n) for n in (
        "consts", "stem", "bn", "leaky", "off", "tr", "pxy", "htcopy", "scr", "hx", "hy",
        "weighted", "sampcopy", "dcn", "bn2", "prep", "act_chain", "dve_chain", "sqrt", "samp_mm")}
    S["patch"], S["bc"] = ([k.sem(f"tk_{n}{u}") for u in range(2)] for n in ("patch", "bc"))
    with ExitStack() as ctx, nc.Block() as block:
        stem_w = k.sb(ctx, "tk_stem_w", [48, CS])
        off_w = k.sb(ctx, "tk_off_w", [CS, TAPS, OFFC])
        dcn_w = k.sb(ctx, "tk_dcn_w", [CS, TAPS, D])
        v96 = k.sb(ctx, "tk_v96", [CS, 5])
        v192 = k.sb(ctx, "tk_v192", [P, 5, D])
        offb = k.sb(ctx, "tk_offb", [OFFC, 1])
        grid = k.sb(ctx, "tk_grid", [OFFC, 64])
        xy = k.sb(ctx, "tk_xy", [P, 1 + YCH])
        pat = k.sb(ctx, "tk_pat", [48, 2, HW])
        pre = k.sb(ctx, "tk_pre", [CS, HW])
        h1 = k.sb(ctx, "tk_h1", [CS, HW])
        pxy = k.sb(ctx, "tk_pxy", [OFFC, 2, 64])
        pos = k.sb(ctx, "tk_pos", [P, 2, TAPS, 2, 64])
        hT = k.sb(ctx, "tk_hT", [P, 2, YCH, CS])
        hx = k.sb(ctx, "tk_hx", [P, HW])
        ab = k.sb(ctx, "tk_ab", [P, 2, HW])
        hy = k.sb(ctx, "tk_hy", [P, 2, HW])
        wt = k.sb(ctx, "tk_wt", [P, 3, HW])
        samp = k.sb(ctx, "tk_samp", [CS, TAPS, 2, 64])
        inv1, sh1 = k.sb(ctx, "tk_inv1", [CS, 1]), k.sb(ctx, "tk_sh1", [CS, 1])
        inv2, sh2 = k.sb(ctx, "tk_inv2", [P, D]), k.sb(ctx, "tk_sh2", [P, D])
        tmp2 = k.sb(ctx, "tk_tmp2", [P, D])
        ps_stem = [k.bank[0], k.bank[1]]
        ps_t = [k.bank[2], k.bank[3]]
        ps_off, ps_dcn = k.bank[4], k.bank[5]
        ps_s = [k.bank[6], k.bank[7]]
        scr = d["positions"]

        @block.sync
        def _(sp):
            for t, name in ((stem_w, "stem_w"), (off_w, "off_w"), (v96, "v96"), (offb, "off_b"), (grid, "grid"),
                            (xy, "xy"), (dcn_w, "dcn_w")):
                flat = t[:] if len(t.shape) == 2 else t[:].rearrange("p a b -> p (a b)")
                sp.dma_start(flat, d[name]).then_inc(S["consts"], 16)
            sp.dma_start(v192[:].rearrange("p a b -> p (a b)"), bcast_rows(d["v192"], 5 * D)).then_inc(S["consts"], 16)

            def load(b, u):
                sp.dma_start(pat[:, u, :], d["patches"][b]).then_inc(S["patch"][u], 16)

            def spread(b, u):
                sp.wait_ge(S["pxy"], b + 1)
                sp.dma_start(scr[b], pxy[:, u, :]).then_inc(S["scr"], 16)
                sp.wait_ge(S["scr"], b * 16 + 16)
                sp.dma_start(pos[:, u, :, :, :].rearrange("p k a s -> p (k a s)"),
                             bass.AP(scr.tensor, b * (OFFC * 64), [[0, P], [1, OFFC * 64]])).then_inc(S["bc"][u], 16)

            rows = d["queue"].rearrange("(n p r) d -> n p (r d)", p=P, r=8)
            ROWS = rows.shape[0] // B

            def clear(b):
                for n in range(ROWS):
                    sp.dma_start(rows[b * ROWS + n], k.nought[:, :]).then_inc(k.zeroed, 16)

            load(0, 0)
            load(1, 1)
            with sp.Fori(0, PAIRS - 1) as j:
                for u in range(2):
                    spread(j * 2 + u, u)
                    load(j * 2 + (2 + u), u)
                    clear(j * 2 + u)
            for u in range(2):
                spread(2 * PAIRS - 2 + u, u)
                clear(2 * PAIRS - 2 + u)

        @block.tensor
        def _(pe):
            def stem(q, u):
                b = q * 2 + u
                pe.wait_ge(S["patch"][u], q * 16 + 16)
                wait(pe, S["bn"], b)
                for n in range(2):
                    mm = nc.tensor.matmul(ps_stem[n][0:CS, :], stem_w[:, :], pat[:, u, n * 512:n * 512 + 512],
                                          start=True, stop=True)
                mm.then_inc(S["stem"], 1)

            def offsets(b, u):
                pe.wait_ge(S["leaky"], b + 1)
                wait(pe, S["pxy"], b)
                taps = h1[:, :].rearrange("c (a e b f) -> c e f a b", a=8, e=4, b=8)
                for t in range(TAPS):
                    mm = nc.tensor.matmul(ps_off[0:OFFC, 0:64], off_w[:, t, :], taps[:, t // 4, t % 4],
                                          start=(t == 0), stop=(t == TAPS - 1))
                mm.then_inc(S["off"], 1)
                wait(pe, S["htcopy"], b)
                for i in range(YCH):
                    mm = nc.tensor.transpose(ps_t[i // 4][:, i % 4 * CS:i % 4 * CS + CS], h1[:, i * P:i * P + P],
                                             k.ident[0:CS, 0:CS])
                mm.then_inc(S["tr"], 1)

            def sample(b, u):
                pe.wait_ge(S["htcopy"], b + 1)
                wait(pe, S["sampcopy"], b)
                for i in range(YCH):
                    pe.wait_ge(S["weighted"], b * YCH + (i + 1))
                    for n in range(2):
                        mm = nc.tensor.matmul(ps_s[n][0:CS, :], hT[:, u, i, :], wt[:, i % 2, n * 512:n * 512 + 512],
                                              start=(i == 0), stop=(i == YCH - 1))
                    mm.then_inc(S["samp_mm"], 1)

            def deform(j):
                pe.wait_ge(S["sampcopy"], j * 2 + 2)
                wait(pe, S["bn2"], j)
                for t in range(TAPS):
                    mm = nc.tensor.matmul(ps_dcn[:, 0:D], samp[:, t, :, :].rearrange("c u s -> c (u s)"), dcn_w[:, t, :],
                                          start=(t == 0), stop=(t == TAPS - 1))
                mm.then_inc(S["dcn"], 1)

            pe.wait_ge(S["consts"], 128)
            stem(0, 0)
            offsets(0, 0)

            def pair(j, last):
                stem(j, 1)
                offsets(j * 2 + 1, 1)
                sample(j * 2, 0)
                if not last:
                    stem(j + 1, 0)
                    offsets(j * 2 + 2, 0)
                sample(j * 2 + 1, 1)
                deform(j)

            pair(0, False)
            with pe.Fori(1, PAIRS - 1) as j:
                pair(j, False)
            pair(PAIRS - 1, True)

        @block.scalar
        def _(act):
            ch = Chain(act, S["act_chain"])
            act.wait_ge(S["consts"], 128)
            act.wait_ge(S["prep"], 2)
            ch.did(nc.scalar.activation(inv1[:, :], v96[:, 4:5], ACT.Sqrt, bias=k.eps[0:CS, :]))
            nc.scalar.activation(inv2[:, :], v192[:, 4, :], ACT.Sqrt, bias=k.eps[:, :]).then_inc(S["sqrt"], 1)
            act.wait_ge(S["prep"], 6)

            def norm(b, u):
                act.wait_ge(S["stem"], b + 1)
                wait(act, S["leaky"], b)
                for n in range(2):
                    a = nc.scalar.activation(pre[:, n * 512:n * 512 + 512], ps_stem[n][0:CS, :], ACT.Identity,
                                             bias=sh1[:, :], scale=inv1[:, :])
                a.then_inc(S["bn"], 1)

            def hats(q, u):
                b = q * 2 + u
                act.wait_ge(S["bc"][u], q * 16 + 16)
                wait(act, S["weighted"], b * YCH)
                ch.link(nc.scalar.activation(hx[:, :], pos[:, u, :, 1, :], ACT.Abs, bias=xy[:, 0:1]))
                ch.did(nc.scalar.activation(hx[:, :], hx[:, :], ACT.Relu, bias=1.0, scale=-1.0))
                for i in range(YCH):
                    ch.link(nc.scalar.activation(ab[:, i % 2, :], pos[:, u, :, 0, :], ACT.Abs,
                                                 bias=xy[:, 1 + i:2 + i]))
                    if i >= 2:
                        act.wait_ge(S["weighted"], b * YCH + (i - 1))
                    nc.scalar.activation(hy[:, i % 2, :], ab[:, i % 2, :], ACT.Relu, bias=1.0,
                                         scale=-1.0).then_inc(S["hy"], 1)

            per = 2 + YCH
            norm(0, 0)

            def pair(j, last):
                norm(j * 2 + 1, 1)
                hats(j, 0)
                if not last:
                    norm(j * 2 + 2, 0)
                hats(j, 1)

            pair(0, False)
            with act.Fori(1, PAIRS - 1) as j:
                ch.enter(j - 1, 2 * per)
                pair(j, False)
                ch.leave(PAIRS - 2)
            pair(PAIRS - 1, True)

        @block.vector
        def _(dve):
            ch = Chain(dve, S["dve_chain"])
            dve.wait_ge(S["consts"], 128)
            nc.vector.memset(tmp2[:, :], 0.0).then_inc(S["prep"], 2)
            dve.wait_ge(S["sqrt"], 1)
            for inv, sh, v, in ((inv1[:, :], sh1[:, :], [v96[:, i:i + 1] for i in range(5)]),
                                (inv2[:, :], sh2[:, :], [v192[:, i, :] for i in range(5)])):
                ch.link(nc.vector.reciprocal(inv, inv))
                ch.link(nc.vector.tensor_tensor(inv, inv, v[1], ALU.mult))
                ch.link(nc.vector.tensor_tensor(sh, v[0], v[3], ALU.subtract))
                ch.link(nc.vector.tensor_tensor(sh, sh, inv, ALU.mult))
                last = nc.vector.tensor_tensor(sh, sh, v[2], ALU.add)
                last.then_inc(S["prep"], 2)
            dve.wait_ge(S["prep"], 6)

            def leaky(b, u):
                dve.wait_ge(S["bn"], b + 1)
                nc.vector.scalar_tensor_tensor(h1[:, :], pre[:, :], 0.01, pre[:, :], ALU.mult,
                                               ALU.max).then_inc(S["leaky"], 1)

            def where(b, u):
                dve.wait_ge(S["off"], b + 1)
                nc.vector.scalar_tensor_tensor(pxy[:, u, :], ps_off[0:OFFC, 0:64], offb[:, 0:1], grid[:, :],
                                               ALU.add, ALU.add).then_inc(S["pxy"], 1)
                dve.wait_ge(S["tr"], b + 1)
                for n in range(2):
                    c = nc.vector.tensor_copy(hT[:, u, 4 * n:4 * n + 4, :].rearrange("p a c -> p (a c)"),
                                              ps_t[n][:, 0:4 * CS])
                c.then_inc(S["htcopy"], 1)

            def weights(b, u):
                for i in range(YCH):
                    dve.wait_ge(S["hy"], b * YCH + (i + 1))
                    if i >= 2:
                        dve.wait_ge(S["samp_mm"], b * YCH + (i - 1))
                    else:
                        wait(dve, S["samp_mm"], b * YCH + (i - 1) if isinstance(b, int) else b * YCH + (i - 1))
                    nc.vector.tensor_tensor(wt[:, i % 2, :], hy[:, i % 2, :], hx[:, :],
                                            ALU.mult).then_inc(S["weighted"], 1)
                dve.wait_ge(S["samp_mm"], b * YCH + YCH)
                for n in range(2):
                    c = nc.vector.tensor_copy(samp[:, 8 * n:8 * n + 8, u, :],
                                              ps_s[n][0:CS, :].rearrange("c (t s) -> c t s", t=8))
                c.then_inc(S["sampcopy"], 1)

            def norm2(j):
                dve.wait_ge(S["dcn"], j + 1)
                ch.link(nc.vector.tensor_tensor(tmp2[:, :], ps_dcn[:, 0:D], inv2[:, :], ALU.mult))
                ch.link(nc.vector.tensor_tensor(tmp2[:, :], tmp2[:, :], sh2[:, :], ALU.add))
                for t, lo in ((0, 0), (1, IMG)):
                    o = nc.vector.scalar_tensor_tensor(k.h[lo:lo + IMG, j, t, :], tmp2[lo:lo + IMG, :], 0.01,
                                                       tmp2[lo:lo + IMG, :], ALU.mult, ALU.max)
                o.then_inc(S["bn2"], 1)

            leaky(0, 0)
            where(0, 0)

            def pair(j, last):
                leaky(j * 2 + 1, 1)
                where(j * 2 + 1, 1)
                weights(j * 2, 0)
                if not last:
                    leaky(j * 2 + 2, 0)
                    where(j * 2 + 2, 0)
                weights(j * 2 + 1, 1)
                norm2(j)

            pair(0, False)
            with dve.Fori(1, PAIRS - 1) as j:
                ch.enter(j - 1, 2)
                pair(j, False)
                ch.leave(PAIRS - 2)
            pair(PAIRS - 1, True)



def norm(k, name, d, src, affine=None, dst=None):
    nc = k.nc
    S = {n: k.sem(f"{name}_{n}") for n in ("vars", "rstd", "inv", "normed", "turned", "x0", "x1", "chain", "rows")}
    tiles = PAIRS * 3
    with ExitStack() as ctx, nc.Block() as block:
        st = k.sb(ctx, name + "_st", [P, PAIRS, 3, 6])
        mv = k.sb(ctx, name + "_mv", [P, 3, PAIRS, 3])
        rs = k.sb(ctx, name + "_rs", [P, PAIRS, 3])
        gb = k.sb(ctx, name + "_gb", [P, 2, D]) if affine else None
        xn = dst if dst is not None else k.xn

        if affine:
            @block.sync
            def _(sp):
                sp.dma_start(gb[:, :, :].rearrange("p a d -> p (a d)"),
                             bcast_rows(d[affine], 2 * D)).then_inc(S["rows"], 16)
                sp.wait_ge(S["rows"], 16)

        @block.scalar
        def _(act):
            act.wait_ge(S["vars"], 1)
            nc.scalar.activation(rs[:, :, :], mv[:, 1], ACT.Sqrt, bias=k.eps[:, :]).then_inc(S["rstd"], 1)
            if dst is None:
                def copy(j, u):
                    act.wait_ge(S["turned"], j + 1)
                    nc.scalar.activation(k.xT0[:, bass.ds(j * PC, PC)], k.bank[2 * u][:, 0:PC],
                                         ACT.Copy).then_inc(S["x0"], 1)

                with act.Fori(0, PAIRS // 2) as q:
                    copy(q * 2, 0)
                    copy(q * 2 + 1, 1)

        @block.tensor
        def _(pe):
            if dst is None:
                def turn(j, u, first):
                    pe.wait_ge(S["normed"], j + 1)
                    if not first:
                        pe.wait_ge(S["x0"], j - 1)
                        pe.wait_ge(S["x1"], j - 1)
                    for t in range(3):
                        nc.tensor.transpose(k.bank[2 * u][:, t * P:t * P + P], xn[:, j, t, 0:P], k.ident[:, :])
                        mm = nc.tensor.transpose(k.bank[2 * u + 1][0:D1, t * P:t * P + P], xn[:, j, t, P:D],
                                                 k.ident[:, :])
                    mm.then_inc(S["turned"], 1)

                for j in range(PAIRS):
                    turn(j, j % 2, j < 2)

        @block.vector
        def _(dve):
            ch = Chain(dve, S["chain"])
            with dve.Fori(0, PAIRS) as j:
                ch.enter(j, 3)
                for t in range(3):
                    ch.did(nc.vector.bn_stats(st[:, j, t, :], src[:, j, t, :]))
                ch.leave(PAIRS)
            ch.sync()
            half = float(D // 2)
            ch.did(nc.vector.tensor_tensor(mv[:, 0], st[:, :, :, 1], st[:, :, :, 4], ALU.add))
            ch.did(nc.vector.tensor_tensor(mv[:, 1], st[:, :, :, 1], st[:, :, :, 4], ALU.subtract))
            ch.did(nc.vector.tensor_tensor(mv[:, 2], st[:, :, :, 2], st[:, :, :, 5], ALU.add))
            ch.sync()
            ch.did(nc.vector.tensor_scalar(mv[:, 0], mv[:, 0], 0.5, None, ALU.mult))
            ch.link(nc.vector.scalar_tensor_tensor(mv[:, 1], mv[:, 1], 0.25, mv[:, 1], ALU.mult, ALU.mult))
            nc.vector.scalar_tensor_tensor(mv[:, 1], mv[:, 2], 0.5 / half, mv[:, 1], ALU.mult,
                                           ALU.add).then_inc(S["vars"], 1)
            dve.wait_ge(S["rstd"], 1)
            if affine:
                dve.wait_ge(S["rows"], 16)
            nc.vector.reciprocal(rs[:, :, :], rs[:, :, :]).then_inc(S["inv"], 1)
            dve.wait_ge(S["inv"], 1)

            def scale(j):
                for t in range(3):
                    ins = nc.vector.tensor_scalar(xn[:, j, t, :], src[:, j, t, :], mv[:, 0, j, t:t + 1], rs[:, j, t:t + 1],
                                                  ALU.subtract, ALU.mult)
                    if affine:
                        ch.did(ins)
                if affine:
                    ch.sync()
                    for t in range(3):
                        ch.did(nc.vector.tensor_tensor(xn[:, j, t, :], xn[:, j, t, :], gb[:, 0, :], ALU.mult))
                    ch.sync()
                    for t in range(3):
                        ins = nc.vector.tensor_tensor(xn[:, j, t, :], xn[:, j, t, :], gb[:, 1, :], ALU.add)
                ins.then_inc(S["normed"], 1)

            def copy(j, u):
                dve.wait_ge(S["turned"], j + 1)
                nc.vector.tensor_copy(k.xT1[0:D1, bass.ds(j * PC, PC)],
                                      k.bank[2 * u + 1][0:D1, 0:PC]).then_inc(S["x1"], 1)

            if dst is not None:
                with dve.Fori(0, PAIRS) as j:
                    ch.enter(j, 6)
                    scale(j)
                    ch.leave(PAIRS)
            else:
                with dve.Fori(0, PAIRS // 2) as q:
                    ch.enter(q, 12 if affine else 0)
                    scale(q * 2)
                    scale(q * 2 + 1)
                    copy(q * 2, 0)
                    copy(q * 2 + 1, 1)
                    ch.leave(PAIRS // 2)



def retention(k, d):
    nc = k.nc
    S = {n: k.sem("re_" + n) for n in ("loaded", "proj", "qk", "v", "scores", "decayed", "out", "added")}
    with ExitStack() as ctx, nc.Block() as block:
        w0, w1 = k.sb(ctx, "re_w0", [P, 3 * D]), k.sb(ctx, "re_w1", [D1 + 1, 3 * D])
        decay = k.sb(ctx, "re_decay", [P, 2, PC])
        qk = k.sb(ctx, "re_qk", [P, 4, PC])
        v = k.sb(ctx, "re_v", [P, 2, 3, D])
        pt = k.sb(ctx, "re_pt", [P, 2, PC])
        Q0, Q1, K0, K1, V0, V1, R0, R1 = k.bank

        @block.sync
        def _(sp):
            sp.dma_start(w0[:, :], d["qkv"][0:P, :]).then_inc(S["loaded"], 16)
            sp.dma_start(w1[:, :], d["qkv"][P:D + 1, :]).then_inc(S["loaded"], 16)
            sp.dma_start(decay[:, :, :].rearrange("p a b -> p (a b)"), d["decay"]).then_inc(S["loaded"], 16)
            for o in range(2):
                for c, n in enumerate((P, D1)):
                    sp.dma_start(d["filters"][o, c * P:c * P + n, :, :],
                                 k.hz[0:n, o, c, :].unsqueeze(1).broadcast_to([n, FC, FPITCH])
                                 ).then_inc(k.filters_stored, 16)
            sp.wait_ge(S["loaded"], 48)

        @block.tensor
        def _(pe):
            def project(j):
                c = j * PC
                x0, x1 = k.xT0[:, bass.ds(c, PC)], k.xT1[0:D1 + 1, bass.ds(c, PC)]
                for n, (ps, at) in enumerate(((Q0, 0), (Q1, P), (K0, D), (K1, D + P))):
                    m = P if n % 2 == 0 else D1
                    nc.tensor.matmul(ps[0:m, 0:PC], w0[:, at:at + m], x0, start=True, stop=False)
                    nc.tensor.matmul(ps[0:m, 0:PC], w1[:, at:at + m], x1, start=False, stop=True)
                for t in range(3):
                    ps = V0[:, t * D:t * D + D] if t < 2 else V1[:, 0:D]
                    nc.tensor.matmul(ps, k.xT0[:, bass.ds(c + t * P, P)], w0[:, 2 * D:], start=True, stop=False)
                    mm = nc.tensor.matmul(ps, k.xT1[0:D1 + 1, bass.ds(c + t * P, P)], w1[:, 2 * D:],
                                          start=False, stop=True)
                mm.then_inc(S["proj"], 1)

            def scores(j):
                pe.wait_ge(S["qk"], j + 1)
                wait(pe, S["added"], j)
                for e, keys, m, lo, at, q0, q1 in ((0, 0, P, 0, 0, 0, L), (0, P, 64, 0, L, P, L),
                                                   (1, L, 64, 64, L, L, PC), (1, L + 64, P, 0, 0, L + 64, PC)):
                    ps = (R0, R1)[e][lo:lo + m, at + q0 - e * L:at + q1 - e * L]
                    for n, r in enumerate((P, D1)):
                        mm = nc.tensor.matmul(ps, qk[0:r, 2 + n, keys:keys + m], qk[0:r, n, q0:q1],
                                              start=(n == 0), stop=(n == 1))
                mm.then_inc(S["scores"], 1)

            def mix(j, u):
                pe.wait_ge(S["decayed"], j + 1)
                big0, big2 = pt[:, 0, 0:L], pt[:, 1, 0:L]
                small0, small2 = pt[0:64, 0, L:PC], pt[64:P, 1, L:PC]
                nc.tensor.matmul(R0[:, 0:D], big0[:, 0:P], v[:, u, 0, :], start=True, stop=True)
                nc.tensor.matmul(R1[:, 0:D], big2[:, 64:L], v[:, u, 2, :], start=True, stop=False)
                nc.tensor.matmul(R1[:, 0:D], small2[:, 64:L], v[64:P, u, 1, :], start=False, stop=True)
                nc.tensor.matmul(R0[0:64, D:2 * D], big0[:, P:L], v[:, u, 0, :], start=True, stop=False)
                nc.tensor.matmul(R0[0:64, D:2 * D], small0[:, P:L], v[0:64, u, 1, :], start=False, stop=True)
                nc.tensor.matmul(R0[64:P, D:2 * D], small2[:, 0:64], v[64:P, u, 1, :], start=True,
                                 stop=True).then_inc(S["out"], 1)

            def step(j, u, last=False):
                scores(j)
                if not last:
                    pe.wait_ge(S["v"], j + 1)
                    project(j + 1)
                mix(j, u)

            pe.wait_ge(S["loaded"], 48)
            project(0)
            for j in range(PAIRS):
                step(j, j % 2, j == PAIRS - 1)

        @block.scalar
        def _(act):
            with act.Fori(0, PAIRS) as j:
                act.wait_ge(S["proj"], j + 1)
                for n, ps in enumerate((Q0, Q1, K0, K1)):
                    m = P if n % 2 == 0 else D1
                    a = nc.scalar.activation(qk[0:m, n, :], ps[0:m, 0:PC], ACT.Copy)
                a.then_inc(S["qk"], 1)

        @block.vector
        def _(dve):
            def values(j, u):
                dve.wait_ge(S["proj"], j + 1)
                nc.vector.tensor_copy(v[:, u, 0:2, :].rearrange("p a d -> p (a d)"), V0[:, 0:2 * D])
                nc.vector.tensor_copy(v[:, u, 2, :], V1[:, 0:D]).then_inc(S["v"], 1)

            def step(j, u, last=False):
                dve.wait_ge(S["scores"], j + 1)
                for e, ps, lo, hi, c0, c1 in ((0, R0, 0, P, 0, L), (0, R0, 0, 64, L + P, PC),
                                              (1, R1, 0, P, 64, L), (1, R1, 64, P, L, PC)):
                    o = nc.vector.tensor_tensor(pt[lo:hi, e, c0:c1], ps[lo:hi, c0:c1], decay[lo:hi, e, c0:c1], ALU.mult)
                o.then_inc(S["decayed"], 1)
                if not last:
                    values(j + 1, 1 - u)
                dve.wait_ge(S["out"], j + 1)
                nc.vector.tensor_tensor(k.h[:, j, 0:2, :].rearrange("p a d -> p (a d)"), R0[:, 0:2 * D],
                                        k.h[:, j, 0:2, :].rearrange("p a d -> p (a d)"), ALU.add)
                nc.vector.tensor_tensor(k.h[:, j, 2, :], R1[:, 0:D], k.h[:, j, 2, :], ALU.add).then_inc(S["added"], 1)

            values(0, 0)
            step(0, 0)
            step(1, 1)
            with dve.Fori(1, PAIRS // 2 - 1) as q:
                step(q * 2, 0)
                step(q * 2 + 1, 1)
            step(PAIRS - 2, 0)
            step(PAIRS - 1, 1, True)



def norm_a(k, d):
    norm(k, "na", d, k.h)


def norm_b(k, d):
    norm(k, "nb", d, k.h)



def choose(nc, ch, x, rank, c, chosen, kept):
    n = x.shape[-1]
    for i in range(n):
        ch.did(nc.vector.memset(rank[:, :, i:i + 1], float(n - 1 - i)))
    ch.sync()
    for step in range(1, n):
        m = n - step
        ch.link(nc.vector.tensor_tensor(c[:, :, 0:m], x[:, :, 0:m], x[:, :, step:n], ALU.is_ge))
        ch.link(nc.vector.tensor_tensor(rank[:, :, step:n], rank[:, :, step:n], c[:, :, 0:m], ALU.add))
        ch.link(nc.vector.tensor_tensor(rank[:, :, 0:m], rank[:, :, 0:m], c[:, :, 0:m], ALU.subtract))
    ch.link(nc.vector.tensor_scalar(chosen, rank, kept - 0.5, None, ALU.is_lt))


def over(ap, n):
    return ap.unsqueeze(2).broadcast_to([ap.shape[0], ap.shape[1], n])


def gates(k, d, name, groups, experts, combine, weight, chosen=None):
    nc = k.nc
    tiles = PAIRS * 3
    nx = groups * experts
    cols = nx + (groups if groups > 1 else 0)
    S = {n: k.sem(f"{name}_{n}") for n in ("loaded", "logits", "shift", "exp", "chain")}
    with ExitStack() as ctx, nc.Block() as block:
        w0, w1 = k.sb(ctx, name + "_w0", [P, cols]), k.sb(ctx, name + "_w1", [D1 + 1, cols])
        lg = k.sb(ctx, name + "_lg", [P, tiles, cols])
        n_all = tiles * groups
        xs = [(k.sb(ctx, name + "_xe", [P, n_all, experts]), n_all, experts, 4 if groups > 1 else 2)]
        if groups > 1:
            xs.append((k.sb(ctx, name + "_xg", [P, tiles, groups]), tiles, groups, 2))
        most = [k.sb(ctx, f"{name}_most{i}", [P, n]) for i, (_, n, _, _) in enumerate(xs)]
        rank = k.sb(ctx, name + "_rank", [P, n_all, experts])
        c = k.sb(ctx, name + "_c", [P, n_all, experts])
        sel = [k.sb(ctx, f"{name}_sel{i}", [P, n, m]) for i, (_, n, m, _) in enumerate(xs)]
        tpb = 12

        @block.sync
        def _(sp):
            sp.dma_start(w0[:, :], d[weight][0:P, :]).then_inc(S["loaded"], 16)
            sp.dma_start(w1[:, :], d[weight][P:D + 1, :]).then_inc(S["loaded"], 16)
            sp.wait_ge(S["loaded"], 32)

        @block.tensor
        def _(pe):
            pe.wait_ge(S["loaded"], 32)
            for t in range(tiles):
                ps = k.bank[t // tpb][:, t % tpb * cols:t % tpb * cols + cols]
                nc.tensor.matmul(ps, k.xT0[:, t * P:t * P + P], w0[:, :], start=True, stop=False)
                mm = nc.tensor.matmul(ps, k.xT1[0:D1 + 1, t * P:t * P + P], w1[:, :], start=False, stop=True)
            mm.then_inc(S["logits"], 1)

        @block.scalar
        def _(act):
            act.wait_ge(S["shift"], 1)
            for x, _, _, _ in xs:
                a = nc.scalar.activation(x[:, :, :], x[:, :, :], ACT.Exp)
            a.then_inc(S["exp"], 1)

        @block.vector
        def _(dve):
            ch = Chain(dve, S["chain"])
            dve.wait_ge(S["logits"], 1)
            for i in range(tiles // tpb):
                ch.did(nc.vector.tensor_copy(lg[:, i * tpb:i * tpb + tpb, :].rearrange("p a c -> p (a c)"),
                                             k.bank[i][:, 0:tpb * cols]))
            ch.sync()
            if groups > 1:
                ch.did(nc.vector.tensor_copy(xs[1][0][:, :, :], lg[:, :, 0:groups]))
                ch.link(nc.vector.tensor_copy(xs[0][0][:, :, :].rearrange("p (t g) e -> p t (g e)", g=groups),
                                              lg[:, :, groups:cols]))
            else:
                ch.link(nc.vector.tensor_copy(xs[0][0][:, :, :], lg[:, :, :]))
            for i, (x, n, m, kept) in enumerate(xs):
                choose(nc, ch, x[:, :, :], rank[:, 0:n, 0:m], c[:, 0:n, 0:m], sel[i][:, :, :], kept)
                ch.link(nc.vector.tensor_reduce(most[i][:, :], x[:, :, :], AX.X, ALU.max))
                s = nc.vector.tensor_tensor(x[:, :, :], x[:, :, :], over(most[i][:, :], m), ALU.subtract)
            s.then_inc(S["shift"], 1)
            if chosen is not None:
                ch.did(nc.vector.tensor_tensor(
                    chosen[:, :, :].rearrange("p t (g e) -> p (t g) e", g=groups), sel[0][:, :, :],
                    over(sel[1][:, :, :].rearrange("p t g -> p (t g)"), experts), ALU.mult))
                ch.sync()
            dve.wait_ge(S["exp"], 1)
            for i, (x, n, m, _) in enumerate(xs):
                if groups > 1:
                    ch.link(nc.vector.tensor_tensor(x[:, :, :], x[:, :, :], sel[i][:, :, :], ALU.mult))
                ch.link(nc.vector.tensor_reduce(most[i][:, :], x[:, :, :], AX.X, ALU.add))
                ch.link(nc.vector.reciprocal(most[i][:, :], most[i][:, :]))
                ch.link(nc.vector.tensor_tensor(x[:, :, :], x[:, :, :], over(most[i][:, :], m), ALU.mult))
                if groups > 1:
                    ch.link(nc.vector.tensor_scalar(sel[i][:, :, :], x[:, :, :], 1e-6, None, ALU.is_ge))
                    ch.link(nc.vector.tensor_tensor(x[:, :, :], x[:, :, :], sel[i][:, :, :], ALU.mult))
            if groups > 1:
                ch.link(nc.vector.tensor_tensor(
                    combine[:, :, :].rearrange("p t (g e) -> p (t g) e", g=groups), xs[0][0][:, :, :],
                    over(xs[1][0][:, :, :].rearrange("p t g -> p (t g)"), experts), ALU.mult))
            else:
                ch.link(nc.vector.tensor_tensor(combine[:, :, :], xs[0][0][:, :, :], sel[0][:, :, :], ALU.mult))



def bias(k, d, name, nx, combine, acc, b2n):
    nc = k.nc
    S = {n: k.sem(f"{name}_{n}") for n in ("b2", "ct", "ctcopy", "bias", "added")}
    with ExitStack() as ctx, nc.Block() as block:
        b2 = k.sb(ctx, name + "_b2", [nx, D])
        cT = k.sb(ctx, name + "_cT", [nx, 2, 3 * P])

        @block.sync
        def _(sp):
            sp.dma_start(b2[:, :], d[b2n]).then_inc(S["b2"], 16)

        @block.tensor
        def _(pe):
            pe.wait_ge(S["b2"], 16)
            for j in range(PAIRS):
                u = j % 2
                if j >= 2:
                    pe.wait_ge(S["ctcopy"], j - 1)
                for t in range(3):
                    mm = nc.tensor.transpose(k.bank[6 + u][0:nx, t * P:t * P + P], combine[:, j * 3 + t, :],
                                             k.ident[:, :])
                mm.then_inc(S["ct"], 1)
                pe.wait_ge(S["ctcopy"], j + 1)
                if j:
                    pe.wait_ge(S["added"], j)
                for t in range(3):
                    mm = nc.tensor.matmul(k.bank[3 + t][:, 0:D], cT[:, u, t * P:t * P + P], b2[:, :],
                                          start=True, stop=True)
                mm.then_inc(S["bias"], 1)

        @block.vector
        def _(dve):
            for j in range(PAIRS):
                dve.wait_ge(S["ct"], j + 1)
                nc.vector.tensor_copy(cT[:, j % 2, :], k.bank[6 + j % 2][0:nx, 0:PC]).then_inc(S["ctcopy"], 1)
                dve.wait_ge(S["bias"], j + 1)
                for t in range(3):
                    a = nc.vector.tensor_tensor(acc[:, j, t, :], k.bank[3 + t][:, 0:D], acc[:, j, t, :], ALU.add)
                a.then_inc(S["added"], 1)



def experts(k, d, name, nx, func, combine, acc, w1n, w2n):
    nc = k.nc
    S = {n: k.sem(f"{name}_{n}") for n in ("up", "act", "down", "acc")}
    win = [k.sem(f"{name}_win{u}") for u in range(2)]
    tiles = PAIRS * 3
    UPC, ACC = 3, 24
    with ExitStack() as ctx, nc.Block() as block:
        wa = k.sb(ctx, name + "_wa", [P, 2, FF])
        wb = k.sb(ctx, name + "_wb", [D1 + 1, 2, FF])
        wc = k.sb(ctx, name + "_wc", [P, 2, MC, D])
        hT = k.sb(ctx, name + "_hT", [P, 2, MC, PC])

        @block.sync
        def _(sp):
            def load(e, u):
                w1, w2 = d[w1n], d[w2n]
                sp.dma_start(wa[:, u, :], w1[e, 0:P, :]).then_inc(win[u], 16)
                sp.dma_start(wb[:, u, :], w1[e, P:D + 1, :]).then_inc(win[u], 16)
                sp.dma_start(wc[:, u, :, :].rearrange("p m d -> p (m d)"), w2[e]).then_inc(win[u], 16)

            load(0, 0)
            load(1, 1)
            with sp.Fori(1, nx // 2) as q:
                for u in range(2):
                    sp.wait_ge(S["down"], q * 48 + 24 * (u - 1))
                    load(q * 2 + u, u)
            sp.wait_ge(win[0], nx // 2 * 48)
            sp.wait_ge(win[1], nx // 2 * 48)

        @block.tensor
        def _(pe):
            def up(t, pair, u):
                x0, x1 = k.xT0[:, bass.ds(pair * PC, PC)], k.xT1[0:D1 + 1, bass.ds(pair * PC, PC)]
                for m in range(MC):
                    ps = k.bank[m % 3][:, 0:PC]
                    pe.wait_ge(S["act"], t * MC + (UPC + m - 2))
                    nc.tensor.matmul(ps, wa[:, u, m * P:m * P + P], x0, start=True, stop=False)
                    nc.tensor.matmul(ps, wb[:, u, m * P:m * P + P], x1, start=False,
                                     stop=True).then_inc(S["up"], 1)

            def down(t, v, u):
                for i in range(3):
                    pe.wait_ge(S["acc"], t * 3 + (ACC + i - 2))
                    for m in range(MC):
                        if i == 0:
                            pe.wait_ge(S["act"], t * MC + (UPC + m + 1))
                        mm = nc.tensor.matmul(k.bank[3 + i][:, 0:D], hT[:, v, m, i * P:i * P + P], wc[:, u, m, :],
                                              start=(m == 0), stop=(m == MC - 1))
                    mm.then_inc(S["down"], 1)
                return mm

            with pe.Fori(0, nx // 2) as q:
                for u in range(2):
                    pe.wait_ge(win[u], q * 48 + 48)
                    at = q * 16 + u * PAIRS
                    up(at, 0, u)
                    with pe.Fori(0, PAIRS // 2 - 1) as i:
                        up(at + i * 2 + 1, i * 2 + 1, u)
                        down(at + i * 2, 0, u)
                        up(at + i * 2 + 2, i * 2 + 2, u)
                        down(at + i * 2 + 1, 1, u)
                    up(at + (PAIRS - 1), PAIRS - 1, u)
                    down(at + (PAIRS - 2), 0, u)
                    down(at + (PAIRS - 1), 1, u)

        @block.scalar
        def _(act):
            act.sem_inc(S["act"], UPC)
            with act.Fori(0, nx * PAIRS // 2) as i:
                for v in range(2):
                    for m in range(MC):
                        act.wait_ge(S["up"], i * (2 * MC) + (v * MC + m + 1))
                        nc.scalar.activation(hT[:, v, m, :], k.bank[m % 3][:, 0:PC], func).then_inc(S["act"], 1)

        @block.vector
        def _(dve):
            dve.sem_inc(S["acc"], ACC)
            with dve.Fori(0, nx) as e:
                with dve.Fori(0, PAIRS) as j:
                    for t in range(3):
                        at = e * (3 * PAIRS) + j * 3 + t
                        dve.wait_ge(S["down"], at + 1)
                        dve.wait_ge(S["acc"], at + 1)
                        nc.vector.scalar_tensor_tensor(acc[:, j, t, :], k.bank[3 + t][:, 0:D],
                                                       combine[:, j * 3 + t, bass.ds(e, 1)], acc[:, j, t, :],
                                                       ALU.mult, ALU.add).then_inc(S["acc"], 1)



UNIT = 2 * P
TILES = PAIRS * 3
KEPT = 8
UNITS = (TILES * P * KEPT - NX0) // UNIT + NX0
UNITS += UNITS % 2


def slots(k, d, chosen, combine, index, share, expert_of):
    nc = k.nc
    S = {n: k.sem("sl_" + n) for n in ("loaded", "sums", "chain")}
    NB = TILES * NX0 // 2
    with ExitStack() as ctx, nc.Block() as block:
        before = k.sb(ctx, "sl_before", [P, P])
        number = k.sb(ctx, "sl_number", [1, UNITS])
        key = k.sb(ctx, "sl_key", [P, TILES, NX0])
        tot = k.sb(ctx, "sl_tot", [P, TILES, NX0])
        run = k.sb(ctx, "sl_run", [P, TILES + 1, NX0])
        whole = k.sb(ctx, "sl_whole", [P, NX0], mybir.dt.int32)
        ends = k.sb(ctx, "sl_ends", [P, 2, NX0])
        top = k.sb(ctx, "sl_top", [P, TILES, KEPT])
        past = k.sb(ctx, "sl_past", [1, UNITS, NX0])
        exp = k.sb(ctx, "sl_exp", [1, UNITS])

        @block.sync
        def _(sp):
            sp.dma_start(before[:, :], d["before"]).then_inc(S["loaded"], 16)
            sp.dma_start(number[:, :], d["unit_numbers"]).then_inc(S["loaded"], 16)
            sp.wait_ge(S["loaded"], 32)

        @block.tensor
        def _(pe):
            pe.wait_ge(S["loaded"], 32)
            flat = chosen[:, :, :].rearrange("p t e -> p (t e)")
            for i in range(2):
                nc.tensor.matmul(k.bank[i][:, 0:NB], before[:, :], flat[:, i * NB:i * NB + NB], start=True, stop=True)
                mm = nc.tensor.matmul(k.bank[2 + i][:, 0:NB], k.ones[:, :], flat[:, i * NB:i * NB + NB],
                                      start=True, stop=True)
            mm.then_inc(S["sums"], 1)

        @block.vector
        def _(dve):
            ch = Chain(dve, S["chain"])
            ch.did(nc.vector.memset(run[:, 0, :], 0.0))
            dve.wait_ge(S["sums"], 1)
            for i in range(2):
                half = slice(i * TILES // 2, (i + 1) * TILES // 2)
                ch.did(nc.vector.tensor_copy(key[:, half, :].rearrange("p t e -> p (t e)"), k.bank[i][:, 0:NB]))
                ch.did(nc.vector.tensor_copy(tot[:, half, :].rearrange("p t e -> p (t e)"), k.bank[2 + i][:, 0:NB]))
            ch.sync()
            for t in range(TILES):
                ch.link(nc.vector.tensor_tensor(run[:, t + 1, :], run[:, t, :], tot[:, t, :], ALU.add))
            ch.link(nc.vector.tensor_scalar(ends[:, 0, :], run[:, TILES, :], float(UNIT - 1), None, ALU.add))
            ch.link(nc.vector.tensor_copy(whole[:, :], ends[:, 0, :]))
            ch.link(nc.vector.tensor_scalar(whole[:, :], whole[:, :], UNIT.bit_length() - 1, None,
                                            ALU.arith_shift_right))
            ch.link(nc.vector.tensor_copy(ends[:, 0, :], whole[:, :]))
            a, step = 0, 1
            while step < NX0:
                ch.did(nc.vector.tensor_copy(ends[:, 1 - a, 0:step], ends[:, a, 0:step]))
                ch.link(nc.vector.tensor_tensor(ends[:, 1 - a, step:NX0], ends[:, a, step:NX0],
                                                ends[:, a, 0:NX0 - step], ALU.add))
                a, step = 1 - a, 2 * step
            ch.did(nc.vector.tensor_tensor(key[:, :, :], key[:, :, :], run[:, 0:TILES, :], ALU.add))
            ch.link(nc.vector.tensor_scalar(ends[:, 1 - a, 1:NX0], ends[:, a, 0:NX0 - 1], float(UNIT), 1.0,
                                            ALU.mult, ALU.add))
            ch.link(nc.vector.memset(ends[:, 1 - a, 0:1], 1.0))
            ch.link(nc.vector.tensor_tensor(key[:, :, :], key[:, :, :],
                                            ends[:, 1 - a, :].unsqueeze(1).broadcast_to([P, TILES, NX0]), ALU.add))
            ch.link(nc.vector.tensor_tensor(key[:, :, :], key[:, :, :], chosen[:, :, :], ALU.mult))
            for t in range(TILES):
                ch.did(nc.vector.max(top[:, t, :], key[:, t, :]))
            ch.sync()
            ch.did(nc.vector.tensor_scalar(index[:, :, :], top[:, :, :], -1.0, None, ALU.add))
            ch.link(nc.vector.tensor_tensor(past[:, :, :], ends[0:1, a, :].unsqueeze(1).broadcast_to([1, UNITS, NX0]),
                                            over(number[:, :], NX0), ALU.is_le))
            ch.link(nc.vector.tensor_reduce(exp[:, :], past[:, :, :], AX.X, ALU.add))
            ch.link(nc.vector.tensor_scalar(expert_of[:, :], exp[:, :], float(NX0 - 1), None, ALU.min))
            for i in range(KEPT):
                ch.link(nc.vector.tensor_tensor(tot[:, :, :], key[:, :, :],
                                                top[:, :, i:i + 1].broadcast_to([P, TILES, NX0]), ALU.is_equal))
                ch.link(nc.vector.tensor_tensor(tot[:, :, :], tot[:, :, :], combine[:, :, :], ALU.mult))
                ch.link(nc.vector.tensor_reduce(share[:, :, i], tot[:, :, :], AX.X, ALU.add))


def routed(k, d, index, share, expert_of):
    nc = k.nc
    S = {n: k.sem("ro_" + n) for n in ("sent", "twice", "turned", "x_hi", "x", "up", "act", "h_hi", "h_lo", "down",
                                       "y", "added", "wa_hi", "wa_lo", "wb_hi", "wb_lo", "wc_hi", "wc_lo")}
    w1_in, w2_in, x_in, y_out = ([k.sem(f"ro_{n}{v}") for v in range(2)] for n in ("w1", "w2", "xin", "yout"))
    got = [k.sem(f"ro_got{i}") for i in range(KEPT)]
    queue, answers = d["queue"], d["answers"]
    UP_BANKS, TURN_BANK, DOWN_BANK = 4, 4, 6
    HP, WP = MC // 2, 3
    with ExitStack() as ctx, nc.Block() as block:
        wa = k.sb(ctx, "ro_wa", [P, 2, FF])
        wb = k.sb(ctx, "ro_wb", [P, 2, FF])
        wc = k.sb(ctx, "ro_wc", [P, 2, MC * D])
        b1 = k.sb(ctx, "ro_b1", [P, 2, MC])
        wa_hi, wa_lo = k.sb(ctx, "ro_wa_hi", [P, 2, FF], F32R), k.sb(ctx, "ro_wa_lo", [P, 2, FF], F32R)
        wb_hl = k.sb(ctx, "ro_wb_hl", [P, 2, FF], F32R)
        wc_hi, wc_lo = k.sb(ctx, "ro_wc_hi", [P, 2, MC * D], F32R), k.sb(ctx, "ro_wc_lo", [P, 2, MC * D], F32R)
        xq = k.sb(ctx, "ro_xq", [P, 2, 2, 2 * P])
        ga_hi, ga_lo = k.sb(ctx, "ro_ga_hi", [P, UNIT], F32R), k.sb(ctx, "ro_ga_lo", [P, UNIT], F32R)
        gb_hi, gb_lo = k.sb(ctx, "ro_gb_hi", [P, UNIT], F32R), k.sb(ctx, "ro_gb_lo", [D1, UNIT], F32R)
        hT = k.sb(ctx, "ro_hT", [P, MC, UNIT])
        h_hi, h_lo = k.sb(ctx, "ro_h_hi", [P, 2, MC, UNIT], F32R), k.sb(ctx, "ro_h_lo", [P, 2, MC, UNIT], F32R)
        y = k.sb(ctx, "ro_y", [P, 2, 2, D])
        back = k.sb(ctx, "ro_back", [P, KEPT, D])
        tile = k.h[:].rearrange("p j t d -> p (j t) d")
        xt = k.xn[:].rearrange("p j t d -> p (j t) d")

        def unit(q, v, ahead):
            q, v = q + (v + ahead) // 2, (v + ahead) % 2
            t = q * 2 + v
            return None if isinstance(t, int) and not 0 <= t < UNITS else (t, v, q)

        def steps(eng, step):
            for t in range(-4, 4):
                step(t // 2, t % 2)
            with eng.Fori(2, UNITS // 2 - 2) as q:
                for v in range(2):
                    step(q, v)
            for t in range(UNITS - 4, UNITS + 1):
                step(t // 2, t % 2)

        @block.gpsimd
        def _(pool):
            pool.wait_ge(k.zeroed, UNITS * UNIT // (8 * P) * 16)
            for t in range(TILES):
                for i in range(KEPT):
                    nc.gpsimd.indirect_dma_start(
                        out=queue, out_offset=bass.IndirectOffsetOnAxis(ap=index[:, t, i:i + 1], axis=0),
                        in_=xt[:, t, :], in_offset=None).then_inc(S["sent"], 16)

            def step(q, v):
                if u := unit(q, v, 2):
                    t, w, n = u
                    pool.wait_ge(S["wb_hi"], t + 1)
                    nc.gpsimd.tensor_tensor(wb_hl[D1:P, w, :], wb[D1:P, w, :], wb_hl[D1:P, w, :].bitcast(F32),
                                            ALU.subtract).then_inc(S["wb_lo"], 1)
                    pool.wait_ge(S["wb_lo"], t + 1)
                if u := unit(q, v, 3):
                    t, w, n = u
                    pool.wait_ge(x_in[w], n * 16 + 16)
                    nc.gpsimd.tensor_tensor(xq[:, w, :, D:2 * P], xq[:, w, :, P:D],
                                            k.nought[:, 0:P].rearrange("p (i c) -> p i c", i=2), ALU.subtract).then_inc(S["twice"], 1)
                    pool.wait_ge(S["twice"], t + 1)
                if u := unit(q, v, 1):
                    t, w, n = u
                    pool.wait_ge(S["wc_hi"], t * WP + WP)
                    nc.gpsimd.tensor_tensor(wc_lo[:, w, :], wc[:, w, :], wc_hi[:, w, :].bitcast(F32),
                                            ALU.subtract).then_inc(S["wc_lo"], 1)
                    pool.wait_ge(S["wc_lo"], t + 1)

            steps(pool, step)
            for v in range(2):
                pool.wait_ge(y_out[v], UNITS // 2 * 16)
            for t in range(TILES):
                for i in range(KEPT):
                    if t:
                        pool.wait_ge(S["added"], (t - 1) * KEPT + i + 1)
                    nc.gpsimd.indirect_dma_start(
                        out=back[:, i, :], out_offset=None, in_=answers,
                        in_offset=bass.IndirectOffsetOnAxis(ap=index[:, t, i:i + 1], axis=0)).then_inc(got[i], 16)

        @block.sync
        def _(sp):
            def expert(t):
                return sp.value_load(expert_of[0:1, bass.ds(t, 1)], min_val=0, max_val=NX0 - 1)

            def step(q, v):
                if u := unit(q, v, 4):
                    t, w, n = u
                    e = expert(t)
                    wait(sp, S["wa_lo"], t - 1)
                    wait(sp, S["wb_lo"], t - 1)
                    sp.dma_start(wa[:, w, :], d["w1_0"][e, 0:P, :]).then_inc(w1_in[w], 16)
                    for r in (0, D1):
                        sp.dma_start(wb[r:r + D1, w, :], d["w1_0"][e, P:D, :]).then_inc(w1_in[w], 16)
                if u := unit(q, v, 3):
                    t, w, n = u
                    e, before = expert(t), t - 1
                    wait(sp, S["act"], before * MC)
                    wait(sp, S["wc_lo"], before)
                    sp.dma_start(wc[:, w, :], d["w2_0"][e]).then_inc(w2_in[w], 16)
                    sp.dma_start(b1[:, w, :], d["b1_0"][e]).then_inc(w2_in[w], 16)
                if u := unit(q, v, 4):
                    t, w, n = u
                    wait(sp, S["turned"], t - 1)
                    if isinstance(t, int) and t == 0:
                        sp.wait_ge(S["sent"], TILES * KEPT * 16)
                    sp.dma_start(xq[:, w, :, 0:D],
                                 queue[bass.ds(t * UNIT, UNIT), :].rearrange("(i p) d -> p i d", p=P)
                                 ).then_inc(x_in[w], 16)
                if u := unit(q, v, -1):
                    t, w, n = u
                    sp.wait_ge(S["y"], t + 1)
                    sp.dma_start(answers[bass.ds(t * UNIT, UNIT), :].rearrange("(i p) d -> p i d", p=P),
                                 y[:, w, :, :]).then_inc(y_out[w], 16)

            sp.wait_ge(k.filters_stored, 64)
            steps(sp, step)

        @block.tensor
        def _(pe):
            def step(q, v):
                if u := unit(q, v, 1):
                    t, w, n = u
                    pe.wait_ge(S["wa_hi"], t + 1)
                    pe.wait_ge(S["wa_lo"], t + 1)
                    pe.wait_ge(S["wb_lo"], t + 1)
                    pe.wait_ge(S["x"], t + 1)
                    for m in range(MC):
                        ps = k.bank[(w * MC + m) % UP_BANKS][:, 0:UNIT]
                        c = slice(m * P, m * P + P)
                        wait(pe, S["act"], t * MC + (m + 1 - UP_BANKS))
                        nc.tensor.matmul(ps, wa_hi[:, w, c], ga_hi[:, :], start=True, stop=False)
                        nc.tensor.matmul(ps, wa_hi[:, w, c], ga_lo[:, :], start=False, stop=False)
                        nc.tensor.matmul(ps, wa_lo[:, w, c], ga_hi[:, :], start=False, stop=False)
                        nc.tensor.matmul(ps, wb_hl[:, w, c], gb_hi[:, :], start=False, stop=False)
                        nc.tensor.matmul(ps, wb_hl[0:D1, w, c], gb_lo[:, :], start=False,
                                         stop=True).then_inc(S["up"], 1)
                if u := unit(q, v, 2):
                    t, w, n = u
                    pe.wait_ge(S["twice"], t + 1)
                    for i in range(2):
                        for c in range(2):
                            mm = nc.tensor.transpose(k.bank[TURN_BANK][:, c * UNIT + i * P:c * UNIT + i * P + P],
                                                     xq[:, w, i, c * P:c * P + P], k.ident[:, :])
                    mm.then_inc(S["turned"], 1)
                if u := unit(q, v, 0):
                    t, w, n = u
                    pe.wait_ge(S["wc_lo"], t + 1)
                    wait(pe, S["y"], t - 1)
                    for i in range(2):
                        ps = k.bank[DOWN_BANK + w][:, i * D:i * D + D]
                        for m in range(MC):
                            if i == 0 and m % 2 == 0:
                                pe.wait_ge(S["h_lo"], t * HP + (m // 2 + 1))
                            hh, hl = (a[:, w, m, i * P:i * P + P] for a in (h_hi, h_lo))
                            wh, wl = (a[:, w, m * D:m * D + D] for a in (wc_hi, wc_lo))
                            nc.tensor.matmul(ps, hh, wh, start=(m == 0), stop=False)
                            nc.tensor.matmul(ps, hh, wl, start=False, stop=False)
                            mm = nc.tensor.matmul(ps, hl, wh, start=False, stop=(m == MC - 1))
                    mm.then_inc(S["down"], 1)

            steps(pe, step)

        @block.scalar
        def _(act):
            def gelu(u, m):
                if u:
                    t, w, n = u
                    act.wait_ge(S["up"], t * MC + (m + 1))
                    wait(act, S["h_lo"], (t - 1) * HP + (m // 2 + 1))
                    nc.scalar.activation(hT[:, m, :], k.bank[(w * MC + m) % UP_BANKS][:, 0:UNIT], ACT.Gelu,
                                         bias=b1[:, w, m:m + 1]).then_inc(S["act"], 1)

            def step(q, v):
                one, two, last = unit(q, v, 1), unit(q, v, 2), unit(q, v, -1)
                if two:
                    t, w, n = two
                    act.wait_ge(w1_in[w], n * 48 + 48)
                    wait(act, S["up"], (t - 1) * MC)
                    nc.scalar.activation(wa_hi[:, w, :], wa[:, w, :], ACT.Identity).then_inc(S["wa_hi"], 1)
                if one:
                    t, w, n = one
                    act.wait_ge(w2_in[w], n * 32 + 32)
                gelu(one, 0)
                if last:
                    t, w, n = last
                    act.wait_ge(S["down"], t + 1)
                    wait(act, y_out[w], n * 16)
                    nc.scalar.activation(y[:, w, :, :].rearrange("p i d -> p (i d)"),
                                         k.bank[DOWN_BANK + w][:, 0:2 * D], ACT.Identity).then_inc(S["y"], 1)
                gelu(one, 1)
                for m in range(2, MC):
                    gelu(one, m)
                    if one and m - 2 < WP:
                        t, w, n = one
                        wait(act, S["down"], t - 1)
                        c = slice((m - 2) * (MC * D // WP), (m - 1) * (MC * D // WP))
                        nc.scalar.activation(wc_hi[:, w, c], wc[:, w, c], ACT.Identity).then_inc(S["wc_hi"], 1)

            steps(act, step)

        @block.vector
        def _(dve):
            def step(q, v):
                one, two = unit(q, v, 1), unit(q, v, 2)

                def split_h(p):
                    if one:
                        t, w, n = one
                        dve.wait_ge(S["act"], t * MC + (2 * p + 2))
                        wait(dve, S["down"], t - 1)
                        m = slice(2 * p, 2 * p + 2)
                        nc.vector.tensor_copy(h_hi[:, w, m, :], hT[:, m, :]).then_inc(S["h_hi"], 1)
                        dve.wait_ge(S["h_hi"], t * HP + (p + 1))
                        nc.vector.tensor_tensor(h_lo[:, w, m, :], hT[:, m, :], h_hi[:, w, m, :].bitcast(F32),
                                                ALU.subtract).then_inc(S["h_lo"], 1)

                if two:
                    t, w, n = two
                    dve.wait_ge(w1_in[w], n * 48 + 48)
                    wait(dve, S["up"], (t - 1) * MC)
                    nc.vector.tensor_copy(wb_hl[:, w, :], wb[:, w, :]).then_inc(S["wb_hi"], 1)
                    dve.wait_ge(S["wa_hi"], t + 1)
                    nc.vector.tensor_tensor(wa_lo[:, w, :], wa[:, w, :], wa_hi[:, w, :].bitcast(F32),
                                            ALU.subtract).then_inc(S["wa_lo"], 1)
                for p in range(HP):
                    split_h(p)
                if two:
                    t, w, n = two
                    dve.wait_ge(S["turned"], t + 1)
                    ps = k.bank[TURN_BANK]
                    nc.vector.tensor_copy(ga_hi[:, :], ps[:, 0:UNIT]).then_inc(S["x_hi"], 1)
                    nc.vector.tensor_copy(gb_hi[:, :], ps[:, UNIT:2 * UNIT]).then_inc(S["x_hi"], 1)
                    dve.wait_ge(S["x_hi"], t * 2 + 2)
                    nc.vector.tensor_tensor(ga_lo[:, :], ps[:, 0:UNIT], ga_hi[:, :].bitcast(F32), ALU.subtract)
                    nc.vector.tensor_tensor(gb_lo[:, :], ps[0:D1, UNIT:2 * UNIT], gb_hi[0:D1, :].bitcast(F32),
                                            ALU.subtract).then_inc(S["x"], 1)

            steps(dve, step)
            for t in range(TILES):
                for i in range(KEPT):
                    dve.wait_ge(got[i], 16 * t + 16)
                    if i:
                        dve.wait_ge(S["added"], t * KEPT + i)
                    nc.vector.scalar_tensor_tensor(tile[:, t, :], back[:, i, :], share[:, t, i:i + 1], tile[:, t, :],
                                                   ALU.mult, ALU.add).then_inc(S["added"], 1)


def experts0(k, d):
    with ExitStack() as ctx:
        index = k.sb(ctx, "index", [P, TILES, KEPT], mybir.dt.uint32)
        share = k.sb(ctx, "share", [P, TILES, KEPT])
        expert_of = k.sb(ctx, "expert_of", [1, UNITS], mybir.dt.int32)
        combine = k.sb(ctx, "combine0", [P, TILES, NX0])
        with ExitStack() as own:
            chosen = k.sb(own, "chosen0", [P, TILES, NX0])
            gates(k, d, "g0", G0, E0, combine, "gate0", chosen)
            bias(k, d, "b0", NX0, combine, k.h, "b2_0")
            slots(k, d, chosen, combine, index, share, expert_of)
        routed(k, d, index, share, expert_of)



def norm_c(k, d):
    norm(k, "nc", d, k.h)


def hyena(k, d):
    nc = k.nc
    S = {n: k.sem("hy_" + n) for n in ("loaded", "z", "zs", "conv", "turned", "zcopy", "shift", "exp", "chain",
                                       "long", "upd", "vt", "vt0", "vt1", "out", "added", "wout")}
    tin = [k.sem(f"hy_tin{u}") for u in range(2)]
    NT = 2 * B
    CH = 5
    with ExitStack() as ctx:
        z = k.sb(ctx, "hy_z", [HALF, NT, 3 * D])
        bm = k.sb(ctx, "hy_b", [HALF, 2, D])
        wo0, wo1 = k.sb(ctx, "hy_wo0", [P, D]), k.sb(ctx, "hy_wo1", [D1 + 1, D])
        with ExitStack() as own, nc.Block() as block:
            w0, w1 = k.sb(own, "hy_w0", [P, 3 * D]), k.sb(own, "hy_w1", [D1 + 1, 3 * D])
            cw = k.sb(own, "hy_cw", [P, CH, 4])
            zs = k.sb(own, "hy_zs", [P, 2, PC])
            zc = k.sb(own, "hy_zc", [P, 2, PC])

            @block.sync
            def _(sp):
                for dst, src in ((w0[:, :], d["w_lin"][0:P, :]), (w1[:, :], d["w_lin"][P:D + 1, :]),
                                 (cw[:, :, :].rearrange("p a b -> p (a b)"), d["conv"]),
                                 (bm[:, :, :].rearrange("p a b -> p (a b)"), bcast_rows(d["bmat"], 2 * D, HALF)),
                                 (wo0[:, :], d["w_out"][0:P, :]), (wo1[:, :], d["w_out"][P:D + 1, :])):
                    sp.dma_start(dst, src).then_inc(S["loaded"], 16)
                sp.wait_ge(S["loaded"], 96)

            units = [(j, c) for j in range(PAIRS) for c in range(CH)]

            @block.tensor
            def _(pe):
                pe.wait_ge(S["loaded"], 96)
                def linear(n):
                    j, c = units[n]
                    m = P if c < CH - 1 else D1
                    if n >= 2:
                        pe.wait_ge(S["zs"], n - 1)
                    ps = k.bank[n % 2][0:m, 0:PC]
                    nc.tensor.matmul(ps, w0[:, c * P:c * P + m], k.xT0[:, j * PC:j * PC + PC], start=True, stop=False)
                    nc.tensor.matmul(ps, w1[:, c * P:c * P + m], k.xT1[0:D1 + 1, j * PC:j * PC + PC], start=False,
                                     stop=True).then_inc(S["z"], 1)

                def turn(n):
                    j, c = units[n]
                    m = P if c < CH - 1 else D1
                    pe.wait_ge(S["conv"], n + 1)
                    if n >= 2:
                        pe.wait_ge(S["zcopy"], n - 1)
                    for i in range(4):
                        mm = nc.tensor.transpose(k.bank[2 + n % 2][0:HALF, i * P:i * P + m],
                                                 zc[0:m, n % 2, i * HALF:i * HALF + HALF], k.ident[0:m, 0:m])
                    mm.then_inc(S["turned"], 1)

                linear(0)
                linear(1)
                for n in range(len(units)):
                    if n + 2 < len(units):
                        linear(n + 2)
                    turn(n)

            @block.scalar
            def _(act):
                def out(n):
                    j, c = units[n]
                    m = P if c < CH - 1 else D1
                    act.wait_ge(S["z"], n + 1)
                    if n >= 2:
                        act.wait_ge(S["conv"], n - 1)
                    nc.scalar.activation(zs[0:m, n % 2, :], k.bank[n % 2][0:m, 0:PC], ACT.Copy).then_inc(S["zs"], 1)

                def back(n):
                    j, c = units[n]
                    m = P if c < CH - 1 else D1
                    act.wait_ge(S["turned"], n + 1)
                    nc.scalar.activation(z[:, 4 * j:4 * j + 4, c * P:c * P + m],
                                         k.bank[2 + n % 2][0:HALF, :].rearrange("p (a b) -> p a b", a=4)[:, :, 0:m],
                                         ACT.Copy).then_inc(S["zcopy"], 1)

                out(0)
                out(1)
                for n in range(len(units)):
                    if n + 2 < len(units):
                        out(n + 2)
                    back(n)

            @block.vector
            def _(dve):
                ch = Chain(dve, S["chain"])
                dve.wait_ge(S["loaded"], 96)
                ch.did(nc.vector.tensor_tensor(wo0[:, 0:P], wo0[:, 0:P], k.ident[:, :], ALU.add))
                ch.did(nc.vector.tensor_tensor(wo1[0:D1, P:D], wo1[0:D1, P:D], k.ident[0:D1, 0:D1], ALU.add))
                for n, (j, c) in enumerate(units):
                    m = P if c < CH - 1 else D1
                    dve.wait_ge(S["zs"], n + 1)
                    if n >= 2:
                        dve.wait_ge(S["turned"], n - 1)
                    src = zs[0:m, n % 2, :].rearrange("p (b l) -> p b l", b=2)
                    dst = zc[0:m, n % 2, :].rearrange("p (b l) -> p b l", b=2)
                    ch.link(nc.vector.tensor_scalar(dst, src, cw[0:m, c, 2:3], cw[0:m, c, 3:4], ALU.mult, ALU.add))
                    if c >= 3:
                        x = (k.xT0, k.xT1)[c - 3][0:m, j * PC:j * PC + PC].rearrange("p (b l) -> p b l", b=2)
                        ch.link(nc.vector.tensor_tensor(dst, dst, x, ALU.add))
                    ch.link(nc.vector.scalar_tensor_tensor(dst[:, :, 1:L], src[:, :, 0:L - 1], cw[0:m, c, 1:2],
                                                           dst[:, :, 1:L], ALU.mult, ALU.add))
                    nc.vector.scalar_tensor_tensor(dst[:, :, 2:L], src[:, :, 0:L - 2], cw[0:m, c, 0:1],
                                                   dst[:, :, 2:L], ALU.mult, ALU.add).then_inc(S["conv"], 1)

        with ExitStack() as own, nc.Block() as block:
            most = k.sb(own, "hy_most", [HALF, 2, NT])
            T = k.sb(own, "hy_T", [HALF, 2, CG, L])
            tmp = k.sb(own, "hy_tmp", [HALF, NT, CG])
            v = z[:, :, 2 * D:3 * D]
            hp = d["filters"]

            @block.sync
            def _(sp):
                def load(g, o):
                    for s in range(0, HALF, FC):
                        src = bass.AP(hp.tensor, g * (CG * FC * FPITCH) + (o * D * FC * FPITCH + HALF - s),
                                      [[FPITCH - 1, FC], [FC * FPITCH, CG], [1, L]])
                        sp.dma_start(T[s:s + FC, o, :, :], src).then_inc(tin[o], 16)

                for o in range(2):
                    load(0, o)
                with sp.Fori(1, NCG) as g:
                    for o in range(2):
                        sp.wait_ge(S["long"], g * 2 + (o - 1))
                        load(g, o)
                for o in range(2):
                    sp.wait_ge(tin[o], NCG * 16 * (HALF // FC))

            @block.tensor
            def _(pe):
                with pe.Fori(0, NCG) as g:
                    for o in range(2):
                        pe.wait_ge(tin[o], g * (16 * (HALF // FC)) + 16 * (HALF // FC))
                        pe.wait_ge(S["upd"], g * 2 + (o + 1))
                        ps = k.bank[o][0:HALF, :].rearrange("p (c n) -> p c n", c=CG)
                        for c in range(CG):
                            vc = v[:, :, bass.ds(g * CG + c, 1)]
                            nc.tensor.matmul(ps[:, c, :], T[:, o, c, 0:HALF], vc.rearrange("p n a -> p (n a)"),
                                             start=True, stop=False)
                            first = v.rearrange("p (b i) c -> p b i c", i=2)[:, :, 0, bass.ds(g * CG + c, 1)]
                            mm = nc.tensor.matmul(ps.rearrange("p c (b i) -> p c b i", i=2)[:, c, :, 1],
                                                  T[:, o, c, HALF:L], first.rearrange("p b a -> p (b a)"),
                                                  start=False, stop=True)
                        mm.then_inc(S["long"], 1)

            @block.scalar
            def _(act):
                act.wait_ge(S["shift"], 1)
                nc.scalar.activation(z[:, :, 0:2 * D], z[:, :, 0:2 * D], ACT.Exp).then_inc(S["exp"], 1)

            @block.vector
            def _(dve):
                ch = Chain(dve, S["chain"])
                ch.n = 0
                base = sum(2 if c < 3 else 3 for c in range(CH)) * PAIRS + 2
                ch.base = base
                dve.wait_ge(S["chain"], base)
                x = [z[:, :, o * D:o * D + D] for o in range(2)]
                for o in range(2):
                    ch.did(nc.vector.tensor_reduce(most[:, o, :], x[o], AX.X, ALU.max))
                ch.sync()
                for o in range(2):
                    ins = nc.vector.tensor_tensor(x[o], x[o], over(most[:, o, :], D), ALU.subtract)
                ins.then_inc(S["shift"], 1)
                dve.wait_ge(S["exp"], 1)
                for o in range(2):
                    ch.link(nc.vector.tensor_reduce(most[:, o, :], x[o], AX.X, ALU.add))
                    ch.link(nc.vector.reciprocal(most[:, o, :], most[:, o, :]))
                for o in range(2):
                    ch.did(nc.vector.tensor_tensor(x[o], x[o], over(most[:, o, :], D), ALU.mult))
                ch.sync()
                dve.sem_inc(S["upd"], 1)
                with dve.Fori(0, NCG) as g:
                    ch.enter(g, 6)
                    for o in range(2):
                        vg = v[:, :, bass.ds(g * CG, CG)]
                        xg = x[o][:, :, bass.ds(g * CG, CG)]
                        ps = k.bank[o][0:HALF, :].rearrange("p (c n) -> p n c", c=CG)
                        bg = bm[:, o, bass.ds(g * CG, CG)].unsqueeze(1).broadcast_to([HALF, NT, CG])
                        dve.wait_ge(S["upd"], g * 2 + (o + 1))
                        ch.link(nc.vector.tensor_tensor(tmp[:, :, :], vg, bg, ALU.mult))
                        dve.wait_ge(S["long"], g * 2 + (o + 1))
                        ch.link(nc.vector.tensor_tensor(tmp[:, :, :], ps, tmp[:, :, :], ALU.add))
                        ch.link(nc.vector.tensor_tensor(tmp[:, :, :], tmp[:, :, :], xg, ALU.mult))
                        nc.vector.tensor_tensor(vg, vg, tmp[:, :, :], ALU.add).then_inc(S["upd"], 1)
                    ch.leave(NCG)

        with ExitStack() as own, nc.Block() as block:
            v = z[:, :, 2 * D:3 * D]

            @block.tensor
            def _(pe):
                for j in range(PAIRS):
                    u = j % 2
                    if j >= 2:
                        pe.wait_ge(S["vt0"], j - 1)
                        pe.wait_ge(S["vt1"], j - 1)
                    for i in range(4):
                        nc.tensor.transpose(k.bank[u][:, i * HALF:i * HALF + HALF], v[:, 4 * j + i, 0:P],
                                            k.ident[0:HALF, 0:HALF])
                        mm = nc.tensor.transpose(k.bank[2 + u][0:D1, i * HALF:i * HALF + HALF], v[:, 4 * j + i, P:D],
                                                 k.ident[0:HALF, 0:HALF])
                    mm.then_inc(S["vt"], 1)
                for j in range(PAIRS):
                    pe.wait_ge(S["vt0"], j + 1)
                    pe.wait_ge(S["vt1"], j + 1)
                    if j:
                        pe.wait_ge(S["added"], j)
                    for t in range(3):
                        at = j * PC + t * P
                        nc.tensor.matmul(k.bank[4 + t][:, 0:D], k.xT0[:, at:at + P], wo0[:, :], start=True, stop=False)
                        mm = nc.tensor.matmul(k.bank[4 + t][:, 0:D], k.xT1[0:D1 + 1, at:at + P], wo1[:, :],
                                              start=False, stop=True)
                    mm.then_inc(S["out"], 1)

            @block.scalar
            def _(act):
                for j in range(PAIRS):
                    act.wait_ge(S["vt"], j + 1)
                    nc.scalar.activation(k.xT0[:, j * PC:j * PC + PC], k.bank[j % 2][:, 0:PC],
                                         ACT.Copy).then_inc(S["vt0"], 1)

            @block.vector
            def _(dve):
                for j in range(PAIRS):
                    dve.wait_ge(S["vt"], j + 1)
                    nc.vector.tensor_copy(k.xT1[0:D1, j * PC:j * PC + PC],
                                          k.bank[2 + j % 2][0:D1, 0:PC]).then_inc(S["vt1"], 1)
                for j in range(PAIRS):
                    dve.wait_ge(S["out"], j + 1)
                    for t in range(3):
                        a = nc.vector.tensor_tensor(k.h[:, j, t, :], k.bank[4 + t][:, 0:D], k.h[:, j, t, :], ALU.add)
                    a.then_inc(S["added"], 1)



def norm_d(k, d):
    norm(k, "nd", d, k.h)


def attention(k, d):
    nc = k.nc
    names = ("loaded", "consts", "staged", "kq", "kt", "qt", "vals", "qtok", "qcopy", "vcopy", "s1", "stats", "sd", "rt",
             "aug", "turned", "qat", "s2", "probs", "pv", "attn", "at", "at0", "at1", "out", "added", "chain",
             "zero", "sign", "dev")
    S = {n: k.sem("at_" + n) for n in names}
    HC = 3
    NCH = HEADS // HC
    HP = HC * 32
    N_S = 3 * HEADS // 2
    with ExitStack() as ctx, nc.Block() as block:
        wq0, wq1 = k.sb(ctx, "at_wq0", [P, NCH * HP]), k.sb(ctx, "at_wq1", [D1 + 1, NCH * HP])
        wk0, wk1 = k.sb(ctx, "at_wk0", [P, NCH * HP]), k.sb(ctx, "at_wk1", [D1 + 1, NCH * HP])
        w0, w1 = k.sb(ctx, "at_w0", [P, 3, D]), k.sb(ctx, "at_w1", [D1 + 1, 3, D])
        gam = k.sb(ctx, "at_gamma", [P, 3])
        x0, x1 = k.sb(ctx, "at_x0", [P, PC]), k.sb(ctx, "at_x1", [D1 + 1, PC])
        kT, qT = k.sb(ctx, "at_kT", [HP, NCH, PC]), k.sb(ctx, "at_qT", [HP, NCH, PC])
        va = k.sb(ctx, "at_va", [P, 2, 3, HEADS, HD + 1])
        qa = k.sb(ctx, "at_qa", [P, 3, HEADS, 32])
        qaT = k.sb(ctx, "at_qaT", [HP, NCH, PC])
        st = k.sb(ctx, "at_st", [P, 3 * HEADS, 6])
        mx = k.sb(ctx, "at_mx", [P, 3 * HEADS])
        dv = k.sb(ctx, "at_dv", [P, 3, 3 * HEADS])
        pT = k.sb(ctx, "at_pT", [P, 3, HEADS, L])
        rec = k.sb(ctx, "at_rec", [P, 3, HEADS])
        att = k.sb(ctx, "at_att", [P, 3, D])
        a0, a1 = k.sb(ctx, "at_a0", [P, PC]), k.sb(ctx, "at_a1", [D1 + 1, PC])
        bank = k.bank
        S2_BANKS = (4, 5, 0, 1, 2, 3)
        K_BANKS, Q_T_BANKS = (6, 7, 4, 5), (0, 1, 2, 3)
        V_BANKS, Q_BANKS = ((6, 0), (6, D), (7, 0)), ((4, 0), (4, D), (5, 0))
        S1_BANKS = (0, 1, 2, 3, 4, 5)
        PV_BANKS = ((6, 0), (7, 0), (7, HEADS * (HD + 1)))
        TURN_BANKS, AT_BANKS = (0, 1, 2, 3), (4, 5)
        O_BANKS = ((6, 0), (6, D), (7, 0))
        NS1, NS2 = len(S1_BANKS), len(S2_BANKS)
        PARTS = (((0, P, 0),), ((0, 64, 0), (64, P, L)), ((0, P, L),))

        def pair_of(n):
            t, m, i = n // (HEADS // 2), n % (HEADS // 2) // HC, n % HC
            return t, (2 * HC * m + i, 2 * HC * m + i + HC)

        def steps(eng, step, ch=None, per=0):
            with eng.Fori(0, PAIRS // 2 - 1) as q:
                if ch:
                    ch.enter(q, 2 * per)
                for u in range(2):
                    step(q * 2 + u, u, False)
                if ch:
                    ch.leave(PAIRS // 2 - 1)
            step(PAIRS - 2, 0, False)
            step(PAIRS - 1, 1, True)

        def two(ap, heads):
            return ap[:, heads[0]:heads[1] + 1:HC]

        @block.sync
        def _(sp):
            for dst, src in ((wq0, d["wq_heads"][0:P, :]), (wq1, d["wq_heads"][P:D + 1, :]),
                             (wk0, d["wk_heads"][0:P, :]), (wk1, d["wk_heads"][P:D + 1, :])):
                sp.dma_start(dst[:, :], src).then_inc(S["loaded"], 16)
            for n, w in enumerate(("wq", "wv", "wo")):
                sp.dma_start(w0[:, n, :], d[w][0:P, :]).then_inc(S["loaded"], 16)
                sp.dma_start(w1[:, n, :], d[w][P:D + 1, :]).then_inc(S["loaded"], 16)
            sp.dma_start(gam[:, 0:1], bcast_rows(d["gamma"], 1)).then_inc(S["loaded"], 16)
            sp.wait_ge(S["loaded"], 176)

        @block.gpsimd
        def _(pool):
            nc.gpsimd.memset(qa[:, :, :, :].rearrange("p a b c -> p (a b c)"), 0.0).then_inc(S["zero"], 1)
            pool.wait_ge(S["zero"], 1)
            nc.gpsimd.memset(va[:].rearrange("p u a b c -> p (u a b c)"), 1.0).then_inc(S["zero"], 1)
            pool.wait_ge(S["zero"], 2)
            nc.gpsimd.memset(a1[D1:D1 + 1, :], 1.0).then_inc(S["zero"], 1)
            pool.wait_ge(S["zero"], 3)

            def stage(j):
                nc.gpsimd.tensor_copy(x0[:, :], k.xT0[:, bass.ds(j * PC, PC)]).then_inc(S["staged"], 1)
                pool.wait_ge(S["staged"], j * 2 + 1)
                nc.gpsimd.tensor_copy(x1[:, :], k.xT1[0:D1 + 1, bass.ds(j * PC, PC)]).then_inc(S["staged"], 1)

            stage(0)
            with pool.Fori(1, PAIRS) as j:
                pool.wait_ge(S["qtok"], j)
                pool.wait_ge(S["staged"], j * 2)
                stage(j)

        @block.tensor
        def _(pe):
            def project(j):
                pe.wait_ge(S["staged"], j * 2 + 2)
                wait(pe, S["added"], j - 1)
                wait(pe, S["probs"], j * N_S - 4)
                for wa, wb, places in ((wk0, wk1, K_BANKS), (wq0, wq1, Q_T_BANKS)):
                    for c in range(NCH):
                        ps = bank[places[c]][0:HP, 0:PC]
                        nc.tensor.matmul(ps, wa[:, c * HP:c * HP + HP], x0[:, :], start=True, stop=False)
                        mm = nc.tensor.matmul(ps, wb[:, c * HP:c * HP + HP], x1[:, :], start=False, stop=True)
                    mm.then_inc(S["kq"], 1)
                    if wa is wk0:
                        wait(pe, S["probs"], j * N_S)

                def tokens(n, places):
                    for t, (b, at) in enumerate(places):
                        nc.tensor.matmul(bank[b][:, at:at + D], x0[:, t * P:t * P + P], w0[:, n, :],
                                         start=True, stop=False)
                        mm = nc.tensor.matmul(bank[b][:, at:at + D], x1[:, t * P:t * P + P], w1[:, n, :],
                                              start=False, stop=True)
                    return mm

                pe.wait_ge(S["kt"], j + 1)
                tokens(1, V_BANKS).then_inc(S["vals"], 1)
                tokens(0, Q_BANKS).then_inc(S["qtok"], 1)

            def first(j):
                pe.wait_ge(S["qt"], j + 1)
                pe.wait_ge(S["qcopy"], j + 1)
                for n in range(N_S):
                    t, heads = pair_of(n)
                    if n >= NS1:
                        pe.wait_ge(S["stats"], j * N_S + (n - NS1 + 1))
                    for i, h in enumerate(heads):
                        r, c = 32 * (h % HC), h // HC
                        for lo, hi, b0 in PARTS[t]:
                            mm = nc.tensor.matmul(bank[S1_BANKS[n % NS1]][lo:hi, i * L:i * L + L],
                                                  qT[r:r + HD, c, t * P + lo:t * P + hi],
                                                  kT[r:r + HD, c, b0:b0 + L], start=True, stop=True)
                    mm.then_inc(S["s1"], 1)

            def turn(j):
                pe.wait_ge(S["aug"], j + 1)
                for c in range(NCH):
                    for t in range(3):
                        mm = nc.tensor.transpose(bank[TURN_BANKS[c]][0:HP, t * P:t * P + P],
                                                 qa[:, t, HC * c:HC * c + HC, :].rearrange("p a b -> p (a b)"),
                                                 k.ident[:, :])
                mm.then_inc(S["turned"], 1)

            def second(j):
                pe.wait_ge(S["qat"], j + 1)
                for n in range(N_S):
                    t, heads = pair_of(n)
                    if n >= NS2:
                        pe.wait_ge(S["probs"], j * N_S + (n - NS2 + 1))
                    for i, h in enumerate(heads):
                        r, c = 32 * (h % HC), h // HC
                        for lo, hi, b0 in PARTS[t]:
                            mm = nc.tensor.matmul(bank[S2_BANKS[n % NS2]][lo:hi, i * L:i * L + L],
                                                  kT[r:r + HD + 1, c, t * P + lo:t * P + hi],
                                                  qaT[r:r + HD + 1, c, b0:b0 + L], start=True, stop=True)
                    mm.then_inc(S["s2"], 1)

            def product(j, u):
                pe.wait_ge(S["probs"], j * N_S + N_S)
                for t in range(3):
                    b, at = PV_BANKS[t]
                    for lo, hi, b0 in PARTS[t]:
                        q0 = t * P + lo - b0
                        e = b0 // L
                        big, s0 = 2 * e, 64 * e
                        for h in range(HEADS):
                            o = bank[b][lo:hi, at + h * (HD + 1):at + (h + 1) * (HD + 1)]
                            nc.tensor.matmul(o, pT[:, big, h, q0:q0 + hi - lo], va[:, u, big, h, :],
                                             start=True, stop=False)
                            mm = nc.tensor.matmul(o, pT[s0:s0 + 64, 1, h, q0:q0 + hi - lo],
                                                  va[s0:s0 + 64, u, 1, h, :], start=False, stop=True)
                    if t != 1:
                        mm.then_inc(S["pv"], 1)

            def project_out(j):
                pe.wait_ge(S["attn"], j + 1)
                for t in range(3):
                    nc.tensor.transpose(bank[AT_BANKS[0]][:, t * P:t * P + P], att[:, t, 0:P], k.ident[:, :])
                    mm = nc.tensor.transpose(bank[AT_BANKS[1]][0:D1, t * P:t * P + P], att[:, t, P:D], k.ident[:, :])
                mm.then_inc(S["at"], 1)
                pe.wait_ge(S["at0"], j + 1)
                pe.wait_ge(S["at1"], j + 1)
                for t, (b, at) in enumerate(O_BANKS):
                    nc.tensor.matmul(bank[b][:, at:at + D], a0[:, t * P:t * P + P], w0[:, 2, :], start=True, stop=False)
                    mm = nc.tensor.matmul(bank[b][:, at:at + D], a1[:, t * P:t * P + P], w1[:, 2, :], start=False,
                                          stop=True)
                mm.then_inc(S["out"], 1)

            def step(j, u, last):
                second(j)
                if not last:
                    project(j + 1)
                    first(j + 1)
                    pe.wait_ge(S["vcopy"], j + 2)
                else:
                    pe.wait_ge(S["added"], j)
                product(j, u)
                if not last:
                    turn(j + 1)
                project_out(j)

            pe.wait_ge(S["loaded"], 176)
            pe.wait_ge(S["zero"], 3)
            project(0)
            first(0)
            turn(0)
            steps(pe, step)

        @block.scalar
        def _(act):
            act.wait_ge(S["loaded"], 176)
            nc.scalar.activation(gam[:, 1:2], gam[:, 0:1], ACT.Sign).then_inc(S["sign"], 1)
            nc.scalar.activation(gam[:, 2:3], gam[:, 0:1], ACT.Abs).then_inc(S["sign"], 1)
            act.wait_ge(S["consts"], 1)

            def project(j):
                act.wait_ge(S["kq"], j * 2 + 1)
                for c in range(NCH):
                    a = nc.scalar.activation(kT[:, c, :], bank[K_BANKS[c]][0:HP, 0:PC], ACT.Copy)
                a.then_inc(S["kt"], 1)
                act.wait_ge(S["kq"], j * 2 + 2)
                for c in range(NCH):
                    a = nc.scalar.activation(qT[:, c, :], bank[Q_T_BANKS[c]][0:HP, 0:PC], ACT.Copy,
                                             scale=gam[0:HP, 1:2])
                a.then_inc(S["qt"], 1)
                act.wait_ge(S["dev"], j + 1)
                nc.scalar.activation(dv[:, 1, :], dv[:, 0, :], ACT.Sqrt).then_inc(S["sd"], 1)
                act.wait_ge(S["turned"], j + 1)
                for c in range(NCH):
                    a = nc.scalar.activation(qaT[:, c, :], bank[TURN_BANKS[c]][0:HP, 0:PC], ACT.Copy)
                a.then_inc(S["qat"], 1)

            def step(j, u, last):
                for n in range(N_S):
                    t, heads = pair_of(n)
                    act.wait_ge(S["s2"], j * N_S + (n + 1))
                    nc.scalar.activation(two(pT[:, t], heads),
                                         bank[S2_BANKS[n % NS2]][:, 0:2 * L].rearrange("p (a b) -> p a b", a=2),
                                         ACT.Exp).then_inc(S["probs"], 1)
                if not last:
                    project(j + 1)
                act.wait_ge(S["at"], j + 1)
                nc.scalar.activation(a0[:, :], bank[AT_BANKS[0]][:, 0:PC], ACT.Copy).then_inc(S["at0"], 1)

            project(0)
            steps(act, step)

        @block.vector
        def _(dve):
            ch = Chain(dve, S["chain"])
            dve.wait_ge(S["sign"], 2)
            nc.vector.tensor_scalar(gam[:, 1:2], gam[:, 1:2], float(HD) ** -0.5, None,
                                    ALU.mult).then_inc(S["consts"], 1)
            dve.wait_ge(S["consts"], 1)
            dve.wait_ge(S["zero"], 3)

            def project(j, u):
                dve.wait_ge(S["vals"], j + 1)
                for t, (b, at) in enumerate(V_BANKS):
                    a = nc.vector.tensor_copy(va[:, u, t, :, 0:HD],
                                              bank[b][:, at:at + D].rearrange("p (h e) -> p h e", h=HEADS))
                a.then_inc(S["vcopy"], 1)
                dve.wait_ge(S["qtok"], j + 1)
                for t, (b, at) in enumerate(Q_BANKS):
                    a = nc.vector.tensor_scalar(qa[:, t, :, 0:HD],
                                                bank[b][:, at:at + D].rearrange("p (h e) -> p h e", h=HEADS),
                                                gam[:, 1:2], None, ALU.mult)
                a.then_inc(S["qcopy"], 1)
                for n in range(N_S):
                    t, heads = pair_of(n)
                    dve.wait_ge(S["s1"], j * N_S + (n + 1))
                    ps = bank[S1_BANKS[n % NS1]][:, 0:2 * L].rearrange("p (a b) -> p a b", a=2)
                    for i, h in enumerate(heads):
                        ch.did(nc.vector.bn_stats(st[:, t * HEADS + h, :], ps[:, i, :]))
                    nc.vector.tensor_reduce(two(mx[:, t * HEADS:t * HEADS + HEADS], heads), ps, AX.X,
                                            ALU.max).then_inc(S["stats"], 1)
                ch.sync()
                dve.wait_ge(S["stats"], j * N_S + N_S)
                ch.did(nc.vector.tensor_tensor(dv[:, 0, :], st[:, :, 1], st[:, :, 4], ALU.subtract))
                ch.did(nc.vector.tensor_tensor(dv[:, 1, :], st[:, :, 2], st[:, :, 5], ALU.add))
                ch.sync()
                ch.link(nc.vector.scalar_tensor_tensor(dv[:, 0, :], dv[:, 0, :], L / 4, dv[:, 0, :], ALU.mult, ALU.mult))
                ch.link(nc.vector.tensor_tensor(dv[:, 0, :], dv[:, 0, :], dv[:, 1, :], ALU.add))
                nc.vector.tensor_scalar(dv[:, 0, :], dv[:, 0, :], 1.0 / (L - 1), None, ALU.mult).then_inc(S["dev"], 1)
                dve.wait_ge(S["sd"], j + 1)
                ch.link(nc.vector.tensor_scalar(dv[:, 1, :], dv[:, 1, :], 1e-5, None, ALU.add))
                ch.link(nc.vector.reciprocal(dv[:, 1, :], dv[:, 1, :]))
                ch.link(nc.vector.tensor_scalar(dv[:, 2, :], dv[:, 1, :], gam[:, 2:3], None, ALU.mult))
                r = dv[:, 2, :].rearrange("p (t h) -> p t h", t=3)
                for t in range(3):
                    ch.did(nc.vector.tensor_tensor(qa[:, t, :, 0:HD], qa[:, t, :, 0:HD], over(r[:, t, :], HD),
                                                   ALU.mult))
                nc.vector.scalar_tensor_tensor(qa[:, :, :, HD], mx[:, :].rearrange("p (t h) -> p t h", t=3), -1.0, r,
                                               ALU.mult, ALU.mult).then_inc(S["aug"], 1)

            def step(j, u, last):
                if not last:
                    project(j + 1, 1 - u)
                for t in range(3):
                    if t != 2:
                        dve.wait_ge(S["pv"], j * 2 + (t + 1))
                    b, at = PV_BANKS[t]
                    o = bank[b][:, at:at + HEADS * (HD + 1)].rearrange("p (h e) -> p h e", h=HEADS)
                    ch.link(nc.vector.reciprocal(rec[:, t, :], o[:, :, HD]))
                    a = nc.vector.tensor_tensor(att[:, t, :].rearrange("p (h e) -> p h e", h=HEADS), o[:, :, 0:HD],
                                                over(rec[:, t, :], HD), ALU.mult)
                a.then_inc(S["attn"], 1)
                dve.wait_ge(S["at"], j + 1)
                nc.vector.tensor_copy(a1[0:D1, :], bank[AT_BANKS[1]][0:D1, 0:PC]).then_inc(S["at1"], 1)
                dve.wait_ge(S["out"], j + 1)
                for t, (b, at) in enumerate(O_BANKS):
                    a = nc.vector.tensor_tensor(k.xn[:, j, t, :],
                                                bank[b][:, at:at + D], k.xn[:, j, t, :], ALU.add)
                a.then_inc(S["added"], 1)

            IN = 2 * N_S + 4 + 3 + 3
            project(0, 0)
            steps(dve, step, ch, IN + 3)


def norm_e(k, d):
    norm(k, "ne", d, k.xn, affine="ln1")


def experts1(k, d):
    with ExitStack() as ctx:
        combine = k.sb(ctx, "combine1", [P, PAIRS * 3, NX1])
        gates(k, d, "g1", 1, NX1, combine, "gate1")
        bias(k, d, "b1", NX1, combine, k.xn, "b2_1")
        experts(k, d, "x1", NX1, ACT.Relu, combine, k.xn, "w1_1", "w2_1")


def finish(k, d):
    nc = k.nc
    norm(k, "nf", d, k.xn, affine="ln2", dst=k.xn)
    done = k.sem("fi_done")
    with nc.Block() as block:
        @block.vector
        def _(dve):
            nc.vector.tensor_tensor(k.h[:].rearrange("p a b c -> p (a b c)"),
                                    k.h[:].rearrange("p a b c -> p (a b c)"),
                                    k.xn[:].rearrange("p a b c -> p (a b c)"), ALU.add).then_inc(done, 1)


PHASES = (setup, tokenizer, norm_a, retention, norm_b, experts0, norm_c, hyena, norm_d, attention, norm_e, experts1,
          finish)



def store(k, out):
    nc = k.nc
    stored = k.sem("stored")
    with nc.Block() as block:
        @block.sync
        def _(sp):
            tiles = out.rearrange("b l d -> (b l) d").rearrange("(j t p) d -> p j t d", t=3, p=P)
            sp.dma_start(tiles, k.h[:, :, :, :]).then_inc(stored, 16)
            sp.wait_ge(stored, 16)


def program(nc, d, out):
    d = dict(d)
    for name, shape in (("filters", (2, D, FC, FPITCH)), ("positions", (B, OFFC, 64)),
                    ("queue", (UNITS * UNIT, D)), ("answers", (UNITS * UNIT, D))):
        d[name] = nc.dram_tensor(name + "_scratch", shape, F32, kind="Internal").ap()
    with ExitStack() as ctx:
        k = Core(nc, ctx)
        for phase in PHASES:
            phase(k, d)
            if phase is experts0:
                k.clear_semaphores()
        store(k, out)



def lay_out(i):
    import numpy as np

    def rows(w, b):
        return np.concatenate([w, b.reshape(w.shape[:-2] + (1, w.shape[-1]))], axis=-2)

    def heads(w, b, one):
        full = rows(w, b)
        out = np.zeros((D + 1, HEADS, 32), np.float32)
        out[:, :, 0:HD] = full.reshape(D + 1, HEADS, HD)
        if one:
            out[D, :, HD] = 1.0
        return out.reshape(D + 1, HEADS * 32)

    part = np.arange(P)
    a = {}
    a["patches"] = i["x"].reshape(B, 3, 32, 4, 32, 4).transpose(0, 1, 3, 5, 2, 4).reshape(B, 48, HW)
    a["txt"] = i["txt"]
    a["stem_w"] = i["L0_tok_stem_w"].reshape(CS, 48).T
    a["v96"] = np.stack([i["L0_tok_" + n] for n in ("stem_b", "bn1_g", "bn1_b", "bn1_m", "bn1_v")], 1)
    a["v192"] = np.stack([i["L0_tok_" + n] for n in ("dcn_b", "bn2_g", "bn2_b", "bn2_m", "bn2_v")]).reshape(-1)
    a["off_w"] = i["L0_tok_off_w"].transpose(1, 2, 3, 0).reshape(CS, TAPS * OFFC)
    a["off_b"] = i["L0_tok_off_b"].reshape(OFFC, 1)
    a["dcn_w"] = i["L0_tok_dcn_w"].transpose(1, 2, 3, 0).reshape(CS, TAPS * D)
    tap, o = np.arange(TAPS), np.arange(8)
    gy = (4 * o[None, :, None] + (tap // 4)[:, None, None]) + 0 * o[None, None, :]
    gx = (4 * o[None, None, :] + (tap % 4)[:, None, None]) + 0 * o[None, :, None]
    a["grid"] = np.stack([gy, gx], 1).reshape(OFFC, 64).astype(np.float32)
    a["xy"] = -np.concatenate([(part % 32)[:, None], 4 * np.arange(YCH)[None, :] + (part // 32)[:, None]],
                              1).astype(np.float32)
    a["ident"] = np.eye(P, dtype=np.float32)
    a["times"] = np.linspace(0.0, 1.0, 512, dtype=np.float32)[0:L]
    a["h_param"] = i["L1_attn_h_param"]
    a["filter_par"] = np.stack([i["L1_attn_alphas"].reshape(D), i["L1_attn_win_b"].reshape(D)], 1)
    at = np.arange(L)
    dist = at[None, :] - at[:, None]
    decay = np.where(dist >= 0, np.float32(0.99) ** np.maximum(dist, 0).astype(np.float32), 0)
    decay = (decay / np.sqrt(np.float32(D))).astype(np.float32)
    a["decay"] = np.zeros((P, 2, 2, L), np.float32)
    a["decay"][:, 0, 0], a["decay"][0:64, 0, 1] = decay[0:P], decay[P:L]
    a["decay"][64:P, 1, 1], a["decay"][:, 1, 0] = decay[0:64], decay[64:L]
    a["decay"] = a["decay"].reshape(P, 4 * L)
    a["qkv"] = rows(i["L0_attn_W_qkv"], i["L0_attn_b_qkv"])
    we = i["L0_ffn_We"].transpose(1, 0, 2).reshape(D, NX0)
    a["gate0"] = rows(np.concatenate([i["L0_ffn_Wg"], we], 1),
                      np.concatenate([i["L0_ffn_bg"], i["L0_ffn_be"].reshape(-1)]))
    a["w1_0"] = i["L0_ffn_W1"].reshape(NX0, D, FF)
    a["b1_0"] = i["L0_ffn_b1"].reshape(NX0, MC, P).transpose(0, 2, 1)
    a["w2_0"] = i["L0_ffn_W2"].reshape(NX0, MC, P, D).transpose(0, 2, 1, 3).reshape(NX0, P, MC * D)
    a["before"] = (part[:, None] < part[None, :]).astype(np.float32)
    a["unit_numbers"] = np.arange(UNITS, dtype=np.float32)[None, :]
    a["b2_0"] = i["L0_ffn_b2"].reshape(NX0, D)
    a["w_lin"] = rows(i["L1_attn_W_lin"].T, i["L1_attn_b_lin"])
    conv = np.zeros((5 * P, 4), np.float32)
    conv[0:3 * D, 0:3] = i["L1_attn_conv_w"].reshape(3 * D, 3)
    conv[0:3 * D, 3] = i["L1_attn_conv_b"]
    a["conv"] = conv.reshape(5, P, 4).transpose(1, 0, 2).reshape(P, 20)
    a["bmat"] = i["L1_attn_Bmat"].reshape(2 * D)
    a["w_out"] = rows(i["L1_attn_W_out"].T, i["L1_attn_b_out"])
    a["wq_heads"] = heads(i["L1_ffn_Wq"].T, i["L1_ffn_bq"], False)
    a["wk_heads"] = heads(i["L1_ffn_Wk"].T, i["L1_ffn_bk"], True)
    a["wq"] = rows(i["L1_ffn_Wq"].T, i["L1_ffn_bq"])
    a["wv"] = rows(i["L1_ffn_Wv"].T, i["L1_ffn_bv"])
    a["wo"] = rows(i["L1_ffn_Wo"].T, i["L1_ffn_bo"])
    a["gamma"] = i["L1_ffn_gamma"].reshape(1)
    a["ln1"] = np.concatenate([i["L1_ffn_ln1_g"], i["L1_ffn_ln1_b"]])
    a["ln2"] = np.concatenate([i["L1_ffn_ln2_g"], i["L1_ffn_ln2_b"]])
    a["gate1"] = rows(i["L1_ffn_Wg"].T, i["L1_ffn_bg"])
    a["w1_1"] = rows(i["L1_ffn_W1"], i["L1_ffn_b1"])
    a["w2_1"] = i["L1_ffn_W2"].reshape(NX1, MC, P, D).transpose(0, 2, 1, 3).reshape(NX1, P, MC * D)
    a["b2_1"] = i["L1_ffn_b2"]
    return {n: np.ascontiguousarray(v) for n, v in a.items()}


def kernel(**inputs):
    import numpy as np
    import concourse.bacc as bacc
    from concourse.bass_utils import run_bass_kernel_spmd

    arrays = lay_out({n: np.asarray(v) for n, v in inputs.items()})
    nc = bacc.Bacc("TRN2", target_bir_lowering=False, num_devices=1)
    d = {n: nc.dram_tensor("in_" + n, a.shape, F32, kind="ExternalInput").ap() for n, a in arrays.items()}
    out = nc.dram_tensor("out", (B, L, D), F32, kind="ExternalOutput").ap()
    program(nc, d, out)
    r = run_bass_kernel_spmd(nc, [{"in_" + n: a for n, a in arrays.items()}], core_ids=[0])
    return r.results[0]["out"]
```

```python
from contextlib import ExitStack

import concourse.bass as bass
from concourse import mybir

F32 = mybir.dt.float32
F32R = mybir.dt.float32r
ALU = mybir.AluOpType
ACT = mybir.ActivationFunctionType
AX = mybir.AxisListType

P = 128
B = 16
PAIRS = B // 2
IMG, TXT = 64, 128
L = IMG + TXT
D = 192
D1 = D - P
PC = 2 * L
CS = 96
HW = 1024
TAPS = 16
OFFC = 2 * TAPS
YCH = HW // P
FF = 768
MC = FF // P
G0, E0 = 4, 8
NX0 = G0 * E0
NX1 = 4
HEADS, HD = 12, 16
LN_EPS = 1e-5
HALF = L // 2
FPITCH = HALF + L
FC = 24
CG = 16
NCG = D // CG


def wait(eng, sem, value):
    if not isinstance(value, int) or value > 0:
        eng.wait_ge(sem, value)


class Chain:

    def __init__(self, eng, sem):
        self.eng, self.sem, self.base, self.n = eng, sem, 0, 0

    def did(self, ins):
        ins.then_inc(self.sem, 1)
        self.n += 1

    def sync(self):
        self.eng.wait_ge(self.sem, self.base + self.n)

    def link(self, ins):
        self.did(ins)
        self.sync()

    def enter(self, index, per):
        self.start, self.per = self.base + self.n, per
        self.base, self.n = index * per + self.start, 0

    def leave(self, turns):
        assert self.n == self.per, (self.n, self.per)
        self.base, self.n = self.start + turns * self.per, 0


class Core:

    def __init__(self, nc, ctx):
        self.nc, self.ctx = nc, ctx
        self.sems = []
        self.h = self.sb(ctx, "h", [P, PAIRS, 3, D])
        self.xn = self.sb(ctx, "xn", [P, PAIRS, 3, D])
        self.xT0 = self.sb(ctx, "xT0", [P, PAIRS * PC])
        self.xT1 = self.sb(ctx, "xT1", [P, PAIRS * PC])
        self.ident = self.sb(ctx, "ident", [P, P])
        self.ones = self.sb(ctx, "ones", [P, P])
        self.eps = self.sb(ctx, "eps", [P, 1])
        self.nought = self.sb(ctx, "nought", [P, 8 * D])
        self.hz = self.sb(ctx, "hz", [P, 2, 2, FPITCH])
        self.bank = [ctx.enter_context(nc.psum_tensor(f"bank{i}", [P, 512], F32)) for i in range(8)]
        self.setup_done = self.sem("setup_done")
        self.zeroed = self.sem("queue_zeroed")
        self.filters_stored = self.sem("filters_stored")

    def sb(self, ctx, name, shape, dt=F32):
        return ctx.enter_context(self.nc.sbuf_tensor(name, shape, dt))

    def sem(self, name):
        s = self.nc.alloc_semaphore(name=name)
        self.sems.append(s)
        return s

    def clear_semaphores(self):
        self.nc.clear_and_free_semaphores(self.sems)
        self.nc.all_engine_barrier()
        self.sems = []


def bcast_rows(ap, n, parts=P):
    return bass.AP(ap.tensor, ap.offset, [[0, parts], [1, n]])



def setup(k, d):
    nc = k.nc
    loaded, zeroed = k.sem("su_loaded"), k.sem("su_zeroed")
    e_done, sums = k.sem("su_e"), k.sem("su_sums")
    chain_s = k.sem("su_chain")
    with ExitStack() as ctx, nc.Block() as block:
        tl = k.sb(ctx, "su_t", [P, L])
        par = k.sb(ctx, "su_par", [P, 2, 2])
        hz = k.hz
        hf = hz[:, :, :, HALF:FPITCH]
        e = k.sb(ctx, "su_exp", [P, 2, L])
        ab = k.sb(ctx, "su_abs", [P, 2, 2, L])
        rec = k.sb(ctx, "su_rec", [P, 2, L])
        parts = (P, D1)

        @block.sync
        def _(sp):
            sp.dma_start(k.ident[:, :], d["ident"]).then_inc(k.setup_done, 16)
            sp.dma_start(tl[:, :], bcast_rows(d["times"], L)).then_inc(loaded, 16)
            for c, n in enumerate(parts):
                sp.dma_start(par[0:n, c, :], d["filter_par"][c * P:c * P + n, :]).then_inc(loaded, 16)
                sp.dma_start(hf[0:n, :, c, :],
                             d["h_param"][:, c * P:c * P + n, 0:L].rearrange("o p l -> p o l")).then_inc(loaded, 16)
            txt = d["txt"].rearrange("(j i) t d -> i t j d", i=2)
            sp.dma_start(k.h[IMG:P, :, 0, :], txt[0, 0:IMG]).then_inc(k.setup_done, 16)
            sp.dma_start(k.h[0:IMG, :, 1, :], txt[0, IMG:TXT]).then_inc(k.setup_done, 16)
            sp.dma_start(k.h[:, :, 2, :], txt[1]).then_inc(k.setup_done, 16)
            sp.wait_ge(k.setup_done, 64)

        @block.gpsimd
        def _(pool):
            nc.gpsimd.memset(hz[:, :, :, 0:HALF], 0.0).then_inc(zeroed, 1)
            pool.wait_ge(zeroed, 1)
            nc.gpsimd.memset(k.nought[:, :], 0.0).then_inc(zeroed, 1)

        @block.scalar
        def _(act):
            act.wait_ge(loaded, 80)
            act.wait_ge(chain_s, 1)
            for c, n in enumerate(parts):
                nc.scalar.activation(e[0:n, c, :], tl[0:n, :], ACT.Exp, scale=par[0:n, c, 0:1]).then_inc(e_done, 1)

        @block.tensor
        def _(pe):
            pe.wait_ge(chain_s, 1 + 4 + 4)
            for o in range(2):
                for c, n in enumerate(parts):
                    nc.tensor.matmul(k.bank[0][:, o * L:o * L + L], k.ones[0:n, :], ab[0:n, o, c, :],
                                     start=(c == 0), stop=(c == 1)).then_inc(sums, 1)

        @block.vector
        def _(dve):
            ch = Chain(dve, chain_s)
            ch.n = 0
            nc.vector.memset(k.eps[:, :], LN_EPS)
            nc.vector.memset(k.xT1[D1:D1 + 1, :], 1.0)
            ch.did(nc.vector.memset(k.ones[:, :], 1.0))
            dve.wait_ge(loaded, 80)
            dve.wait_ge(e_done, 2)
            for o in range(2):
                for c, n in enumerate(parts):
                    ch.did(nc.vector.scalar_tensor_tensor(hf[0:n, o, c, :], e[0:n, c, :], par[0:n, c, 1:2],
                                                          hf[0:n, o, c, :], ALU.add, ALU.mult))
            ch.sync()
            for o in range(2):
                for c, n in enumerate(parts):
                    ch.did(nc.vector.scalar_tensor_tensor(ab[0:n, o, c, :], hf[0:n, o, c, :], -1.0,
                                                          hf[0:n, o, c, :], ALU.mult, ALU.max))
            dve.wait_ge(sums, 4)
            for o in range(2):
                ch.did(nc.vector.reciprocal(rec[:, o, :], k.bank[0][:, o * L:o * L + L]))
            ch.sync()
            for o in range(2):
                for c, n in enumerate(parts):
                    ch.did(nc.vector.tensor_tensor(hf[0:n, o, c, :], hf[0:n, o, c, :], rec[0:n, o, :], ALU.mult))



def tokenizer(k, d):
    nc = k.nc
    S = {n: k.sem("tk_" + n) for n in (
        "consts", "stem", "bn", "leaky", "off", "tr", "pxy", "htcopy", "scr", "hx", "hy",
        "weighted", "sampcopy", "dcn", "bn2", "prep", "act_chain", "dve_chain", "sqrt", "samp_mm")}
    S["patch"], S["bc"] = ([k.sem(f"tk_{n}{u}") for u in range(2)] for n in ("patch", "bc"))
    with ExitStack() as ctx, nc.Block() as block:
        stem_w = k.sb(ctx, "tk_stem_w", [48, CS])
        off_w = k.sb(ctx, "tk_off_w", [CS, TAPS, OFFC])
        dcn_w = k.sb(ctx, "tk_dcn_w", [CS, TAPS, D])
        v96 = k.sb(ctx, "tk_v96", [CS, 5])
        v192 = k.sb(ctx, "tk_v192", [P, 5, D])
        offb = k.sb(ctx, "tk_offb", [OFFC, 1])
        grid = k.sb(ctx, "tk_grid", [OFFC, 64])
        xy = k.sb(ctx, "tk_xy", [P, 1 + YCH])
        pat = k.sb(ctx, "tk_pat", [48, 2, HW])
        pre = k.sb(ctx, "tk_pre", [CS, HW])
        h1 = k.sb(ctx, "tk_h1", [CS, HW])
        pxy = k.sb(ctx, "tk_pxy", [OFFC, 2, 64])
        pos = k.sb(ctx, "tk_pos", [P, 2, TAPS, 2, 64])
        hT = k.sb(ctx, "tk_hT", [P, 2, YCH, CS])
        hx = k.sb(ctx, "tk_hx", [P, HW])
        ab = k.sb(ctx, "tk_ab", [P, 2, HW])
        hy = k.sb(ctx, "tk_hy", [P, 2, HW])
        wt = k.sb(ctx, "tk_wt", [P, 3, HW])
        samp = k.sb(ctx, "tk_samp", [CS, TAPS, 2, 64])
        inv1, sh1 = k.sb(ctx, "tk_inv1", [CS, 1]), k.sb(ctx, "tk_sh1", [CS, 1])
        inv2, sh2 = k.sb(ctx, "tk_inv2", [P, D]), k.sb(ctx, "tk_sh2", [P, D])
        tmp2 = k.sb(ctx, "tk_tmp2", [P, D])
        ps_stem = [k.bank[0], k.bank[1]]
        ps_t = [k.bank[2], k.bank[3]]
        ps_off, ps_dcn = k.bank[4], k.bank[5]
        ps_s = [k.bank[6], k.bank[7]]
        scr = d["positions"]

        @block.sync
        def _(sp):
            for t, name in ((stem_w, "stem_w"), (off_w, "off_w"), (v96, "v96"), (offb, "off_b"), (grid, "grid"),
                            (xy, "xy"), (dcn_w, "dcn_w")):
                flat = t[:] if len(t.shape) == 2 else t[:].rearrange("p a b -> p (a b)")
                sp.dma_start(flat, d[name]).then_inc(S["consts"], 16)
            sp.dma_start(v192[:].rearrange("p a b -> p (a b)"), bcast_rows(d["v192"], 5 * D)).then_inc(S["consts"], 16)

            def load(b, u):
                sp.dma_start(pat[:, u, :], d["patches"][b]).then_inc(S["patch"][u], 16)

            def spread(b, u):
                sp.wait_ge(S["pxy"], b + 1)
                sp.dma_start(scr[b], pxy[:, u, :]).then_inc(S["scr"], 16)
                sp.wait_ge(S["scr"], b * 16 + 16)
                sp.dma_start(pos[:, u, :, :, :].rearrange("p k a s -> p (k a s)"),
                             bass.AP(scr.tensor, b * (OFFC * 64), [[0, P], [1, OFFC * 64]])).then_inc(S["bc"][u], 16)

            rows = d["queue"].rearrange("(n p r) d -> n p (r d)", p=P, r=8)
            ROWS = rows.shape[0] // B

            def clear(b):
                for n in range(ROWS):
                    sp.dma_start(rows[b * ROWS + n], k.nought[:, :]).then_inc(k.zeroed, 16)

            load(0, 0)
            load(1, 1)
            with sp.Fori(0, PAIRS - 1) as j:
                for u in range(2):
                    spread(j * 2 + u, u)
                    load(j * 2 + (2 + u), u)
                    clear(j * 2 + u)
            for u in range(2):
                spread(2 * PAIRS - 2 + u, u)
                clear(2 * PAIRS - 2 + u)

        @block.tensor
        def _(pe):
            def stem(q, u):
                b = q * 2 + u
                pe.wait_ge(S["patch"][u], q * 16 + 16)
                wait(pe, S["bn"], b)
                for n in range(2):
                    mm = nc.tensor.matmul(ps_stem[n][0:CS, :], stem_w[:, :], pat[:, u, n * 512:n * 512 + 512],
                                          start=True, stop=True)
                mm.then_inc(S["stem"], 1)

            def offsets(b, u):
                pe.wait_ge(S["leaky"], b + 1)
                wait(pe, S["pxy"], b)
                taps = h1[:, :].rearrange("c (a e b f) -> c e f a b", a=8, e=4, b=8)
                for t in range(TAPS):
                    mm = nc.tensor.matmul(ps_off[0:OFFC, 0:64], off_w[:, t, :], taps[:, t // 4, t % 4],
                                          start=(t == 0), stop=(t == TAPS - 1))
                mm.then_inc(S["off"], 1)
                wait(pe, S["htcopy"], b)
                for i in range(YCH):
                    mm = nc.tensor.transpose(ps_t[i // 4][:, i % 4 * CS:i % 4 * CS + CS], h1[:, i * P:i * P + P],
                                             k.ident[0:CS, 0:CS])
                mm.then_inc(S["tr"], 1)

            def sample(b, u):
                pe.wait_ge(S["htcopy"], b + 1)
                wait(pe, S["sampcopy"], b)
                for i in range(YCH):
                    pe.wait_ge(S["weighted"], b * YCH + (i + 1))
                    for n in range(2):
                        mm = nc.tensor.matmul(ps_s[n][0:CS, :], hT[:, u, i, :], wt[:, i % 2, n * 512:n * 512 + 512],
                                              start=(i == 0), stop=(i == YCH - 1))
                    mm.then_inc(S["samp_mm"], 1)

            def deform(j):
                pe.wait_ge(S["sampcopy"], j * 2 + 2)
                wait(pe, S["bn2"], j)
                for t in range(TAPS):
                    mm = nc.tensor.matmul(ps_dcn[:, 0:D], samp[:, t, :, :].rearrange("c u s -> c (u s)"), dcn_w[:, t, :],
                                          start=(t == 0), stop=(t == TAPS - 1))
                mm.then_inc(S["dcn"], 1)

            pe.wait_ge(S["consts"], 128)
            stem(0, 0)
            offsets(0, 0)

            def pair(j, last):
                stem(j, 1)
                offsets(j * 2 + 1, 1)
                sample(j * 2, 0)
                if not last:
                    stem(j + 1, 0)
                    offsets(j * 2 + 2, 0)
                sample(j * 2 + 1, 1)
                deform(j)

            pair(0, False)
            with pe.Fori(1, PAIRS - 1) as j:
                pair(j, False)
            pair(PAIRS - 1, True)

        @block.scalar
        def _(act):
            ch = Chain(act, S["act_chain"])
            act.wait_ge(S["consts"], 128)
            act.wait_ge(S["prep"], 2)
            ch.did(nc.scalar.activation(inv1[:, :], v96[:, 4:5], ACT.Sqrt, bias=k.eps[0:CS, :]))
            nc.scalar.activation(inv2[:, :], v192[:, 4, :], ACT.Sqrt, bias=k.eps[:, :]).then_inc(S["sqrt"], 1)
            act.wait_ge(S["prep"], 6)

            def norm(b, u):
                act.wait_ge(S["stem"], b + 1)
                wait(act, S["leaky"], b)
                for n in range(2):
                    a = nc.scalar.activation(pre[:, n * 512:n * 512 + 512], ps_stem[n][0:CS, :], ACT.Identity,
                                             bias=sh1[:, :], scale=inv1[:, :])
                a.then_inc(S["bn"], 1)

            def hats(q, u):
                b = q * 2 + u
                act.wait_ge(S["bc"][u], q * 16 + 16)
                wait(act, S["weighted"], b * YCH)
                ch.link(nc.scalar.activation(hx[:, :], pos[:, u, :, 1, :], ACT.Abs, bias=xy[:, 0:1]))
                ch.did(nc.scalar.activation(hx[:, :], hx[:, :], ACT.Relu, bias=1.0, scale=-1.0))
                for i in range(YCH):
                    ch.link(nc.scalar.activation(ab[:, i % 2, :], pos[:, u, :, 0, :], ACT.Abs,
                                                 bias=xy[:, 1 + i:2 + i]))
                    if i >= 2:
                        act.wait_ge(S["weighted"], b * YCH + (i - 1))
                    nc.scalar.activation(hy[:, i % 2, :], ab[:, i % 2, :], ACT.Relu, bias=1.0,
                                         scale=-1.0).then_inc(S["hy"], 1)

            per = 2 + YCH
            norm(0, 0)

            def pair(j, last):
                norm(j * 2 + 1, 1)
                hats(j, 0)
                if not last:
                    norm(j * 2 + 2, 0)
                hats(j, 1)

            pair(0, False)
            with act.Fori(1, PAIRS - 1) as j:
                ch.enter(j - 1, 2 * per)
                pair(j, False)
                ch.leave(PAIRS - 2)
            pair(PAIRS - 1, True)

        @block.vector
        def _(dve):
            ch = Chain(dve, S["dve_chain"])
            dve.wait_ge(S["consts"], 128)
            nc.vector.memset(tmp2[:, :], 0.0).then_inc(S["prep"], 2)
            dve.wait_ge(S["sqrt"], 1)
            for inv, sh, v, in ((inv1[:, :], sh1[:, :], [v96[:, i:i + 1] for i in range(5)]),
                                (inv2[:, :], sh2[:, :], [v192[:, i, :] for i in range(5)])):
                ch.link(nc.vector.reciprocal(inv, inv))
                ch.link(nc.vector.tensor_tensor(inv, inv, v[1], ALU.mult))
                ch.link(nc.vector.tensor_tensor(sh, v[0], v[3], ALU.subtract))
                ch.link(nc.vector.tensor_tensor(sh, sh, inv, ALU.mult))
                last = nc.vector.tensor_tensor(sh, sh, v[2], ALU.add)
                last.then_inc(S["prep"], 2)
            dve.wait_ge(S["prep"], 6)

            def leaky(b, u):
                dve.wait_ge(S["bn"], b + 1)
                nc.vector.scalar_tensor_tensor(h1[:, :], pre[:, :], 0.01, pre[:, :], ALU.mult,
                                               ALU.max).then_inc(S["leaky"], 1)

            def where(b, u):
                dve.wait_ge(S["off"], b + 1)
                nc.vector.scalar_tensor_tensor(pxy[:, u, :], ps_off[0:OFFC, 0:64], offb[:, 0:1], grid[:, :],
                                               ALU.add, ALU.add).then_inc(S["pxy"], 1)
                dve.wait_ge(S["tr"], b + 1)
                for n in range(2):
                    c = nc.vector.tensor_copy(hT[:, u, 4 * n:4 * n + 4, :].rearrange("p a c -> p (a c)"),
                                              ps_t[n][:, 0:4 * CS])
                c.then_inc(S["htcopy"], 1)

            def weights(b, u):
                for i in range(YCH):
                    dve.wait_ge(S["hy"], b * YCH + (i + 1))
                    if i >= 2:
                        dve.wait_ge(S["samp_mm"], b * YCH + (i - 1))
                    else:
                        wait(dve, S["samp_mm"], b * YCH + (i - 1) if isinstance(b, int) else b * YCH + (i - 1))
                    nc.vector.tensor_tensor(wt[:, i % 2, :], hy[:, i % 2, :], hx[:, :],
                                            ALU.mult).then_inc(S["weighted"], 1)
                dve.wait_ge(S["samp_mm"], b * YCH + YCH)
                for n in range(2):
                    c = nc.vector.tensor_copy(samp[:, 8 * n:8 * n + 8, u, :],
                                              ps_s[n][0:CS, :].rearrange("c (t s) -> c t s", t=8))
                c.then_inc(S["sampcopy"], 1)

            def norm2(j):
                dve.wait_ge(S["dcn"], j + 1)
                ch.link(nc.vector.tensor_tensor(tmp2[:, :], ps_dcn[:, 0:D], inv2[:, :], ALU.mult))
                ch.link(nc.vector.tensor_tensor(tmp2[:, :], tmp2[:, :], sh2[:, :], ALU.add))
                for t, lo in ((0, 0), (1, IMG)):
                    o = nc.vector.scalar_tensor_tensor(k.h[lo:lo + IMG, j, t, :], tmp2[lo:lo + IMG, :], 0.01,
                                                       tmp2[lo:lo + IMG, :], ALU.mult, ALU.max)
                o.then_inc(S["bn2"], 1)

            leaky(0, 0)
            where(0, 0)

            def pair(j, last):
                leaky(j * 2 + 1, 1)
                where(j * 2 + 1, 1)
                weights(j * 2, 0)
                if not last:
                    leaky(j * 2 + 2, 0)
                    where(j * 2 + 2, 0)
                weights(j * 2 + 1, 1)
                norm2(j)

            pair(0, False)
            with dve.Fori(1, PAIRS - 1) as j:
                ch.enter(j - 1, 2)
                pair(j, False)
                ch.leave(PAIRS - 2)
            pair(PAIRS - 1, True)



def norm(k, name, d, src, affine=None):
    nc = k.nc
    S = {n: k.sem(f"{name}_{n}") for n in ("vars", "rstd", "inv", "normed", "turned", "x0", "x1", "chain", "rows")}
    with ExitStack() as ctx, nc.Block() as block:
        st = k.sb(ctx, name + "_st", [P, PAIRS, 3, 6])
        mv = k.sb(ctx, name + "_mv", [P, 3, PAIRS, 3])
        rs = k.sb(ctx, name + "_rs", [P, PAIRS, 3])
        gb = k.sb(ctx, name + "_gb", [P, 2, D]) if affine else None
        xn = k.xn

        if affine:
            @block.sync
            def _(sp):
                sp.dma_start(gb[:, :, :].rearrange("p a d -> p (a d)"),
                             bcast_rows(d[affine], 2 * D)).then_inc(S["rows"], 16)
                sp.wait_ge(S["rows"], 16)

        @block.scalar
        def _(act):
            act.wait_ge(S["vars"], 1)
            nc.scalar.activation(rs[:, :, :], mv[:, 1], ACT.Sqrt, bias=k.eps[:, :]).then_inc(S["rstd"], 1)
            def copy(j, u):
                act.wait_ge(S["turned"], j + 1)
                nc.scalar.activation(k.xT0[:, bass.ds(j * PC, PC)], k.bank[2 * u][:, 0:PC],
                                     ACT.Copy).then_inc(S["x0"], 1)

            with act.Fori(0, PAIRS // 2) as q:
                copy(q * 2, 0)
                copy(q * 2 + 1, 1)

        @block.tensor
        def _(pe):
            def turn(j, u, first):
                pe.wait_ge(S["normed"], j + 1)
                if not first:
                    pe.wait_ge(S["x0"], j - 1)
                    pe.wait_ge(S["x1"], j - 1)
                for t in range(3):
                    nc.tensor.transpose(k.bank[2 * u][:, t * P:t * P + P], xn[:, j, t, 0:P], k.ident[:, :])
                    mm = nc.tensor.transpose(k.bank[2 * u + 1][0:D1, t * P:t * P + P], xn[:, j, t, P:D],
                                             k.ident[:, :])
                mm.then_inc(S["turned"], 1)

            for j in range(PAIRS):
                turn(j, j % 2, j < 2)

        @block.vector
        def _(dve):
            ch = Chain(dve, S["chain"])
            with dve.Fori(0, PAIRS) as j:
                ch.enter(j, 3)
                for t in range(3):
                    ch.did(nc.vector.bn_stats(st[:, j, t, :], src[:, j, t, :]))
                ch.leave(PAIRS)
            ch.sync()
            half = float(D // 2)
            ch.did(nc.vector.tensor_tensor(mv[:, 0], st[:, :, :, 1], st[:, :, :, 4], ALU.add))
            ch.did(nc.vector.tensor_tensor(mv[:, 1], st[:, :, :, 1], st[:, :, :, 4], ALU.subtract))
            ch.did(nc.vector.tensor_tensor(mv[:, 2], st[:, :, :, 2], st[:, :, :, 5], ALU.add))
            ch.sync()
            ch.did(nc.vector.tensor_scalar(mv[:, 0], mv[:, 0], 0.5, None, ALU.mult))
            ch.link(nc.vector.scalar_tensor_tensor(mv[:, 1], mv[:, 1], 0.25, mv[:, 1], ALU.mult, ALU.mult))
            nc.vector.scalar_tensor_tensor(mv[:, 1], mv[:, 2], 0.5 / half, mv[:, 1], ALU.mult,
                                           ALU.add).then_inc(S["vars"], 1)
            dve.wait_ge(S["rstd"], 1)
            if affine:
                dve.wait_ge(S["rows"], 16)
            nc.vector.reciprocal(rs[:, :, :], rs[:, :, :]).then_inc(S["inv"], 1)
            dve.wait_ge(S["inv"], 1)

            def scale(j):
                for t in range(3):
                    ins = nc.vector.tensor_scalar(xn[:, j, t, :], src[:, j, t, :], mv[:, 0, j, t:t + 1], rs[:, j, t:t + 1],
                                                  ALU.subtract, ALU.mult)
                    if affine:
                        ch.did(ins)
                if affine:
                    ch.sync()
                    for t in range(3):
                        ch.did(nc.vector.tensor_tensor(xn[:, j, t, :], xn[:, j, t, :], gb[:, 0, :], ALU.mult))
                    ch.sync()
                    for t in range(3):
                        ins = nc.vector.tensor_tensor(xn[:, j, t, :], xn[:, j, t, :], gb[:, 1, :], ALU.add)
                ins.then_inc(S["normed"], 1)

            def copy(j, u):
                dve.wait_ge(S["turned"], j + 1)
                nc.vector.tensor_copy(k.xT1[0:D1, bass.ds(j * PC, PC)],
                                      k.bank[2 * u + 1][0:D1, 0:PC]).then_inc(S["x1"], 1)

            with dve.Fori(0, PAIRS // 2) as q:
                ch.enter(q, 12 if affine else 0)
                scale(q * 2)
                scale(q * 2 + 1)
                copy(q * 2, 0)
                copy(q * 2 + 1, 1)
                ch.leave(PAIRS // 2)



def retention(k, d):
    nc = k.nc
    S = {n: k.sem("re_" + n) for n in ("loaded", "proj", "qk", "v", "scores", "decayed", "out", "added")}
    with ExitStack() as ctx, nc.Block() as block:
        w0, w1 = k.sb(ctx, "re_w0", [P, 3 * D]), k.sb(ctx, "re_w1", [D1 + 1, 3 * D])
        decay = k.sb(ctx, "re_decay", [P, 2, PC])
        qk = k.sb(ctx, "re_qk", [P, 4, PC])
        v = k.sb(ctx, "re_v", [P, 2, 3, D])
        pt = k.sb(ctx, "re_pt", [P, 2, PC])
        Q0, Q1, K0, K1, V0, V1, R0, R1 = k.bank

        @block.sync
        def _(sp):
            sp.dma_start(w0[:, :], d["qkv"][0:P, :]).then_inc(S["loaded"], 16)
            sp.dma_start(w1[:, :], d["qkv"][P:D + 1, :]).then_inc(S["loaded"], 16)
            sp.dma_start(decay[:, :, :].rearrange("p a b -> p (a b)"), d["decay"]).then_inc(S["loaded"], 16)
            for o in range(2):
                for c, n in enumerate((P, D1)):
                    sp.dma_start(d["filters"][o, c * P:c * P + n, :, :],
                                 k.hz[0:n, o, c, :].unsqueeze(1).broadcast_to([n, FC, FPITCH])
                                 ).then_inc(k.filters_stored, 16)
            sp.wait_ge(S["loaded"], 48)

        @block.tensor
        def _(pe):
            def project(j):
                c = j * PC
                x0, x1 = k.xT0[:, bass.ds(c, PC)], k.xT1[0:D1 + 1, bass.ds(c, PC)]
                for n, (ps, at) in enumerate(((Q0, 0), (Q1, P), (K0, D), (K1, D + P))):
                    m = P if n % 2 == 0 else D1
                    nc.tensor.matmul(ps[0:m, 0:PC], w0[:, at:at + m], x0, start=True, stop=False)
                    nc.tensor.matmul(ps[0:m, 0:PC], w1[:, at:at + m], x1, start=False, stop=True)
                for t in range(3):
                    ps = V0[:, t * D:t * D + D] if t < 2 else V1[:, 0:D]
                    nc.tensor.matmul(ps, k.xT0[:, bass.ds(c + t * P, P)], w0[:, 2 * D:], start=True, stop=False)
                    mm = nc.tensor.matmul(ps, k.xT1[0:D1 + 1, bass.ds(c + t * P, P)], w1[:, 2 * D:],
                                          start=False, stop=True)
                mm.then_inc(S["proj"], 1)

            def scores(j):
                pe.wait_ge(S["qk"], j + 1)
                wait(pe, S["added"], j)
                for e, keys, m, lo, at, q0, q1 in ((0, 0, P, 0, 0, 0, L), (0, P, 64, 0, L, P, L),
                                                   (1, L, 64, 64, L, L, PC), (1, L + 64, P, 0, 0, L + 64, PC)):
                    ps = (R0, R1)[e][lo:lo + m, at + q0 - e * L:at + q1 - e * L]
                    for n, r in enumerate((P, D1)):
                        mm = nc.tensor.matmul(ps, qk[0:r, 2 + n, keys:keys + m], qk[0:r, n, q0:q1],
                                              start=(n == 0), stop=(n == 1))
                mm.then_inc(S["scores"], 1)

            def mix(j, u):
                pe.wait_ge(S["decayed"], j + 1)
                big0, big2 = pt[:, 0, 0:L], pt[:, 1, 0:L]
                small0, small2 = pt[0:64, 0, L:PC], pt[64:P, 1, L:PC]
                nc.tensor.matmul(R0[:, 0:D], big0[:, 0:P], v[:, u, 0, :], start=True, stop=True)
                nc.tensor.matmul(R1[:, 0:D], big2[:, 64:L], v[:, u, 2, :], start=True, stop=False)
                nc.tensor.matmul(R1[:, 0:D], small2[:, 64:L], v[64:P, u, 1, :], start=False, stop=True)
                nc.tensor.matmul(R0[0:64, D:2 * D], big0[:, P:L], v[:, u, 0, :], start=True, stop=False)
                nc.tensor.matmul(R0[0:64, D:2 * D], small0[:, P:L], v[0:64, u, 1, :], start=False, stop=True)
                nc.tensor.matmul(R0[64:P, D:2 * D], small2[:, 0:64], v[64:P, u, 1, :], start=True,
                                 stop=True).then_inc(S["out"], 1)

            def step(j, u, last=False):
                scores(j)
                if not last:
                    pe.wait_ge(S["v"], j + 1)
                    project(j + 1)
                mix(j, u)

            pe.wait_ge(S["loaded"], 48)
            project(0)
            for j in range(PAIRS):
                step(j, j % 2, j == PAIRS - 1)

        @block.scalar
        def _(act):
            with act.Fori(0, PAIRS) as j:
                act.wait_ge(S["proj"], j + 1)
                for n, ps in enumerate((Q0, Q1, K0, K1)):
                    m = P if n % 2 == 0 else D1
                    a = nc.scalar.activation(qk[0:m, n, :], ps[0:m, 0:PC], ACT.Copy)
                a.then_inc(S["qk"], 1)

        @block.vector
        def _(dve):
            def values(j, u):
                dve.wait_ge(S["proj"], j + 1)
                nc.vector.tensor_copy(v[:, u, 0:2, :].rearrange("p a d -> p (a d)"), V0[:, 0:2 * D])
                nc.vector.tensor_copy(v[:, u, 2, :], V1[:, 0:D]).then_inc(S["v"], 1)

            def step(j, u, last=False):
                dve.wait_ge(S["scores"], j + 1)
                for e, ps, lo, hi, c0, c1 in ((0, R0, 0, P, 0, L), (0, R0, 0, 64, L + P, PC),
                                              (1, R1, 0, P, 64, L), (1, R1, 64, P, L, PC)):
                    o = nc.vector.tensor_tensor(pt[lo:hi, e, c0:c1], ps[lo:hi, c0:c1], decay[lo:hi, e, c0:c1], ALU.mult)
                o.then_inc(S["decayed"], 1)
                if not last:
                    values(j + 1, 1 - u)
                dve.wait_ge(S["out"], j + 1)
                nc.vector.tensor_tensor(k.h[:, j, 0:2, :].rearrange("p a d -> p (a d)"), R0[:, 0:2 * D],
                                        k.h[:, j, 0:2, :].rearrange("p a d -> p (a d)"), ALU.add)
                nc.vector.tensor_tensor(k.h[:, j, 2, :], R1[:, 0:D], k.h[:, j, 2, :], ALU.add).then_inc(S["added"], 1)

            values(0, 0)
            step(0, 0)
            step(1, 1)
            with dve.Fori(1, PAIRS // 2 - 1) as q:
                step(q * 2, 0)
                step(q * 2 + 1, 1)
            step(PAIRS - 2, 0)
            step(PAIRS - 1, 1, True)



def norm_a(k, d):
    norm(k, "na", d, k.h)


def norm_b(k, d):
    norm(k, "nb", d, k.h)



def choose(nc, ch, x, rank, c, chosen, kept):
    n = x.shape[-1]
    for i in range(n):
        ch.did(nc.vector.memset(rank[:, :, i:i + 1], float(n - 1 - i)))
    ch.sync()
    for step in range(1, n):
        m = n - step
        ch.link(nc.vector.tensor_tensor(c[:, :, 0:m], x[:, :, 0:m], x[:, :, step:n], ALU.is_ge))
        ch.link(nc.vector.tensor_tensor(rank[:, :, step:n], rank[:, :, step:n], c[:, :, 0:m], ALU.add))
        ch.link(nc.vector.tensor_tensor(rank[:, :, 0:m], rank[:, :, 0:m], c[:, :, 0:m], ALU.subtract))
    ch.link(nc.vector.tensor_scalar(chosen, rank, kept - 0.5, None, ALU.is_lt))


def over(ap, n):
    return ap.unsqueeze(2).broadcast_to([ap.shape[0], ap.shape[1], n])


def gates(k, d, name, groups, experts, combine, weight, chosen=None):
    nc = k.nc
    tiles = PAIRS * 3
    nx = groups * experts
    cols = nx + (groups if groups > 1 else 0)
    S = {n: k.sem(f"{name}_{n}") for n in ("loaded", "logits", "shift", "exp", "chain")}
    with ExitStack() as ctx, nc.Block() as block:
        w0, w1 = k.sb(ctx, name + "_w0", [P, cols]), k.sb(ctx, name + "_w1", [D1 + 1, cols])
        lg = k.sb(ctx, name + "_lg", [P, tiles, cols])
        n_all = tiles * groups
        xs = [(k.sb(ctx, name + "_xe", [P, n_all, experts]), n_all, experts, 4 if groups > 1 else 2)]
        if groups > 1:
            xs.append((k.sb(ctx, name + "_xg", [P, tiles, groups]), tiles, groups, 2))
        most = [k.sb(ctx, f"{name}_most{i}", [P, n]) for i, (_, n, _, _) in enumerate(xs)]
        rank = k.sb(ctx, name + "_rank", [P, n_all, experts])
        c = k.sb(ctx, name + "_c", [P, n_all, experts])
        sel = [k.sb(ctx, f"{name}_sel{i}", [P, n, m]) for i, (_, n, m, _) in enumerate(xs)]
        tpb = 12

        @block.sync
        def _(sp):
            sp.dma_start(w0[:, :], d[weight][0:P, :]).then_inc(S["loaded"], 16)
            sp.dma_start(w1[:, :], d[weight][P:D + 1, :]).then_inc(S["loaded"], 16)
            sp.wait_ge(S["loaded"], 32)

        @block.tensor
        def _(pe):
            pe.wait_ge(S["loaded"], 32)
            for t in range(tiles):
                ps = k.bank[t // tpb][:, t % tpb * cols:t % tpb * cols + cols]
                nc.tensor.matmul(ps, k.xT0[:, t * P:t * P + P], w0[:, :], start=True, stop=False)
                mm = nc.tensor.matmul(ps, k.xT1[0:D1 + 1, t * P:t * P + P], w1[:, :], start=False, stop=True)
            mm.then_inc(S["logits"], 1)

        @block.scalar
        def _(act):
            act.wait_ge(S["shift"], 1)
            for x, _, _, _ in xs:
                a = nc.scalar.activation(x[:, :, :], x[:, :, :], ACT.Exp)
            a.then_inc(S["exp"], 1)

        @block.vector
        def _(dve):
            ch = Chain(dve, S["chain"])
            dve.wait_ge(S["logits"], 1)
            for i in range(tiles // tpb):
                ch.did(nc.vector.tensor_copy(lg[:, i * tpb:i * tpb + tpb, :].rearrange("p a c -> p (a c)"),
                                             k.bank[i][:, 0:tpb * cols]))
            ch.sync()
            if groups > 1:
                ch.did(nc.vector.tensor_copy(xs[1][0][:, :, :], lg[:, :, 0:groups]))
                ch.link(nc.vector.tensor_copy(xs[0][0][:, :, :].rearrange("p (t g) e -> p t (g e)", g=groups),
                                              lg[:, :, groups:cols]))
            else:
                ch.link(nc.vector.tensor_copy(xs[0][0][:, :, :], lg[:, :, :]))
            for i, (x, n, m, kept) in enumerate(xs):
                choose(nc, ch, x[:, :, :], rank[:, 0:n, 0:m], c[:, 0:n, 0:m], sel[i][:, :, :], kept)
                ch.link(nc.vector.tensor_reduce(most[i][:, :], x[:, :, :], AX.X, ALU.max))
                s = nc.vector.tensor_tensor(x[:, :, :], x[:, :, :], over(most[i][:, :], m), ALU.subtract)
            s.then_inc(S["shift"], 1)
            if chosen is not None:
                ch.did(nc.vector.tensor_tensor(
                    chosen[:, :, :].rearrange("p t (g e) -> p (t g) e", g=groups), sel[0][:, :, :],
                    over(sel[1][:, :, :].rearrange("p t g -> p (t g)"), experts), ALU.mult))
                ch.sync()
            dve.wait_ge(S["exp"], 1)
            for i, (x, n, m, _) in enumerate(xs):
                if groups > 1:
                    ch.link(nc.vector.tensor_tensor(x[:, :, :], x[:, :, :], sel[i][:, :, :], ALU.mult))
                ch.link(nc.vector.tensor_reduce(most[i][:, :], x[:, :, :], AX.X, ALU.add))
                ch.link(nc.vector.reciprocal(most[i][:, :], most[i][:, :]))
                ch.link(nc.vector.tensor_tensor(x[:, :, :], x[:, :, :], over(most[i][:, :], m), ALU.mult))
                if groups > 1:
                    ch.link(nc.vector.tensor_scalar(sel[i][:, :, :], x[:, :, :], 1e-6, None, ALU.is_ge))
                    ch.link(nc.vector.tensor_tensor(x[:, :, :], x[:, :, :], sel[i][:, :, :], ALU.mult))
            if groups > 1:
                ch.link(nc.vector.tensor_tensor(
                    combine[:, :, :].rearrange("p t (g e) -> p (t g) e", g=groups), xs[0][0][:, :, :],
                    over(xs[1][0][:, :, :].rearrange("p t g -> p (t g)"), experts), ALU.mult))
            else:
                ch.link(nc.vector.tensor_tensor(combine[:, :, :], xs[0][0][:, :, :], sel[0][:, :, :], ALU.mult))



def bias_parts(k, d, ctx, name, nx, combine, acc, b2n):
    nc = k.nc
    S = {n: k.sem(f"{name}_{n}") for n in ("b2", "ct", "ctcopy", "bias", "added")}
    b2 = k.sb(ctx, name + "_b2", [nx, D])
    cT = k.sb(ctx, name + "_cT", [nx, 2, 3 * P])

    def sync(sp):
        sp.dma_start(b2[:, :], d[b2n]).then_inc(S["b2"], 16)

    def tensor(pe):
        pe.wait_ge(S["b2"], 16)
        for j in range(PAIRS):
            u = j % 2
            if j >= 2:
                pe.wait_ge(S["ctcopy"], j - 1)
            for t in range(3):
                mm = nc.tensor.transpose(k.bank[6 + u][0:nx, t * P:t * P + P], combine[:, j * 3 + t, :],
                                         k.ident[:, :])
            mm.then_inc(S["ct"], 1)
            pe.wait_ge(S["ctcopy"], j + 1)
            if j:
                pe.wait_ge(S["added"], j)
            for t in range(3):
                mm = nc.tensor.matmul(k.bank[3 + t][:, 0:D], cT[:, u, t * P:t * P + P], b2[:, :],
                                      start=True, stop=True)
            mm.then_inc(S["bias"], 1)
        pe.wait_ge(S["added"], PAIRS)

    def vector(dve):
        for j in range(PAIRS):
            dve.wait_ge(S["ct"], j + 1)
            nc.vector.tensor_copy(cT[:, j % 2, :], k.bank[6 + j % 2][0:nx, 0:PC]).then_inc(S["ctcopy"], 1)
            dve.wait_ge(S["bias"], j + 1)
            for t in range(3):
                a = nc.vector.tensor_tensor(acc[:, j, t, :], k.bank[3 + t][:, 0:D], acc[:, j, t, :], ALU.add)
            a.then_inc(S["added"], 1)
        dve.wait_ge(S["added"], PAIRS)

    return sync, tensor, vector


def bias(k, d, name, nx, combine, acc, b2n):
    with ExitStack() as ctx, k.nc.Block() as block:
        sync, tensor, vector = bias_parts(k, d, ctx, name, nx, combine, acc, b2n)
        block.sync(sync)
        block.tensor(tensor)
        block.vector(vector)




UNIT = 2 * P
TILES = PAIRS * 3
KEPT = 8
UNITS = (TILES * P * KEPT - NX0) // UNIT + NX0
UNITS += UNITS % 2


def slots(k, d, chosen, key, top, index, expert_of):
    nc = k.nc
    S = {n: k.sem("sl_" + n) for n in ("loaded", "sums", "chain")}
    NB = TILES * NX0 // 2
    with ExitStack() as ctx, nc.Block() as block:
        before = k.sb(ctx, "sl_before", [P, P])
        number = k.sb(ctx, "sl_number", [1, UNITS])
        tot = k.sb(ctx, "sl_tot", [P, TILES, NX0])
        run = k.sb(ctx, "sl_run", [P, TILES + 1, NX0])
        whole = k.sb(ctx, "sl_whole", [P, NX0], mybir.dt.int32)
        ends = k.sb(ctx, "sl_ends", [P, 2, NX0])
        past = k.sb(ctx, "sl_past", [1, UNITS, NX0])
        exp = k.sb(ctx, "sl_exp", [1, UNITS])

        @block.sync
        def _(sp):
            sp.dma_start(before[:, :], d["before"]).then_inc(S["loaded"], 16)
            sp.dma_start(number[:, :], d["unit_numbers"]).then_inc(S["loaded"], 16)
            sp.wait_ge(S["loaded"], 32)

        @block.tensor
        def _(pe):
            pe.wait_ge(S["loaded"], 32)
            flat = chosen[:, :, :].rearrange("p t e -> p (t e)")
            for i in range(2):
                nc.tensor.matmul(k.bank[i][:, 0:NB], before[:, :], flat[:, i * NB:i * NB + NB], start=True, stop=True)
                mm = nc.tensor.matmul(k.bank[2 + i][:, 0:NB], k.ones[:, :], flat[:, i * NB:i * NB + NB],
                                      start=True, stop=True)
            mm.then_inc(S["sums"], 1)

        @block.vector
        def _(dve):
            ch = Chain(dve, S["chain"])
            ch.did(nc.vector.memset(run[:, 0, :], 0.0))
            dve.wait_ge(S["sums"], 1)
            for i in range(2):
                half = slice(i * TILES // 2, (i + 1) * TILES // 2)
                ch.did(nc.vector.tensor_copy(key[:, half, :].rearrange("p t e -> p (t e)"), k.bank[i][:, 0:NB]))
                ch.did(nc.vector.tensor_copy(tot[:, half, :].rearrange("p t e -> p (t e)"), k.bank[2 + i][:, 0:NB]))
            ch.sync()
            for t in range(TILES):
                ch.link(nc.vector.tensor_tensor(run[:, t + 1, :], run[:, t, :], tot[:, t, :], ALU.add))
            ch.link(nc.vector.tensor_scalar(ends[:, 0, :], run[:, TILES, :], float(UNIT - 1), None, ALU.add))
            ch.link(nc.vector.tensor_copy(whole[:, :], ends[:, 0, :]))
            ch.link(nc.vector.tensor_scalar(whole[:, :], whole[:, :], UNIT.bit_length() - 1, None,
                                            ALU.arith_shift_right))
            ch.link(nc.vector.tensor_copy(ends[:, 0, :], whole[:, :]))
            a, step = 0, 1
            while step < NX0:
                ch.did(nc.vector.tensor_copy(ends[:, 1 - a, 0:step], ends[:, a, 0:step]))
                ch.link(nc.vector.tensor_tensor(ends[:, 1 - a, step:NX0], ends[:, a, step:NX0],
                                                ends[:, a, 0:NX0 - step], ALU.add))
                a, step = 1 - a, 2 * step
            ch.did(nc.vector.tensor_tensor(key[:, :, :], key[:, :, :], run[:, 0:TILES, :], ALU.add))
            ch.link(nc.vector.tensor_scalar(ends[:, 1 - a, 1:NX0], ends[:, a, 0:NX0 - 1], float(UNIT), 1.0,
                                            ALU.mult, ALU.add))
            ch.link(nc.vector.memset(ends[:, 1 - a, 0:1], 1.0))
            ch.link(nc.vector.tensor_tensor(key[:, :, :], key[:, :, :],
                                            ends[:, 1 - a, :].unsqueeze(1).broadcast_to([P, TILES, NX0]), ALU.add))
            ch.link(nc.vector.tensor_tensor(key[:, :, :], key[:, :, :], chosen[:, :, :], ALU.mult))
            for t in range(TILES):
                ch.did(nc.vector.max(top[:, t, :], key[:, t, :]))
            ch.sync()
            ch.did(nc.vector.tensor_scalar(index[:, :, :], top[:, :, :], -1.0, None, ALU.add))
            ch.link(nc.vector.tensor_tensor(past[:, :, :], ends[0:1, a, :].unsqueeze(1).broadcast_to([1, UNITS, NX0]),
                                            over(number[:, :], NX0), ALU.is_le))
            ch.link(nc.vector.tensor_reduce(exp[:, :], past[:, :, :], AX.X, ALU.add))
            ch.link(nc.vector.tensor_scalar(expert_of[:, :], exp[:, :], float(NX0 - 1), None, ALU.min))


def routed(k, d, combine, key, top, index, expert_of):
    nc = k.nc
    S = {n: k.sem("ro_" + n) for n in ("sent", "twice", "turned", "x_hi", "x", "up", "act", "h_hi", "h_lo", "down",
                                       "y", "half", "added", "chain", "var", "rstd",
                                       "normed", "t_turned", "x0", "x1", "wa_hi", "wa_lo", "wb_hi", "wb_lo", "wc_hi", "wc_lo")}
    w1_in, w2_in, b_in, x_in, y_out = ([k.sem(f"ro_{n}{v}") for v in range(2)]
                                       for n in ("w1", "w2", "b", "xin", "yout"))
    BACK = 2 * KEPT
    got = [k.sem(f"ro_got{i}") for i in range(BACK)]
    queue, answers = d["queue"], d["answers"]
    UP_BANKS, TURN_BANK, DOWN_BANK = 3, 3, 4
    HP, WP = MC // 2, 3
    with ExitStack() as ctx, nc.Block() as block:
        wa = k.sb(ctx, "ro_wa", [P, 2, FF])
        wb = k.sb(ctx, "ro_wb", [P, 2, FF])
        wc = k.sb(ctx, "ro_wc", [P, 2, MC, D])
        b1 = k.sb(ctx, "ro_b1", [P, 2, MC])
        wa_hi, wa_lo = k.sb(ctx, "ro_wa_hi", [P, 2, FF], F32R), k.sb(ctx, "ro_wa_lo", [P, 2, FF], F32R)
        wb_hl = k.sb(ctx, "ro_wb_hl", [P, 2, FF], F32R)
        xq = k.sb(ctx, "ro_xq", [P, 2, 2, 2 * P])
        ga_hi, ga_lo = k.sb(ctx, "ro_ga_hi", [P, UNIT], F32R), k.sb(ctx, "ro_ga_lo", [P, UNIT], F32R)
        gb_hi, gb_lo = k.sb(ctx, "ro_gb_hi", [P, UNIT], F32R), k.sb(ctx, "ro_gb_lo", [D1, UNIT], F32R)
        wc_hl = k.sb(ctx, "ro_wc_hl", [P, 2, MC, 2, D], F32R)
        hT = k.sb(ctx, "ro_hT", [P, MC, UNIT])
        h_hi, h_lo = k.sb(ctx, "ro_h_hi", [P, 2, MC, UNIT], F32R), k.sb(ctx, "ro_h_lo", [P, 2, MC, UNIT], F32R)
        y = k.sb(ctx, "ro_y", [P, 2, 2, D])
        back = k.sb(ctx, "ro_back", [P, BACK, D])
        st, mv = k.sb(ctx, "ro_st", [P, PAIRS, 3, 6]), k.sb(ctx, "ro_mv", [P, 4, PAIRS, 3])
        share, hit = k.sb(ctx, "ro_share", [P, TILES, KEPT]), k.sb(ctx, "ro_hit", [P, TILES, NX0])
        bias_sync, bias_tensor, bias_vector = bias_parts(k, d, ctx, "b0", NX0, combine, k.h, "b2_0")
        tile = k.h[:].rearrange("p j t d -> p (j t) d")
        xt = k.xn[:].rearrange("p j t d -> p (j t) d")

        def unit(q, v, ahead):
            q, v = q + (v + ahead) // 2, (v + ahead) % 2
            t = q * 2 + v
            return None if isinstance(t, int) and not 0 <= t < UNITS else (t, v, q)

        def steps(eng, step):
            for t in range(-4, 4):
                step(t // 2, t % 2)
            with eng.Fori(2, UNITS // 2 - 2) as q:
                for v in range(2):
                    step(q, v)
            for t in range(UNITS - 4, UNITS + 1):
                step(t // 2, t % 2)

        @block.gpsimd
        def _(pool):
            pool.wait_ge(k.zeroed, UNITS * UNIT // (8 * P) * 16)
            for t in range(TILES):
                for i in range(KEPT):
                    nc.gpsimd.indirect_dma_start(
                        out=queue, out_offset=bass.IndirectOffsetOnAxis(ap=index[:, t, i:i + 1], axis=0),
                        in_=xt[:, t, :], in_offset=None).then_inc(S["sent"], 16)

            def step(q, v):
                if u := unit(q, v, 2):
                    t, w, n = u
                    pool.wait_ge(S["wb_hi"], t + 1)
                    nc.gpsimd.tensor_tensor(wb_hl[D1:P, w, :], wb[D1:P, w, :], wb_hl[D1:P, w, :].bitcast(F32),
                                            ALU.subtract).then_inc(S["wb_lo"], 1)
                    pool.wait_ge(S["wb_lo"], t + 1)
                if u := unit(q, v, 3):
                    t, w, n = u
                    pool.wait_ge(x_in[w], n * 16 + 16)
                    nc.gpsimd.tensor_tensor(xq[:, w, :, D:2 * P], xq[:, w, :, P:D],
                                            k.nought[:, 0:P].rearrange("p (i c) -> p i c", i=2), ALU.subtract).then_inc(S["twice"], 1)
                    pool.wait_ge(S["twice"], t + 1)

                if u := unit(q, v, 1):
                    t, w, n = u
                    pool.wait_ge(S["wc_hi"], t * WP + WP)
                    nc.gpsimd.tensor_tensor(wc_hl[:, w, :, 1, :], wc[:, w, :, :], wc_hl[:, w, :, 0, :].bitcast(F32),
                                            ALU.subtract).then_inc(S["wc_lo"], 1)
                    pool.wait_ge(S["wc_lo"], t + 1)

            steps(pool, step)
            for v in range(2):
                pool.wait_ge(y_out[v], UNITS // 2 * 16)
            for t in range(TILES):
                for i in range(KEPT):
                    n = t * KEPT + i
                    wait(pool, S["added"], n - BACK + 1)
                    nc.gpsimd.indirect_dma_start(
                        out=back[:, n % BACK, :], out_offset=None, in_=answers,
                        in_offset=bass.IndirectOffsetOnAxis(ap=index[:, t, i:i + 1], axis=0)).then_inc(got[n % BACK], 16)

        @block.sync
        def _(sp):
            def expert(t):
                return sp.value_load(expert_of[0:1, bass.ds(t, 1)], min_val=0, max_val=NX0 - 1)

            def step(q, v):
                if u := unit(q, v, 4):
                    t, w, n = u
                    e = expert(t)
                    wait(sp, S["wa_lo"], t - 1)
                    wait(sp, S["wb_lo"], t - 1)
                    sp.dma_start(wa[:, w, :], d["w1_0"][e, 0:P, :]).then_inc(w1_in[w], 16)
                    for r in (0, D1):
                        sp.dma_start(wb[r:r + D1, w, :], d["w1_0"][e, P:D, :]).then_inc(w1_in[w], 16)
                if u := unit(q, v, 4):
                    t, w, n = u
                    wait(sp, S["turned"], t - 1)
                    if isinstance(t, int) and t == 0:
                        sp.wait_ge(S["sent"], TILES * KEPT * 16)
                    sp.dma_start(xq[:, w, :, 0:D],
                                 queue[bass.ds(t * UNIT, UNIT), :].rearrange("(i p) d -> p i d", p=P)
                                 ).then_inc(x_in[w], 16)
                if u := unit(q, v, -1):
                    t, w, n = u
                    sp.wait_ge(S["y"], t + 1)
                    sp.dma_start(answers[bass.ds(t * UNIT, UNIT), :].rearrange("(i p) d -> p i d", p=P),
                                 y[:, w, :, :]).then_inc(y_out[w], 16)
                if u := unit(q, v, 3):
                    t, w, n = u
                    e = expert(t)
                    wait(sp, S["act"], (t - 1) * MC)
                    sp.dma_start(b1[:, w, :], d["b1_0"][e]).then_inc(b_in[w], 16)
                if u := unit(q, v, 3):
                    t, w, n = u
                    e = expert(t)
                    wait(sp, S["wc_lo"], t - 1)
                    sp.dma_start(wc[:, w, :, :].rearrange("p m d -> p (m d)"), d["w2_0"][e]).then_inc(w2_in[w], 16)

            bias_sync(sp)
            sp.wait_ge(k.filters_stored, 64)
            steps(sp, step)

        @block.tensor
        def _(pe):
            def step(q, v):
                if u := unit(q, v, 1):
                    t, w, n = u
                    pe.wait_ge(S["wa_hi"], t + 1)
                    pe.wait_ge(S["wa_lo"], t + 1)
                    pe.wait_ge(S["wb_lo"], t + 1)
                    pe.wait_ge(S["x"], t + 1)
                    for m in range(MC):
                        ps = k.bank[(w * MC + m) % UP_BANKS][:, 0:UNIT]
                        c = slice(m * P, m * P + P)
                        wait(pe, S["act"], t * MC + (m + 1 - UP_BANKS))
                        nc.tensor.matmul(ps, wa_hi[:, w, c], ga_hi[:, :], start=True, stop=False)
                        nc.tensor.matmul(ps, wa_hi[:, w, c], ga_lo[:, :], start=False, stop=False)
                        nc.tensor.matmul(ps, wa_lo[:, w, c], ga_hi[:, :], start=False, stop=False)
                        nc.tensor.matmul(ps, wb_hl[:, w, c], gb_hi[:, :], start=False, stop=False)
                        nc.tensor.matmul(ps, wb_hl[0:D1, w, c], gb_lo[:, :], start=False,
                                         stop=True).then_inc(S["up"], 1)
                if u := unit(q, v, 2):
                    t, w, n = u
                    pe.wait_ge(S["twice"], t + 1)
                    for i in range(2):
                        for c in range(2):
                            mm = nc.tensor.transpose(k.bank[TURN_BANK][:, c * UNIT + i * P:c * UNIT + i * P + P],
                                                     xq[:, w, i, c * P:c * P + P], k.ident[:, :])
                    mm.then_inc(S["turned"], 1)
                if u := unit(q, v, 0):
                    t, w, n = u
                    pe.wait_ge(S["wc_lo"], t + 1)
                    wait(pe, S["y"], t - 1)
                    for i in range(2):
                        ps = k.bank[DOWN_BANK + 2 * w + i]
                        for m in range(MC):
                            if i == 0 and m % 2 == 0:
                                pe.wait_ge(S["h_lo"], t * HP + (m // 2 + 1))
                            hh, hl = (a[:, w, m, i * P:i * P + P] for a in (h_hi, h_lo))
                            nc.tensor.matmul(ps[:, 0:2 * D], hh, wc_hl[:, w, m, :, :].rearrange("p a d -> p (a d)"),
                                             start=(m == 0), stop=False)
                            mm = nc.tensor.matmul(ps[:, 0:D], hl, wc_hl[:, w, m, 0, :], start=False,
                                                  stop=(m == MC - 1))
                    mm.then_inc(S["down"], 1)

            bias_tensor(pe)
            steps(pe, step)
            for j in range(PAIRS):
                pe.wait_ge(S["normed"], j + 1)
                wait(pe, S["x0"], j)
                wait(pe, S["x1"], j)
                for i in range(3):
                    nc.tensor.transpose(k.bank[0][:, i * P:i * P + P], xt[:, 3 * j + i, 0:P], k.ident[:, :])
                    mm = nc.tensor.transpose(k.bank[1][0:D1, i * P:i * P + P], xt[:, 3 * j + i, P:D], k.ident[:, :])
                mm.then_inc(S["t_turned"], 1)

        @block.scalar
        def _(act):
            def gelu(u, m):
                if u:
                    t, w, n = u
                    act.wait_ge(S["up"], t * MC + (m + 1))
                    wait(act, S["h_lo"], (t - 1) * HP + (m // 2 + 1))
                    nc.scalar.activation(hT[:, m, :], k.bank[(w * MC + m) % UP_BANKS][:, 0:UNIT], ACT.Gelu,
                                         bias=b1[:, w, m:m + 1]).then_inc(S["act"], 1)

            def step(q, v):
                one, two, last = unit(q, v, 1), unit(q, v, 2), unit(q, v, -1)
                if two:
                    t, w, n = two
                    act.wait_ge(w1_in[w], n * 48 + 48)
                    wait(act, S["up"], (t - 1) * MC)
                    nc.scalar.activation(wa_hi[:, w, :], wa[:, w, :], ACT.Identity).then_inc(S["wa_hi"], 1)
                if one:
                    t, w, n = one
                    act.wait_ge(b_in[w], n * 16 + 16)
                if last:
                    t, w, n = last
                    act.wait_ge(S["down"], t + 1)
                    wait(act, y_out[w], n * 16)
                    for i in range(2):
                        a = nc.scalar.activation(y[:, w, i, :], k.bank[DOWN_BANK + 2 * w + i][:, 0:D], ACT.Identity)
                    a.then_inc(S["half"], 1)
                gelu(one, 0)
                gelu(one, 1)
                for m in range(2, MC):
                    gelu(one, m)
                    if one and m - 2 < WP:
                        t, w, n = one
                        act.wait_ge(w2_in[w], n * 16 + 16)
                        wait(act, S["down"], t - 1)
                        c = slice((m - 2) * (MC // WP), (m - 1) * (MC // WP))
                        nc.scalar.activation(wc_hl[:, w, c, 0, :], wc[:, w, c, :], ACT.Identity).then_inc(S["wc_hi"], 1)
                if two:
                    t, w, n = two
                    act.wait_ge(S["turned"], t + 1)
                    ps = k.bank[TURN_BANK]
                    nc.scalar.activation(ga_hi[:, :], ps[:, 0:UNIT], ACT.Identity)
                    nc.scalar.activation(gb_hi[:, :], ps[:, UNIT:2 * UNIT], ACT.Identity).then_inc(S["x_hi"], 1)

            steps(act, step)
            for j in range(PAIRS):
                act.wait_ge(S["var"], j + 1)
                nc.scalar.activation(mv[:, 3, j, :], mv[:, 1, j, :], ACT.Sqrt, bias=k.eps[:, :]).then_inc(S["rstd"], 1)
                act.wait_ge(S["t_turned"], j + 1)
                nc.scalar.activation(k.xT0[:, j * PC:j * PC + PC], k.bank[0][:, 0:PC], ACT.Copy).then_inc(S["x0"], 1)

        @block.vector
        def _(dve):
            def step(q, v):
                one, two, last = unit(q, v, 1), unit(q, v, 2), unit(q, v, -1)
                if two:
                    t, w, n = two
                    dve.wait_ge(w1_in[w], n * 48 + 48)
                    wait(dve, S["up"], (t - 1) * MC)
                    nc.vector.tensor_copy(wb_hl[:, w, :], wb[:, w, :]).then_inc(S["wb_hi"], 1)
                    dve.wait_ge(S["wa_hi"], t + 1)
                    nc.vector.tensor_tensor(wa_lo[:, w, :], wa[:, w, :], wa_hi[:, w, :].bitcast(F32),
                                            ALU.subtract).then_inc(S["wa_lo"], 1)
                if last:
                    t, w, n = last
                    dve.wait_ge(S["half"], t + 1)
                    for i in range(2):
                        a = nc.vector.tensor_tensor(y[:, w, i, :], k.bank[DOWN_BANK + 2 * w + i][:, D:2 * D], y[:, w, i, :],
                                                    ALU.add)
                    a.then_inc(S["y"], 1)
                for p in range(HP):
                    if one:
                        t, w, n = one
                        dve.wait_ge(S["act"], t * MC + (2 * p + 2))
                        wait(dve, S["down"], t - 1)
                        m = slice(2 * p, 2 * p + 2)
                        nc.vector.tensor_copy(h_hi[:, w, m, :], hT[:, m, :]).then_inc(S["h_hi"], 1)
                        dve.wait_ge(S["h_hi"], t * HP + (p + 1))
                        nc.vector.tensor_tensor(h_lo[:, w, m, :], hT[:, m, :], h_hi[:, w, m, :].bitcast(F32),
                                                ALU.subtract).then_inc(S["h_lo"], 1)
                if two:
                    t, w, n = two
                    dve.wait_ge(S["x_hi"], t + 1)
                    ps = k.bank[TURN_BANK]
                    nc.vector.tensor_tensor(ga_lo[:, :], ps[:, 0:UNIT], ga_hi[:, :].bitcast(F32), ALU.subtract)
                    nc.vector.tensor_tensor(gb_lo[:, :], ps[0:D1, UNIT:2 * UNIT], gb_hi[0:D1, :].bitcast(F32),
                                            ALU.subtract).then_inc(S["x"], 1)

            ch = Chain(dve, S["chain"])
            for i in range(KEPT):
                ch.link(nc.vector.tensor_tensor(hit[:, :, :], key[:, :, :],
                                                top[:, :, i:i + 1].broadcast_to([P, TILES, NX0]), ALU.is_equal))
                ch.link(nc.vector.tensor_tensor(hit[:, :, :], hit[:, :, :], combine[:, :, :], ALU.mult))
                ch.link(nc.vector.tensor_reduce(share[:, :, i], hit[:, :, :], AX.X, ALU.add))
            bias_vector(dve)
            steps(dve, step)

            def normalise(j):
                dve.wait_ge(S["added"], (3 * j + 3) * KEPT)
                for i in range(3):
                    ch.did(nc.vector.bn_stats(st[:, j, i, :], tile[:, 3 * j + i, :]))
                ch.sync()
                ch.did(nc.vector.tensor_tensor(mv[:, 0, j, :], st[:, j, :, 1], st[:, j, :, 4], ALU.add))
                ch.did(nc.vector.tensor_tensor(mv[:, 1, j, :], st[:, j, :, 1], st[:, j, :, 4], ALU.subtract))
                ch.did(nc.vector.tensor_tensor(mv[:, 2, j, :], st[:, j, :, 2], st[:, j, :, 5], ALU.add))
                ch.sync()
                ch.did(nc.vector.tensor_scalar(mv[:, 0, j, :], mv[:, 0, j, :], 0.5, None, ALU.mult))
                ch.link(nc.vector.scalar_tensor_tensor(mv[:, 1, j, :], mv[:, 1, j, :], 0.25, mv[:, 1, j, :],
                                                       ALU.mult, ALU.mult))
                nc.vector.scalar_tensor_tensor(mv[:, 1, j, :], mv[:, 2, j, :], 1.0 / D, mv[:, 1, j, :], ALU.mult,
                                               ALU.add).then_inc(S["var"], 1)
                dve.wait_ge(S["rstd"], j + 1)
                ch.link(nc.vector.reciprocal(mv[:, 3, j, :], mv[:, 3, j, :]))
                for i in range(3):
                    a = nc.vector.tensor_scalar(xt[:, 3 * j + i, :], tile[:, 3 * j + i, :], mv[:, 0, j, i:i + 1],
                                                mv[:, 3, j, i:i + 1], ALU.subtract, ALU.mult)
                a.then_inc(S["normed"], 1)
                dve.wait_ge(S["t_turned"], j + 1)
                nc.vector.tensor_copy(k.xT1[0:D1, j * PC:j * PC + PC], k.bank[1][0:D1, 0:PC]).then_inc(S["x1"], 1)

            for t in range(TILES):
                for i in range(KEPT):
                    n = t * KEPT + i
                    dve.wait_ge(got[n % BACK], n // BACK * 16 + 16)
                    if i:
                        dve.wait_ge(S["added"], t * KEPT + i)
                    nc.vector.scalar_tensor_tensor(tile[:, t, :], back[:, n % BACK, :], share[:, t, i:i + 1], tile[:, t, :],
                                                   ALU.mult, ALU.add).then_inc(S["added"], 1)
                if t % 3 == 2:
                    normalise(t // 3)


def experts0(k, d):
    with ExitStack() as ctx:
        index = k.sb(ctx, "index", [P, TILES, KEPT], mybir.dt.uint32)
        expert_of = k.sb(ctx, "expert_of", [1, UNITS], mybir.dt.int32)
        combine, key = k.sb(ctx, "combine0", [P, TILES, NX0]), k.sb(ctx, "key", [P, TILES, NX0])
        top = k.sb(ctx, "top", [P, TILES, KEPT])
        with ExitStack() as own:
            chosen = k.sb(own, "chosen0", [P, TILES, NX0])
            gates(k, d, "g0", G0, E0, combine, "gate0", chosen)
            slots(k, d, chosen, key, top, index, expert_of)
        routed(k, d, combine, key, top, index, expert_of)



def hyena(k, d):
    nc = k.nc
    S = {n: k.sem("hy_" + n) for n in ("loaded", "z", "zs", "conv", "turned", "zcopy", "shift", "exp", "chain",
                                       "vt", "vt0", "vt1", "out", "added", "wout")}
    tin, made, upd = ([k.sem(f"hy_{n}{o}") for o in range(2)] for n in ("tin", "long", "upd"))
    NT = 2 * B
    CH = 5
    with ExitStack() as ctx:
        z = k.sb(ctx, "hy_z", [HALF, NT, 3 * D])
        bm = k.sb(ctx, "hy_b", [HALF, 2, D])
        wo0, wo1 = k.sb(ctx, "hy_wo0", [P, D]), k.sb(ctx, "hy_wo1", [D1 + 1, D])
        with ExitStack() as own, nc.Block() as block:
            w0, w1 = k.sb(own, "hy_w0", [P, 3 * D]), k.sb(own, "hy_w1", [D1 + 1, 3 * D])
            cw = k.sb(own, "hy_cw", [P, CH, 4])
            zs = k.sb(own, "hy_zs", [P, 2, PC])
            zc = k.sb(own, "hy_zc", [P, 2, PC])

            @block.sync
            def _(sp):
                for dst, src in ((w0[:, :], d["w_lin"][0:P, :]), (w1[:, :], d["w_lin"][P:D + 1, :]),
                                 (cw[:, :, :].rearrange("p a b -> p (a b)"), d["conv"]),
                                 (bm[:, :, :].rearrange("p a b -> p (a b)"), bcast_rows(d["bmat"], 2 * D, HALF)),
                                 (wo0[:, :], d["w_out"][0:P, :]), (wo1[:, :], d["w_out"][P:D + 1, :])):
                    sp.dma_start(dst, src).then_inc(S["loaded"], 16)
                sp.wait_ge(S["loaded"], 96)

            units = [(j, c) for j in range(PAIRS) for c in range(CH)]

            @block.tensor
            def _(pe):
                pe.wait_ge(S["loaded"], 96)
                def linear(n):
                    j, c = units[n]
                    m = P if c < CH - 1 else D1
                    if n >= 2:
                        pe.wait_ge(S["zs"], n - 1)
                    ps = k.bank[n % 2][0:m, 0:PC]
                    nc.tensor.matmul(ps, w0[:, c * P:c * P + m], k.xT0[:, j * PC:j * PC + PC], start=True, stop=False)
                    nc.tensor.matmul(ps, w1[:, c * P:c * P + m], k.xT1[0:D1 + 1, j * PC:j * PC + PC], start=False,
                                     stop=True).then_inc(S["z"], 1)

                def turn(n):
                    j, c = units[n]
                    m = P if c < CH - 1 else D1
                    pe.wait_ge(S["conv"], n + 1)
                    if n >= 2:
                        pe.wait_ge(S["zcopy"], n - 1)
                    for i in range(4):
                        mm = nc.tensor.transpose(k.bank[2 + n % 2][0:HALF, i * P:i * P + m],
                                                 zc[0:m, n % 2, i * HALF:i * HALF + HALF], k.ident[0:m, 0:m])
                    mm.then_inc(S["turned"], 1)

                linear(0)
                linear(1)
                for n in range(len(units)):
                    if n + 2 < len(units):
                        linear(n + 2)
                    turn(n)

            @block.scalar
            def _(act):
                def out(n):
                    j, c = units[n]
                    m = P if c < CH - 1 else D1
                    act.wait_ge(S["z"], n + 1)
                    if n >= 2:
                        act.wait_ge(S["conv"], n - 1)
                    nc.scalar.activation(zs[0:m, n % 2, :], k.bank[n % 2][0:m, 0:PC], ACT.Copy).then_inc(S["zs"], 1)

                def back(n):
                    j, c = units[n]
                    m = P if c < CH - 1 else D1
                    act.wait_ge(S["turned"], n + 1)
                    nc.scalar.activation(z[:, 4 * j:4 * j + 4, c * P:c * P + m],
                                         k.bank[2 + n % 2][0:HALF, :].rearrange("p (a b) -> p a b", a=4)[:, :, 0:m],
                                         ACT.Copy).then_inc(S["zcopy"], 1)

                out(0)
                out(1)
                for n in range(len(units)):
                    if n + 2 < len(units):
                        out(n + 2)
                    back(n)

            @block.vector
            def _(dve):
                ch = Chain(dve, S["chain"])
                dve.wait_ge(S["loaded"], 96)
                ch.did(nc.vector.tensor_tensor(wo0[:, 0:P], wo0[:, 0:P], k.ident[:, :], ALU.add))
                ch.did(nc.vector.tensor_tensor(wo1[0:D1, P:D], wo1[0:D1, P:D], k.ident[0:D1, 0:D1], ALU.add))
                for n, (j, c) in enumerate(units):
                    m = P if c < CH - 1 else D1
                    dve.wait_ge(S["zs"], n + 1)
                    if n >= 2:
                        dve.wait_ge(S["turned"], n - 1)
                    src = zs[0:m, n % 2, :].rearrange("p (b l) -> p b l", b=2)
                    dst = zc[0:m, n % 2, :].rearrange("p (b l) -> p b l", b=2)
                    ch.link(nc.vector.tensor_scalar(dst, src, cw[0:m, c, 2:3], cw[0:m, c, 3:4], ALU.mult, ALU.add))
                    if c >= 3:
                        x = (k.xT0, k.xT1)[c - 3][0:m, j * PC:j * PC + PC].rearrange("p (b l) -> p b l", b=2)
                        ch.link(nc.vector.tensor_tensor(dst, dst, x, ALU.add))
                    ch.link(nc.vector.scalar_tensor_tensor(dst[:, :, 1:L], src[:, :, 0:L - 1], cw[0:m, c, 1:2],
                                                           dst[:, :, 1:L], ALU.mult, ALU.add))
                    nc.vector.scalar_tensor_tensor(dst[:, :, 2:L], src[:, :, 0:L - 2], cw[0:m, c, 0:1],
                                                   dst[:, :, 2:L], ALU.mult, ALU.add).then_inc(S["conv"], 1)

        with ExitStack() as own, nc.Block() as block:
            most, total = k.sb(own, "hy_most", [HALF, 2, NT]), k.sb(own, "hy_total", [HALF, 2, NT])
            T = k.sb(own, "hy_T", [HALF, 2, CG, L])
            tmp = k.sb(own, "hy_tmp", [HALF, 2, NT, CG])
            v = z[:, :, 2 * D:3 * D]
            hp = d["filters"]

            def groups(eng, one, ch=None, per=0):
                def step(g, u):
                    one(g + 1, 0, 1 - u)
                    one(g, 1, u)

                one(0, 0, 0)
                for u in range(2):
                    step(u, u)
                with eng.Fori(1, NCG // 2 - 1) as q:
                    if ch:
                        ch.enter(q - 1, 4 * per)
                    for u in range(2):
                        step(q * 2 + u, u)
                    if ch:
                        ch.leave(NCG // 2 - 2)
                step(NCG - 2, 0)
                one(NCG - 1, 1, 1)


            @block.sync
            def _(sp):
                def load(g, o, u):
                    wait(sp, made[o], g)
                    for s in range(0, HALF, FC):
                        src = bass.AP(hp.tensor, g * (CG * FC * FPITCH) + (o * D * FC * FPITCH + HALF - s),
                                      [[FPITCH - 1, FC], [FC * FPITCH, CG], [1, L]])
                        sp.dma_start(T[s:s + FC, o, :, :], src).then_inc(tin[o], 16)

                groups(sp, load)
                for o in range(2):
                    sp.wait_ge(tin[o], NCG * 16 * (HALF // FC))

            @block.tensor
            def _(pe):
                def convolve(g, o, u):
                    pe.wait_ge(tin[o], g * (16 * (HALF // FC)) + 16 * (HALF // FC))
                    if o == 1:
                        pe.wait_ge(upd[0], g + 1)
                        wait(pe, upd[1], g - 1)
                    ps = k.bank[2 * o + u][0:HALF, :].rearrange("p (c n) -> p c n", c=CG)
                    for c in range(CG):
                        vc = v[:, :, bass.ds(g * CG + c, 1)]
                        nc.tensor.matmul(ps[:, c, :], T[:, o, c, 0:HALF], vc.rearrange("p n a -> p (n a)"),
                                         start=True, stop=False)
                        first = v.rearrange("p (b i) c -> p b i c", i=2)[:, :, 0, bass.ds(g * CG + c, 1)]
                        mm = nc.tensor.matmul(ps.rearrange("p c (b i) -> p c b i", i=2)[:, c, :, 1],
                                              T[:, o, c, HALF:L], first.rearrange("p b a -> p (b a)"),
                                              start=False, stop=True)
                    mm.then_inc(made[o], 1)

                groups(pe, convolve)

            @block.scalar
            def _(act):
                act.wait_ge(S["shift"], 1)
                nc.scalar.activation(z[:, :, 0:D], z[:, :, 0:D], ACT.Exp).then_inc(S["exp"], 1)
                act.wait_ge(S["shift"], 2)
                with act.Fori(0, NT) as n:
                    one = bass.ds(n, 1)
                    x = z[:, one, D:2 * D].rearrange("p n c -> p (n c)")
                    nc.scalar.activation(x, x, ACT.Exp, bias=most[:, 1, one],
                                         accum_out=total[:, 1, one]).then_inc(S["exp"], 1)

            @block.vector
            def _(dve):
                ch = Chain(dve, S["chain"])
                ch.n = 0
                base = sum(2 if c < 3 else 3 for c in range(CH)) * PAIRS + 2
                ch.base = base
                dve.wait_ge(S["chain"], base)
                x = [z[:, :, o * D:o * D + D] for o in range(2)]
                ch.link(nc.vector.tensor_reduce(most[:, 0, :], x[0], AX.X, ALU.max))
                nc.vector.tensor_tensor(x[0], x[0], over(most[:, 0, :], D), ALU.subtract).then_inc(S["shift"], 1)
                ch.link(nc.vector.tensor_reduce(most[:, 1, :], x[1], AX.X, ALU.max))
                nc.vector.tensor_scalar(most[:, 1, :], most[:, 1, :], -1.0, None, ALU.mult).then_inc(S["shift"], 1)

                def soften(o):
                    ch.link(nc.vector.reciprocal(total[:, o, :], total[:, o, :]))
                    ch.link(nc.vector.tensor_tensor(x[o], x[o], over(total[:, o, :], D), ALU.mult))

                dve.wait_ge(S["exp"], 1)
                ch.link(nc.vector.tensor_reduce(total[:, 0, :], x[0], AX.X, ALU.add))
                soften(0)

                def update(g, o, u):
                    c = bass.ds(g * CG, CG)
                    vg, xg, to = v[:, :, c], x[o][:, :, c], tmp[:, o, :, :]
                    ps = k.bank[2 * o + u][0:HALF, :].rearrange("p (c n) -> p n c", c=CG)
                    bg = bm[:, o, c].unsqueeze(1).broadcast_to([HALF, NT, CG])
                    wait(dve, upd[o], g)
                    if o == 1:
                        dve.wait_ge(upd[0], g + 1)
                    ch.link(nc.vector.tensor_tensor(to, vg, bg, ALU.mult))
                    dve.wait_ge(made[o], g + 1)
                    ch.link(nc.vector.tensor_tensor(to, ps, to, ALU.add))
                    ch.link(nc.vector.tensor_tensor(to, to, xg, ALU.mult))
                    nc.vector.tensor_tensor(vg, vg, to, ALU.add).then_inc(upd[o], 1)
                    if isinstance(g, int) and g == 1 and o == 0:
                        dve.wait_ge(S["exp"], 1 + NT)
                        soften(1)

                groups(dve, update, ch, 3)

        with ExitStack() as own, nc.Block() as block:
            v = z[:, :, 2 * D:3 * D]

            @block.tensor
            def _(pe):
                for j in range(PAIRS):
                    u = j % 2
                    if j >= 2:
                        pe.wait_ge(S["vt0"], j - 1)
                        pe.wait_ge(S["vt1"], j - 1)
                    for i in range(4):
                        nc.tensor.transpose(k.bank[u][:, i * HALF:i * HALF + HALF], v[:, 4 * j + i, 0:P],
                                            k.ident[0:HALF, 0:HALF])
                        mm = nc.tensor.transpose(k.bank[2 + u][0:D1, i * HALF:i * HALF + HALF], v[:, 4 * j + i, P:D],
                                                 k.ident[0:HALF, 0:HALF])
                    mm.then_inc(S["vt"], 1)
                for j in range(PAIRS):
                    pe.wait_ge(S["vt0"], j + 1)
                    pe.wait_ge(S["vt1"], j + 1)
                    if j:
                        pe.wait_ge(S["added"], j)
                    for t in range(3):
                        at = j * PC + t * P
                        nc.tensor.matmul(k.bank[4 + t][:, 0:D], k.xT0[:, at:at + P], wo0[:, :], start=True, stop=False)
                        mm = nc.tensor.matmul(k.bank[4 + t][:, 0:D], k.xT1[0:D1 + 1, at:at + P], wo1[:, :],
                                              start=False, stop=True)
                    mm.then_inc(S["out"], 1)

            @block.scalar
            def _(act):
                for j in range(PAIRS):
                    act.wait_ge(S["vt"], j + 1)
                    nc.scalar.activation(k.xT0[:, j * PC:j * PC + PC], k.bank[j % 2][:, 0:PC],
                                         ACT.Copy).then_inc(S["vt0"], 1)

            @block.vector
            def _(dve):
                for j in range(PAIRS):
                    dve.wait_ge(S["vt"], j + 1)
                    nc.vector.tensor_copy(k.xT1[0:D1, j * PC:j * PC + PC],
                                          k.bank[2 + j % 2][0:D1, 0:PC]).then_inc(S["vt1"], 1)
                for j in range(PAIRS):
                    dve.wait_ge(S["out"], j + 1)
                    for t in range(3):
                        a = nc.vector.tensor_tensor(k.h[:, j, t, :], k.bank[4 + t][:, 0:D], k.h[:, j, t, :], ALU.add)
                    a.then_inc(S["added"], 1)



def norm_d(k, d):
    norm(k, "nd", d, k.h)


def attention(k, d):
    nc = k.nc
    names = ("loaded", "consts", "staged", "kq", "kt", "qt", "vals", "qtok", "qcopy", "vcopy", "s1", "stats", "sd", "rt",
             "aug", "turned", "qat", "s2", "probs", "pv", "attn", "at", "at0", "at1", "out", "added", "chain",
             "zero", "sign", "dev")
    S = {n: k.sem("at_" + n) for n in names}
    HC = 3
    NCH = HEADS // HC
    HP = HC * 32
    N_S = 3 * HEADS // 2
    with ExitStack() as ctx, nc.Block() as block:
        wq0, wq1 = k.sb(ctx, "at_wq0", [P, NCH * HP]), k.sb(ctx, "at_wq1", [D1 + 1, NCH * HP])
        wk0, wk1 = k.sb(ctx, "at_wk0", [P, NCH * HP]), k.sb(ctx, "at_wk1", [D1 + 1, NCH * HP])
        w0, w1 = k.sb(ctx, "at_w0", [P, 3, D]), k.sb(ctx, "at_w1", [D1 + 1, 3, D])
        gam = k.sb(ctx, "at_gamma", [P, 3])
        x0, x1 = k.sb(ctx, "at_x0", [P, PC]), k.sb(ctx, "at_x1", [D1 + 1, PC])
        kT, qT = k.sb(ctx, "at_kT", [HP, NCH, PC]), k.sb(ctx, "at_qT", [HP, NCH, PC])
        va = k.sb(ctx, "at_va", [P, 2, 3, HEADS, HD + 1])
        qa = k.sb(ctx, "at_qa", [P, 3, HEADS, 32])
        qaT = k.sb(ctx, "at_qaT", [HP, NCH, PC])
        st = k.sb(ctx, "at_st", [P, 3 * HEADS, 6])
        mx = k.sb(ctx, "at_mx", [P, 3 * HEADS])
        dv = k.sb(ctx, "at_dv", [P, 3, 3 * HEADS])
        pT = k.sb(ctx, "at_pT", [P, 3, HEADS, L])
        rec = k.sb(ctx, "at_rec", [P, 3, HEADS])
        att = k.sb(ctx, "at_att", [P, 3, D])
        a0, a1 = k.sb(ctx, "at_a0", [P, PC]), k.sb(ctx, "at_a1", [D1 + 1, PC])
        bank = k.bank
        S2_BANKS = (4, 5, 0, 1, 2, 3)
        K_BANKS, Q_T_BANKS = (6, 7, 4, 5), (0, 1, 2, 3)
        V_BANKS, Q_BANKS = ((6, 0), (6, D), (7, 0)), ((4, 0), (4, D), (5, 0))
        S1_BANKS = (0, 1, 2, 3, 4, 5)
        PV_BANKS = ((6, 0), (7, 0), (7, HEADS * (HD + 1)))
        TURN_BANKS, AT_BANKS = (0, 1, 2, 3), (4, 5)
        O_BANKS = ((6, 0), (6, D), (7, 0))
        NS1, NS2 = len(S1_BANKS), len(S2_BANKS)
        PARTS = (((0, P, 0),), ((0, 64, 0), (64, P, L)), ((0, P, L),))

        def pair_of(n):
            t, m, i = n // (HEADS // 2), n % (HEADS // 2) // HC, n % HC
            return t, (2 * HC * m + i, 2 * HC * m + i + HC)

        def steps(eng, step, ch=None, per=0):
            with eng.Fori(0, PAIRS // 2 - 1) as q:
                if ch:
                    ch.enter(q, 2 * per)
                for u in range(2):
                    step(q * 2 + u, u, False)
                if ch:
                    ch.leave(PAIRS // 2 - 1)
            step(PAIRS - 2, 0, False)
            step(PAIRS - 1, 1, True)

        def two(ap, heads):
            return ap[:, heads[0]:heads[1] + 1:HC]

        @block.sync
        def _(sp):
            for dst, src in ((wq0, d["wq_heads"][0:P, :]), (wq1, d["wq_heads"][P:D + 1, :]),
                             (wk0, d["wk_heads"][0:P, :]), (wk1, d["wk_heads"][P:D + 1, :])):
                sp.dma_start(dst[:, :], src).then_inc(S["loaded"], 16)
            for n, w in enumerate(("wq", "wv", "wo")):
                sp.dma_start(w0[:, n, :], d[w][0:P, :]).then_inc(S["loaded"], 16)
                sp.dma_start(w1[:, n, :], d[w][P:D + 1, :]).then_inc(S["loaded"], 16)
            sp.dma_start(gam[:, 0:1], bcast_rows(d["gamma"], 1)).then_inc(S["loaded"], 16)
            sp.wait_ge(S["loaded"], 176)

        @block.gpsimd
        def _(pool):
            nc.gpsimd.memset(qa[:, :, :, :].rearrange("p a b c -> p (a b c)"), 0.0).then_inc(S["zero"], 1)
            pool.wait_ge(S["zero"], 1)
            nc.gpsimd.memset(va[:].rearrange("p u a b c -> p (u a b c)"), 1.0).then_inc(S["zero"], 1)
            pool.wait_ge(S["zero"], 2)
            nc.gpsimd.memset(a1[D1:D1 + 1, :], 1.0).then_inc(S["zero"], 1)
            pool.wait_ge(S["zero"], 3)

            def stage(j):
                nc.gpsimd.tensor_copy(x0[:, :], k.xT0[:, bass.ds(j * PC, PC)]).then_inc(S["staged"], 1)
                pool.wait_ge(S["staged"], j * 2 + 1)
                nc.gpsimd.tensor_copy(x1[:, :], k.xT1[0:D1 + 1, bass.ds(j * PC, PC)]).then_inc(S["staged"], 1)

            stage(0)
            with pool.Fori(1, PAIRS) as j:
                pool.wait_ge(S["qtok"], j)
                pool.wait_ge(S["staged"], j * 2)
                stage(j)

        @block.tensor
        def _(pe):
            def project(j):
                pe.wait_ge(S["staged"], j * 2 + 2)
                wait(pe, S["added"], j - 1)
                wait(pe, S["probs"], j * N_S - 4)
                for wa, wb, places in ((wk0, wk1, K_BANKS), (wq0, wq1, Q_T_BANKS)):
                    for c in range(NCH):
                        ps = bank[places[c]][0:HP, 0:PC]
                        nc.tensor.matmul(ps, wa[:, c * HP:c * HP + HP], x0[:, :], start=True, stop=False)
                        mm = nc.tensor.matmul(ps, wb[:, c * HP:c * HP + HP], x1[:, :], start=False, stop=True)
                    mm.then_inc(S["kq"], 1)
                    if wa is wk0:
                        wait(pe, S["probs"], j * N_S)

                def tokens(n, places):
                    for t, (b, at) in enumerate(places):
                        nc.tensor.matmul(bank[b][:, at:at + D], x0[:, t * P:t * P + P], w0[:, n, :],
                                         start=True, stop=False)
                        mm = nc.tensor.matmul(bank[b][:, at:at + D], x1[:, t * P:t * P + P], w1[:, n, :],
                                              start=False, stop=True)
                    return mm

                pe.wait_ge(S["kt"], j + 1)
                tokens(1, V_BANKS).then_inc(S["vals"], 1)
                tokens(0, Q_BANKS).then_inc(S["qtok"], 1)

            def first(j):
                pe.wait_ge(S["qt"], j + 1)
                pe.wait_ge(S["qcopy"], j + 1)
                for n in range(N_S):
                    t, heads = pair_of(n)
                    if n >= NS1:
                        pe.wait_ge(S["stats"], j * N_S + (n - NS1 + 1))
                    for i, h in enumerate(heads):
                        r, c = 32 * (h % HC), h // HC
                        for lo, hi, b0 in PARTS[t]:
                            mm = nc.tensor.matmul(bank[S1_BANKS[n % NS1]][lo:hi, i * L:i * L + L],
                                                  qT[r:r + HD, c, t * P + lo:t * P + hi],
                                                  kT[r:r + HD, c, b0:b0 + L], start=True, stop=True)
                    mm.then_inc(S["s1"], 1)

            def turn(j):
                pe.wait_ge(S["aug"], j + 1)
                for c in range(NCH):
                    for t in range(3):
                        mm = nc.tensor.transpose(bank[TURN_BANKS[c]][0:HP, t * P:t * P + P],
                                                 qa[:, t, HC * c:HC * c + HC, :].rearrange("p a b -> p (a b)"),
                                                 k.ident[:, :])
                mm.then_inc(S["turned"], 1)

            def second(j):
                pe.wait_ge(S["qat"], j + 1)
                for n in range(N_S):
                    t, heads = pair_of(n)
                    if n >= NS2:
                        pe.wait_ge(S["probs"], j * N_S + (n - NS2 + 1))
                    for i, h in enumerate(heads):
                        r, c = 32 * (h % HC), h // HC
                        for lo, hi, b0 in PARTS[t]:
                            mm = nc.tensor.matmul(bank[S2_BANKS[n % NS2]][lo:hi, i * L:i * L + L],
                                                  kT[r:r + HD + 1, c, t * P + lo:t * P + hi],
                                                  qaT[r:r + HD + 1, c, b0:b0 + L], start=True, stop=True)
                    mm.then_inc(S["s2"], 1)

            def product(j, u):
                pe.wait_ge(S["probs"], j * N_S + N_S)
                for t in range(3):
                    b, at = PV_BANKS[t]
                    for lo, hi, b0 in PARTS[t]:
                        q0 = t * P + lo - b0
                        e = b0 // L
                        big, s0 = 2 * e, 64 * e
                        for h in range(HEADS):
                            o = bank[b][lo:hi, at + h * (HD + 1):at + (h + 1) * (HD + 1)]
                            nc.tensor.matmul(o, pT[:, big, h, q0:q0 + hi - lo], va[:, u, big, h, :],
                                             start=True, stop=False)
                            mm = nc.tensor.matmul(o, pT[s0:s0 + 64, 1, h, q0:q0 + hi - lo],
                                                  va[s0:s0 + 64, u, 1, h, :], start=False, stop=True)
                    if t != 1:
                        mm.then_inc(S["pv"], 1)

            def project_out(j):
                pe.wait_ge(S["attn"], j + 1)
                for t in range(3):
                    nc.tensor.transpose(bank[AT_BANKS[0]][:, t * P:t * P + P], att[:, t, 0:P], k.ident[:, :])
                    mm = nc.tensor.transpose(bank[AT_BANKS[1]][0:D1, t * P:t * P + P], att[:, t, P:D], k.ident[:, :])
                mm.then_inc(S["at"], 1)
                pe.wait_ge(S["at0"], j + 1)
                pe.wait_ge(S["at1"], j + 1)
                for t, (b, at) in enumerate(O_BANKS):
                    nc.tensor.matmul(bank[b][:, at:at + D], a0[:, t * P:t * P + P], w0[:, 2, :], start=True, stop=False)
                    mm = nc.tensor.matmul(bank[b][:, at:at + D], a1[:, t * P:t * P + P], w1[:, 2, :], start=False,
                                          stop=True)
                mm.then_inc(S["out"], 1)

            def step(j, u, last):
                second(j)
                if not last:
                    project(j + 1)
                    first(j + 1)
                    pe.wait_ge(S["vcopy"], j + 2)
                else:
                    pe.wait_ge(S["added"], j)
                product(j, u)
                if not last:
                    turn(j + 1)
                project_out(j)

            pe.wait_ge(S["loaded"], 176)
            pe.wait_ge(S["zero"], 3)
            project(0)
            first(0)
            turn(0)
            steps(pe, step)

        @block.scalar
        def _(act):
            act.wait_ge(S["loaded"], 176)
            nc.scalar.activation(gam[:, 1:2], gam[:, 0:1], ACT.Sign).then_inc(S["sign"], 1)
            nc.scalar.activation(gam[:, 2:3], gam[:, 0:1], ACT.Abs).then_inc(S["sign"], 1)
            act.wait_ge(S["consts"], 1)

            def project(j):
                act.wait_ge(S["kq"], j * 2 + 1)
                for c in range(NCH):
                    a = nc.scalar.activation(kT[:, c, :], bank[K_BANKS[c]][0:HP, 0:PC], ACT.Copy)
                a.then_inc(S["kt"], 1)
                act.wait_ge(S["kq"], j * 2 + 2)
                for c in range(NCH):
                    a = nc.scalar.activation(qT[:, c, :], bank[Q_T_BANKS[c]][0:HP, 0:PC], ACT.Copy,
                                             scale=gam[0:HP, 1:2])
                a.then_inc(S["qt"], 1)
                act.wait_ge(S["dev"], j + 1)
                nc.scalar.activation(dv[:, 1, :], dv[:, 0, :], ACT.Sqrt).then_inc(S["sd"], 1)
                act.wait_ge(S["turned"], j + 1)
                for c in range(NCH):
                    a = nc.scalar.activation(qaT[:, c, :], bank[TURN_BANKS[c]][0:HP, 0:PC], ACT.Copy)
                a.then_inc(S["qat"], 1)

            def step(j, u, last):
                for n in range(N_S):
                    t, heads = pair_of(n)
                    act.wait_ge(S["s2"], j * N_S + (n + 1))
                    nc.scalar.activation(two(pT[:, t], heads),
                                         bank[S2_BANKS[n % NS2]][:, 0:2 * L].rearrange("p (a b) -> p a b", a=2),
                                         ACT.Exp).then_inc(S["probs"], 1)
                if not last:
                    project(j + 1)
                act.wait_ge(S["at"], j + 1)
                nc.scalar.activation(a0[:, :], bank[AT_BANKS[0]][:, 0:PC], ACT.Copy).then_inc(S["at0"], 1)

            project(0)
            steps(act, step)

        @block.vector
        def _(dve):
            ch = Chain(dve, S["chain"])
            dve.wait_ge(S["sign"], 2)
            nc.vector.tensor_scalar(gam[:, 1:2], gam[:, 1:2], float(HD) ** -0.5, None,
                                    ALU.mult).then_inc(S["consts"], 1)
            dve.wait_ge(S["consts"], 1)
            dve.wait_ge(S["zero"], 3)

            def project(j, u):
                dve.wait_ge(S["vals"], j + 1)
                for t, (b, at) in enumerate(V_BANKS):
                    a = nc.vector.tensor_copy(va[:, u, t, :, 0:HD],
                                              bank[b][:, at:at + D].rearrange("p (h e) -> p h e", h=HEADS))
                a.then_inc(S["vcopy"], 1)
                dve.wait_ge(S["qtok"], j + 1)
                for t, (b, at) in enumerate(Q_BANKS):
                    a = nc.vector.tensor_scalar(qa[:, t, :, 0:HD],
                                                bank[b][:, at:at + D].rearrange("p (h e) -> p h e", h=HEADS),
                                                gam[:, 1:2], None, ALU.mult)
                a.then_inc(S["qcopy"], 1)
                for n in range(N_S):
                    t, heads = pair_of(n)
                    dve.wait_ge(S["s1"], j * N_S + (n + 1))
                    ps = bank[S1_BANKS[n % NS1]][:, 0:2 * L].rearrange("p (a b) -> p a b", a=2)
                    for i, h in enumerate(heads):
                        ch.did(nc.vector.bn_stats(st[:, t * HEADS + h, :], ps[:, i, :]))
                    nc.vector.tensor_reduce(two(mx[:, t * HEADS:t * HEADS + HEADS], heads), ps, AX.X,
                                            ALU.max).then_inc(S["stats"], 1)
                ch.sync()
                dve.wait_ge(S["stats"], j * N_S + N_S)
                ch.did(nc.vector.tensor_tensor(dv[:, 0, :], st[:, :, 1], st[:, :, 4], ALU.subtract))
                ch.did(nc.vector.tensor_tensor(dv[:, 1, :], st[:, :, 2], st[:, :, 5], ALU.add))
                ch.sync()
                ch.link(nc.vector.scalar_tensor_tensor(dv[:, 0, :], dv[:, 0, :], L / 4, dv[:, 0, :], ALU.mult, ALU.mult))
                ch.link(nc.vector.tensor_tensor(dv[:, 0, :], dv[:, 0, :], dv[:, 1, :], ALU.add))
                nc.vector.tensor_scalar(dv[:, 0, :], dv[:, 0, :], 1.0 / (L - 1), None, ALU.mult).then_inc(S["dev"], 1)
                dve.wait_ge(S["sd"], j + 1)
                ch.link(nc.vector.tensor_scalar(dv[:, 1, :], dv[:, 1, :], 1e-5, None, ALU.add))
                ch.link(nc.vector.reciprocal(dv[:, 1, :], dv[:, 1, :]))
                ch.link(nc.vector.tensor_scalar(dv[:, 2, :], dv[:, 1, :], gam[:, 2:3], None, ALU.mult))
                r = dv[:, 2, :].rearrange("p (t h) -> p t h", t=3)
                for t in range(3):
                    ch.did(nc.vector.tensor_tensor(qa[:, t, :, 0:HD], qa[:, t, :, 0:HD], over(r[:, t, :], HD),
                                                   ALU.mult))
                nc.vector.scalar_tensor_tensor(qa[:, :, :, HD], mx[:, :].rearrange("p (t h) -> p t h", t=3), -1.0, r,
                                               ALU.mult, ALU.mult).then_inc(S["aug"], 1)

            def step(j, u, last):
                if not last:
                    project(j + 1, 1 - u)
                for t in range(3):
                    if t != 2:
                        dve.wait_ge(S["pv"], j * 2 + (t + 1))
                    b, at = PV_BANKS[t]
                    o = bank[b][:, at:at + HEADS * (HD + 1)].rearrange("p (h e) -> p h e", h=HEADS)
                    ch.link(nc.vector.reciprocal(rec[:, t, :], o[:, :, HD]))
                    a = nc.vector.tensor_tensor(att[:, t, :].rearrange("p (h e) -> p h e", h=HEADS), o[:, :, 0:HD],
                                                over(rec[:, t, :], HD), ALU.mult)
                a.then_inc(S["attn"], 1)
                dve.wait_ge(S["at"], j + 1)
                nc.vector.tensor_copy(a1[0:D1, :], bank[AT_BANKS[1]][0:D1, 0:PC]).then_inc(S["at1"], 1)
                dve.wait_ge(S["out"], j + 1)
                for t, (b, at) in enumerate(O_BANKS):
                    a = nc.vector.tensor_tensor(k.xn[:, j, t, :],
                                                bank[b][:, at:at + D], k.xn[:, j, t, :], ALU.add)
                a.then_inc(S["added"], 1)

            IN = 2 * N_S + 4 + 3 + 3
            project(0, 0)
            steps(dve, step, ch, IN + 3)


def norm_e(k, d):
    norm(k, "ne", d, k.xn, affine="ln1")


def experts(k, d, nx, combine, acc):
    nc = k.nc
    S = {n: k.sem("x1_" + n) for n in ("twice", "x_hi", "x", "b_in", "w1_in", "wa_hi", "wa_lo", "wb_hi", "wb_lo",
                                       "up", "act", "down", "acc")}
    w2_in = [k.sem(f"x1_w2_in{u}") for u in range(2)]
    UP_BANKS, DOWN_BANK = 4, 4
    with ExitStack() as ctx, nc.Block() as block:
        wa, wb = k.sb(ctx, "x1_wa", [P, FF]), k.sb(ctx, "x1_wb", [P, FF])
        wc = k.sb(ctx, "x1_wc", [P, 2, MC * D])
        b1 = k.sb(ctx, "x1_b1", [P, nx * MC])
        wa_hi, wa_lo = k.sb(ctx, "x1_wa_hi", [P, 2, FF], F32R), k.sb(ctx, "x1_wa_lo", [P, 2, FF], F32R)
        wb_hl = k.sb(ctx, "x1_wb_hl", [P, 2, FF], F32R)
        xa_hi, xa_lo = k.sb(ctx, "x1_xa_hi", [P, PAIRS * PC], F32R), k.sb(ctx, "x1_xa_lo", [P, PAIRS * PC], F32R)
        xb_hi, xb_lo = k.sb(ctx, "x1_xb_hi", [P, PAIRS * PC], F32R), k.sb(ctx, "x1_xb_lo", [D1, PAIRS * PC], F32R)
        hT = k.sb(ctx, "x1_hT", [P, 2, MC, PC])

        def run(eng, split, up, down):
            split(0)
            for e in range(nx):
                at = e * PAIRS
                up(at, e, 0, 0)
                if e:
                    down(at - 1, e - 1, PAIRS - 1, 1)
                if e + 1 < nx:
                    split(e + 1)

                def two(i):
                    for v in range(2):
                        up(i * 2 + (at + 1 + v), e, i * 2 + (1 + v), 1 - v)
                        down(i * 2 + (at + v), e, i * 2 + v, v)

                if e == 0:
                    two(0)
                with eng.Fori(1 if e == 0 else 0, PAIRS // 2 - 1) as i:
                    two(i)
                up(at + PAIRS - 1, e, PAIRS - 1, 1)
                down(at + PAIRS - 2, e, PAIRS - 2, 0)
            down(nx * PAIRS - 1, nx - 1, PAIRS - 1, 1)

        @block.sync
        def _(sp):
            sp.dma_start(k.xT1[D1:P, :], k.xT1[0:D1, :]).then_inc(S["twice"], 16)
            sp.dma_start(b1[:, :], d["b1_1"]).then_inc(S["b_in"], 16)
            for e in range(nx):
                wait(sp, S["wa_lo"], e)
                wait(sp, S["wb_lo"], e)
                sp.dma_start(wa[:, :], d["w1_1"][e, 0:P, :]).then_inc(S["w1_in"], 16)
                for r in (0, D1):
                    sp.dma_start(wb[r:r + D1, :], d["w1_1"][e, P:D, :]).then_inc(S["w1_in"], 16)
                wait(sp, S["down"], (e - 1) * 3 * PAIRS)
                sp.dma_start(wc[:, e % 2, :], d["w2_1"][e]).then_inc(w2_in[e % 2], 16)

        @block.tensor
        def _(pe):
            def up(t, e, j, v):
                pe.wait_ge(S["wa_hi"], e + 1)
                pe.wait_ge(S["wa_lo"], e + 1)
                pe.wait_ge(S["wb_lo"], e + 1)
                pe.wait_ge(S["x"], j + 1)
                x, u = bass.ds(j * PC, PC), e % 2
                for m in range(MC):
                    ps = k.bank[(v * MC + m) % UP_BANKS][:, 0:PC]
                    c = slice(m * P, m * P + P)
                    wait(pe, S["act"], t * MC + (m + 1 - UP_BANKS))
                    nc.tensor.matmul(ps, wa_hi[:, u, c], xa_hi[:, x], start=True, stop=False)
                    nc.tensor.matmul(ps, wa_hi[:, u, c], xa_lo[:, x], start=False, stop=False)
                    nc.tensor.matmul(ps, wa_lo[:, u, c], xa_hi[:, x], start=False, stop=False)
                    nc.tensor.matmul(ps, wb_hl[:, u, c], xb_hi[:, x], start=False, stop=False)
                    nc.tensor.matmul(ps, wb_hl[0:D1, u, c], xb_lo[:, x], start=False, stop=True).then_inc(S["up"], 1)

            def down(t, e, j, v):
                pe.wait_ge(w2_in[e % 2], e // 2 * 16 + 16)
                for i in range(3):
                    wait(pe, S["acc"], t * 3 + (i - 2))
                    for m in range(MC):
                        if i == 0:
                            pe.wait_ge(S["act"], t * MC + (m + 1))
                        mm = nc.tensor.matmul(k.bank[DOWN_BANK + i][:, 0:D], hT[:, v, m, i * P:i * P + P],
                                              wc[:, e % 2, m * D:m * D + D], start=(m == 0), stop=(m == MC - 1))
                    mm.then_inc(S["down"], 1)

            run(pe, lambda e: None, up, down)

        @block.scalar
        def _(act):
            act.wait_ge(S["b_in"], 16)

            def split(e):
                act.wait_ge(S["w1_in"], e * 48 + 48)
                wait(act, S["up"], (e - 1) * PAIRS * MC)
                nc.scalar.activation(wa_hi[:, e % 2, :], wa[:, :], ACT.Identity).then_inc(S["wa_hi"], 1)

            def up(t, e, j, v):
                for m in range(MC):
                    act.wait_ge(S["up"], t * MC + (m + 1))
                    wait(act, S["down"], t * 3 - 3)
                    nc.scalar.activation(hT[:, v, m, :], k.bank[(v * MC + m) % UP_BANKS][:, 0:PC], ACT.Relu,
                                         bias=b1[:, e * MC + m:e * MC + m + 1]).then_inc(S["act"], 1)

            run(act, split, up, lambda t, e, j, v: None)

        @block.vector
        def _(dve):
            weights = combine[:, :, :].rearrange("p t e -> p (t e)")
            dve.wait_ge(S["twice"], 16)
            with dve.Fori(0, PAIRS) as j:
                x = bass.ds(j * PC, PC)
                nc.vector.tensor_copy(xa_hi[:, x], k.xT0[:, x]).then_inc(S["x_hi"], 1)
                nc.vector.tensor_copy(xb_hi[:, x], k.xT1[:, x]).then_inc(S["x_hi"], 1)
                dve.wait_ge(S["x_hi"], j * 2 + 2)
                nc.vector.tensor_tensor(xa_lo[:, x], k.xT0[:, x], xa_hi[:, x].bitcast(F32), ALU.subtract)
                nc.vector.tensor_tensor(xb_lo[:, x], k.xT1[0:D1, x], xb_hi[0:D1, x].bitcast(F32),
                                        ALU.subtract).then_inc(S["x"], 1)

            def split(e):
                u = e % 2
                dve.wait_ge(S["w1_in"], e * 48 + 48)
                wait(dve, S["up"], (e - 1) * PAIRS * MC)
                nc.vector.tensor_copy(wb_hl[:, u, :], wb[:, :]).then_inc(S["wb_hi"], 1)
                dve.wait_ge(S["wa_hi"], e + 1)
                nc.vector.tensor_tensor(wa_lo[:, u, :], wa[:, :], wa_hi[:, u, :].bitcast(F32),
                                        ALU.subtract).then_inc(S["wa_lo"], 1)
                dve.wait_ge(S["wb_hi"], e + 1)
                nc.vector.tensor_tensor(wb_hl[D1:P, u, :], wb[D1:P, :], wb_hl[D1:P, u, :].bitcast(F32),
                                        ALU.subtract).then_inc(S["wb_lo"], 1)

            def down(t, e, j, v):
                for i in range(3):
                    at = t * 3 + i
                    dve.wait_ge(S["down"], at + 1)
                    if e:
                        wait(dve, S["acc"], at + (1 - 3 * PAIRS))
                    nc.vector.scalar_tensor_tensor(acc[:, j, i, :], k.bank[DOWN_BANK + i][:, 0:D],
                                                   weights[:, bass.ds(j * (3 * nx) + (e + i * nx), 1)],
                                                   acc[:, j, i, :], ALU.mult, ALU.add).then_inc(S["acc"], 1)

            run(dve, split, lambda t, e, j, v: None, down)


def experts1(k, d):
    with ExitStack() as ctx:
        combine = k.sb(ctx, "combine1", [P, PAIRS * 3, NX1])
        gates(k, d, "g1", 1, NX1, combine, "gate1")
        bias(k, d, "b1", NX1, combine, k.xn, "b2_1")
        experts(k, d, NX1, combine, k.xn)


def finish(k, d, out):
    nc = k.nc
    S = {n: k.sem("fi_" + n) for n in ("rows", "vars", "rstd", "inv", "lifted", "normed", "added", "stored", "chain")}
    with ExitStack() as ctx, nc.Block() as block:
        st = k.sb(ctx, "fi_st", [P, PAIRS, 3, 6])
        mv = k.sb(ctx, "fi_mv", [P, 3, PAIRS, 3])
        rs = k.sb(ctx, "fi_rs", [P, PAIRS, 3])
        gb = k.sb(ctx, "fi_gb", [P, 2, D])
        gain, shift = (gb[:, i, :].unsqueeze(1).broadcast_to([P, 3, D]) for i in range(2))

        @block.sync
        def _(sp):
            sp.dma_start(gb[:, :, :].rearrange("p a d -> p (a d)"), bcast_rows(d["ln2"], 2 * D)).then_inc(S["rows"], 16)
            tiles = out.rearrange("b l d -> (b l) d").rearrange("(j t p) d -> j p t d", t=3, p=P)
            for j in range(PAIRS):
                sp.wait_ge(S["added"], j + 1)
                sp.dma_start(tiles[j], k.h[:, j, :, :]).then_inc(S["stored"], 16)
            sp.wait_ge(S["stored"], PAIRS * 16)

        @block.gpsimd
        def _(pool):
            pool.wait_ge(S["rows"], 16)
            for j in range(PAIRS):
                nc.gpsimd.tensor_tensor(k.h[:, j, :, :], k.h[:, j, :, :], shift, ALU.add).then_inc(S["lifted"], 1)
                pool.wait_ge(S["lifted"], j + 1)

        @block.scalar
        def _(act):
            act.wait_ge(S["vars"], 1)
            nc.scalar.activation(rs[:, :, :], mv[:, 1], ACT.Sqrt, bias=k.eps[:, :]).then_inc(S["rstd"], 1)
            act.wait_ge(S["inv"], 1)
            for j in range(PAIRS):
                for t in range(3):
                    a = nc.scalar.activation(k.xn[:, j, t, :], k.xn[:, j, t, :], ACT.Identity,
                                             bias=mv[:, 2, j, t:t + 1], scale=rs[:, j, t:t + 1])
                a.then_inc(S["normed"], 1)

        @block.vector
        def _(dve):
            ch = Chain(dve, S["chain"])
            for j in range(PAIRS):
                for t in range(3):
                    ch.did(nc.vector.bn_stats(st[:, j, t, :], k.xn[:, j, t, :]))
            ch.sync()
            half = float(D // 2)
            ch.did(nc.vector.tensor_tensor(mv[:, 0], st[:, :, :, 1], st[:, :, :, 4], ALU.add))
            ch.did(nc.vector.tensor_tensor(mv[:, 1], st[:, :, :, 1], st[:, :, :, 4], ALU.subtract))
            ch.did(nc.vector.tensor_tensor(mv[:, 2], st[:, :, :, 2], st[:, :, :, 5], ALU.add))
            ch.sync()
            ch.link(nc.vector.scalar_tensor_tensor(mv[:, 1], mv[:, 1], 0.25, mv[:, 1], ALU.mult, ALU.mult))
            nc.vector.scalar_tensor_tensor(mv[:, 1], mv[:, 2], 0.5 / half, mv[:, 1], ALU.mult,
                                           ALU.add).then_inc(S["vars"], 1)
            dve.wait_ge(S["rstd"], 1)
            ch.link(nc.vector.reciprocal(rs[:, :, :], rs[:, :, :]))
            nc.vector.scalar_tensor_tensor(mv[:, 2], mv[:, 0], -0.5, rs[:, :, :], ALU.mult,
                                           ALU.mult).then_inc(S["inv"], 1)
            dve.wait_ge(S["rows"], 16)
            for j in range(PAIRS):
                dve.wait_ge(S["normed"], j + 1)
                ch.link(nc.vector.tensor_tensor(k.xn[:, j, :, :], k.xn[:, j, :, :], gain, ALU.mult))
                dve.wait_ge(S["lifted"], j + 1)
                nc.vector.tensor_tensor(k.h[:, j, :, :], k.h[:, j, :, :], k.xn[:, j, :, :],
                                        ALU.add).then_inc(S["added"], 1)


PHASES = (setup, tokenizer, norm_a, retention, norm_b, experts0, hyena, norm_d, attention, norm_e, experts1)



def program(nc, d, out):
    d = dict(d)
    for name, shape in (("filters", (2, D, FC, FPITCH)), ("positions", (B, OFFC, 64)),
                    ("queue", (UNITS * UNIT, D)), ("answers", (UNITS * UNIT, D))):
        d[name] = nc.dram_tensor(name + "_scratch", shape, F32, kind="Internal").ap()
    with ExitStack() as ctx:
        k = Core(nc, ctx)
        for phase in PHASES:
            phase(k, d)
            if phase is experts0:
                k.clear_semaphores()
        finish(k, d, out)



def lay_out(i):
    import numpy as np

    def rows(w, b):
        return np.concatenate([w, b.reshape(w.shape[:-2] + (1, w.shape[-1]))], axis=-2)

    def heads(w, b, one):
        full = rows(w, b)
        out = np.zeros((D + 1, HEADS, 32), np.float32)
        out[:, :, 0:HD] = full.reshape(D + 1, HEADS, HD)
        if one:
            out[D, :, HD] = 1.0
        return out.reshape(D + 1, HEADS * 32)

    part = np.arange(P)
    a = {}
    a["patches"] = i["x"].reshape(B, 3, 32, 4, 32, 4).transpose(0, 1, 3, 5, 2, 4).reshape(B, 48, HW)
    a["txt"] = i["txt"]
    a["stem_w"] = i["L0_tok_stem_w"].reshape(CS, 48).T
    a["v96"] = np.stack([i["L0_tok_" + n] for n in ("stem_b", "bn1_g", "bn1_b", "bn1_m", "bn1_v")], 1)
    a["v192"] = np.stack([i["L0_tok_" + n] for n in ("dcn_b", "bn2_g", "bn2_b", "bn2_m", "bn2_v")]).reshape(-1)
    a["off_w"] = i["L0_tok_off_w"].transpose(1, 2, 3, 0).reshape(CS, TAPS * OFFC)
    a["off_b"] = i["L0_tok_off_b"].reshape(OFFC, 1)
    a["dcn_w"] = i["L0_tok_dcn_w"].transpose(1, 2, 3, 0).reshape(CS, TAPS * D)
    tap, o = np.arange(TAPS), np.arange(8)
    gy = (4 * o[None, :, None] + (tap // 4)[:, None, None]) + 0 * o[None, None, :]
    gx = (4 * o[None, None, :] + (tap % 4)[:, None, None]) + 0 * o[None, :, None]
    a["grid"] = np.stack([gy, gx], 1).reshape(OFFC, 64).astype(np.float32)
    a["xy"] = -np.concatenate([(part % 32)[:, None], 4 * np.arange(YCH)[None, :] + (part // 32)[:, None]],
                              1).astype(np.float32)
    a["ident"] = np.eye(P, dtype=np.float32)
    a["times"] = np.linspace(0.0, 1.0, 512, dtype=np.float32)[0:L]
    a["h_param"] = i["L1_attn_h_param"]
    a["filter_par"] = np.stack([i["L1_attn_alphas"].reshape(D), i["L1_attn_win_b"].reshape(D)], 1)
    at = np.arange(L)
    dist = at[None, :] - at[:, None]
    decay = np.where(dist >= 0, np.float32(0.99) ** np.maximum(dist, 0).astype(np.float32), 0)
    decay = (decay / np.sqrt(np.float32(D))).astype(np.float32)
    a["decay"] = np.zeros((P, 2, 2, L), np.float32)
    a["decay"][:, 0, 0], a["decay"][0:64, 0, 1] = decay[0:P], decay[P:L]
    a["decay"][64:P, 1, 1], a["decay"][:, 1, 0] = decay[0:64], decay[64:L]
    a["decay"] = a["decay"].reshape(P, 4 * L)
    a["qkv"] = rows(i["L0_attn_W_qkv"], i["L0_attn_b_qkv"])
    we = i["L0_ffn_We"].transpose(1, 0, 2).reshape(D, NX0)
    a["gate0"] = rows(np.concatenate([i["L0_ffn_Wg"], we], 1),
                      np.concatenate([i["L0_ffn_bg"], i["L0_ffn_be"].reshape(-1)]))
    a["w1_0"] = i["L0_ffn_W1"].reshape(NX0, D, FF)
    a["b1_0"] = i["L0_ffn_b1"].reshape(NX0, MC, P).transpose(0, 2, 1)
    a["w2_0"] = i["L0_ffn_W2"].reshape(NX0, MC, P, D).transpose(0, 2, 1, 3).reshape(NX0, P, MC * D)
    a["before"] = (part[:, None] < part[None, :]).astype(np.float32)
    a["unit_numbers"] = np.arange(UNITS, dtype=np.float32)[None, :]
    a["b2_0"] = i["L0_ffn_b2"].reshape(NX0, D)
    a["w_lin"] = rows(i["L1_attn_W_lin"].T, i["L1_attn_b_lin"])
    conv = np.zeros((5 * P, 4), np.float32)
    conv[0:3 * D, 0:3] = i["L1_attn_conv_w"].reshape(3 * D, 3)
    conv[0:3 * D, 3] = i["L1_attn_conv_b"]
    a["conv"] = conv.reshape(5, P, 4).transpose(1, 0, 2).reshape(P, 20)
    a["bmat"] = i["L1_attn_Bmat"].reshape(2 * D)
    a["w_out"] = rows(i["L1_attn_W_out"].T, i["L1_attn_b_out"])
    a["wq_heads"] = heads(i["L1_ffn_Wq"].T, i["L1_ffn_bq"], False)
    a["wk_heads"] = heads(i["L1_ffn_Wk"].T, i["L1_ffn_bk"], True)
    a["wq"] = rows(i["L1_ffn_Wq"].T, i["L1_ffn_bq"])
    a["wv"] = rows(i["L1_ffn_Wv"].T, i["L1_ffn_bv"])
    a["wo"] = rows(i["L1_ffn_Wo"].T, i["L1_ffn_bo"])
    a["gamma"] = i["L1_ffn_gamma"].reshape(1)
    a["ln1"] = np.concatenate([i["L1_ffn_ln1_g"], i["L1_ffn_ln1_b"]])
    a["ln2"] = np.concatenate([i["L1_ffn_ln2_g"], i["L1_ffn_ln2_b"]])
    a["gate1"] = rows(i["L1_ffn_Wg"].T, i["L1_ffn_bg"])
    a["w1_1"] = i["L1_ffn_W1"]
    a["b1_1"] = i["L1_ffn_b1"].reshape(NX1, MC, P).transpose(2, 0, 1).reshape(P, NX1 * MC)
    a["w2_1"] = i["L1_ffn_W2"].reshape(NX1, MC, P, D).transpose(0, 2, 1, 3).reshape(NX1, P, MC * D)
    a["b2_1"] = i["L1_ffn_b2"]
    return {n: np.ascontiguousarray(v) for n, v in a.items()}


def kernel(**inputs):
    import numpy as np
    import concourse.bacc as bacc
    from concourse.bass_utils import run_bass_kernel_spmd

    arrays = lay_out({n: np.asarray(v) for n, v in inputs.items()})
    nc = bacc.Bacc("TRN2", target_bir_lowering=False, num_devices=1)
    d = {n: nc.dram_tensor("in_" + n, a.shape, F32, kind="ExternalInput").ap() for n, a in arrays.items()}
    out = nc.dram_tensor("out", (B, L, D), F32, kind="ExternalOutput").ap()
    program(nc, d, out)
    r = run_bass_kernel_spmd(nc, [{"in_" + n: a for n, a in arrays.items()}], core_ids=[0])
    return r.results[0]["out"]
```
